# Optimizing a Trainium2 kernel written in Bass

```python
import numpy as np
import jax
import jax.numpy as jnp

def _softmax(x, axis=-1):
    return jax.nn.softmax(x, axis=axis)

def _gelu(x):
    return jax.nn.gelu(x, approximate=True)

def _silu(x):
    return jax.nn.silu(x)

def _sigmoid(x):
    return jax.nn.sigmoid(x)

def _layernorm(x, axis=-1, eps=1e-05):
    m = jnp.mean(x, axis=axis, keepdims=True)
    v = jnp.var(x, axis=axis, keepdims=True)
    return (x - m) / jnp.sqrt(v + eps)

def _scatter_add(tgt, idx, src, axis=0):
    return tgt.at[idx].add(src)

def _segment_sum(src, seg, n):
    return jax.ops.segment_sum(src, seg, n)
kernel_name = 'mk_early_fusion_d2_tok_img1024_r4_2ac64b'

def setup_inputs(seed: int=0):
    np.random.seed(seed)
    _w = jnp.asarray

    def _rec_inputs():
        import jax
        import jax.numpy as jnp
        _rk = jax.random.key(seed)
        x = -0.000222058 + 0.999998 * jax.random.normal(jax.random.fold_in(_rk, 1), (32, 3, 224, 224), jnp.float32)
        txt = 0.00193382 + 0.183443 * jax.random.normal(jax.random.fold_in(_rk, 2), (32, 128, 256), jnp.float32)
        return (x, txt)
    x, txt = _rec_inputs()

    def _L0_tok_setup():
        import jax, jax.numpy as jnp
        import numpy as np
        P = 16
        C = 3
        D = 256

        def _patchify(x, p):
            B, Cc, H, W = x.shape
            gh, gw = (H // p, W // p)
            x = x.reshape(B, Cc, gh, p, gw, p)
            x = x.transpose(0, 2, 4, 1, 3, 5)
            return x.reshape(B, gh * gw, Cc * p * p)
        key = jax.random.key(seed)
        k1, k2, k3, k4, k5 = jax.random.split(key, 5)
        patch_dim = C * P * P
        s1 = 1.0 / np.sqrt(patch_dim)
        s2 = 1.0 / np.sqrt(D)
        return {'x': jax.random.normal(k1, (32, C, 128, 128), dtype=jnp.float32), 'W1': jax.random.uniform(k2, (patch_dim, D), jnp.float32, -s1, s1), 'b1': jax.random.uniform(k3, (D,), jnp.float32, -s1, s1), 'W2': jax.random.uniform(k4, (D, D), jnp.float32, -s2, s2), 'b2': jax.random.uniform(k5, (D,), jnp.float32, -s2, s2)}
    _L0_tok_all = _L0_tok_setup()
    _L0_tok_in = {k: v for k, v in _L0_tok_all.items() if k in ('W1', 'b1', 'W2', 'b2')}
    del _L0_tok_all

    def _L0_attn_setup():
        import jax, jax.numpy as jnp
        import numpy as np
        import math
        L, B, D = (512, 4, 256)
        ZDIM, HDIM, NDIM = (128, 512, 16)

        def _laplace(x, mu=0.707107, sigma=0.282095):
            return 0.5 * (1.0 + jax.lax.erf((x - mu) / (sigma * math.sqrt(2.0))))

        def _ema(x, delta, alpha, beta, gamma, omega):
            seq_len = x.shape[0]
            scale = math.sqrt(1.0 / delta.shape[1])
            residual = x * omega
            xe = jnp.transpose(x, (1, 2, 0))
            p = jax.nn.sigmoid(delta)
            q = 1.0 - p * jax.nn.sigmoid(alpha)
            vander = jnp.arange(seq_len, dtype=x.dtype)[None, None, :] * jnp.log(q)
            kern = jnp.einsum('dnl,dn->dl', p * beta * jnp.exp(vander), gamma * scale)
            n = 2 * seq_len
            out = jnp.fft.irfft(jnp.fft.rfft(xe, n=n) * jnp.fft.rfft(kern, n=n), n=n)[..., :seq_len]
            out = jnp.transpose(out, (2, 0, 1)).astype(x.dtype)
            return jax.nn.silu(out + residual)

        def _rotary_bias(seq_len, zdim, alpha, beta):
            half = zdim // 2
            freqs = jnp.exp(jnp.arange(half, dtype=jnp.float32) * (-math.log(10000.0) / half))
            ang = jnp.arange(seq_len, dtype=jnp.float32)[:, None] * freqs[None, :]
            sin, cos = (jnp.sin(ang), jnp.cos(ang))

            def rot(v):
                v = jnp.broadcast_to(v, (seq_len, zdim))
                v1, v2 = (v[:, :half], v[:, half:])
                return jnp.concatenate([v1 * cos - v2 * sin, v2 * cos + v1 * sin], axis=1)
            return rot(alpha) @ rot(beta).T
        key = jax.random.key(seed)
        ks = jax.random.split(key, 12)
        std = 0.02
        val = np.ones((NDIM, 1), np.float32)
        val[1::2] = -1.0
        inp = {'x': jax.random.normal(ks[0], (L, B, D), jnp.float32), 'ema_delta': 0.2 * jax.random.normal(ks[1], (D, NDIM, 1), jnp.float32), 'ema_alpha': 0.2 * jax.random.normal(ks[2], (D, NDIM, 1), jnp.float32), 'ema_beta': 0.02 * jax.random.normal(ks[3], (D, NDIM, 1), jnp.float32) + jnp.asarray(val), 'ema_gamma': jax.random.normal(ks[4], (D, NDIM), jnp.float32), 'ema_omega': jax.random.normal(ks[5], (D,), jnp.float32), 'ln_w': jnp.ones((D,), jnp.float32), 'ln_b': jnp.zeros((D,), jnp.float32), 'Wv': std * jax.random.normal(ks[6], (HDIM, D), jnp.float32), 'bv': jnp.zeros((HDIM,), jnp.float32), 'Wmx': std * jax.random.normal(ks[7], (ZDIM + HDIM + 2 * D, D), jnp.float32), 'bmx': jnp.zeros((ZDIM + HDIM + 2 * D,), jnp.float32), 'Wh': std * jax.random.normal(ks[8], (D, HDIM), jnp.float32), 'bh': jnp.zeros((D,), jnp.float32), 'qk_gamma': std * jax.random.normal(ks[9], (2, ZDIM), jnp.float32), 'qk_beta': jnp.zeros((2, ZDIM), jnp.float32), 'rot_alpha': std * jax.random.normal(ks[10], (1, ZDIM), jnp.float32), 'rot_beta': std * jax.random.normal(ks[11], (1, ZDIM), jnp.float32)}
        return inp
    _L0_attn_all = _L0_attn_setup()
    _L0_attn_in = {k: v for k, v in _L0_attn_all.items() if k in ('ema_delta', 'ema_alpha', 'ema_beta', 'ema_gamma', 'ema_omega', 'ln_w', 'ln_b', 'Wv', 'bv', 'Wmx', 'bmx', 'Wh', 'bh', 'qk_gamma', 'qk_beta', 'rot_alpha', 'rot_beta')}
    del _L0_attn_all

    def _L0_ffn_setup():
        import jax, jax.numpy as jnp
        import numpy as np
        D = 256
        F = 256
        E = 8
        K = 2
        B, T = (2, 512)

        def _moe_forward(x, router_w, w1, w2, shared_gate_up, shared_down, shared_gate_w):
            b, t, d = x.shape
            xf = x.reshape(-1, d)
            n = xf.shape[0]
            logits = xf @ router_w
            probs = jax.nn.softmax(logits, axis=-1)
            topw, topi = jax.lax.top_k(probs, K)
            combine = jnp.zeros((n, E), dtype=probs.dtype).at[jnp.arange(n)[:, None], topi].add(topw)
            h = jax.nn.silu(jnp.einsum('nd,edf->nef', xf, w1))
            ye = jnp.einsum('nef,efd->ned', h, w2)
            routed = jnp.einsum('ne,ned->nd', combine, ye)
            gu = xf @ shared_gate_up
            gate, up = (gu[:, :F], gu[:, F:])
            shared = jax.nn.silu(gate) * up @ shared_down
            shared = jax.nn.sigmoid(xf @ shared_gate_w) * shared
            return (routed + shared).reshape(b, t, d)
        key = jax.random.key(seed)
        ks = jax.random.split(key, 7)
        std = 0.02
        x = jax.random.normal(ks[0], (B, T, D), dtype=jnp.float32)
        router_w = jax.random.normal(ks[1], (D, E), dtype=jnp.float32) * std
        w1 = jax.random.normal(ks[2], (E, D, F), dtype=jnp.float32) * std
        w2 = jax.random.normal(ks[3], (E, F, D), dtype=jnp.float32) * std
        shared_gate_up = jax.random.normal(ks[4], (D, 2 * F), dtype=jnp.float32) * std
        shared_down = jax.random.normal(ks[5], (F, D), dtype=jnp.float32) * std
        shared_gate_w = jax.random.normal(ks[6], (D, 1), dtype=jnp.float32) * std
        return {'x': x, 'router_w': router_w, 'w1': w1, 'w2': w2, 'shared_gate_up': shared_gate_up, 'shared_down': shared_down, 'shared_gate_w': shared_gate_w}
    _L0_ffn_all = _L0_ffn_setup()
    _L0_ffn_in = {k: v for k, v in _L0_ffn_all.items() if k in ('router_w', 'w1', 'w2', 'shared_gate_up', 'shared_down', 'shared_gate_w')}
    del _L0_ffn_all

    def _L1_attn_setup():
        import jax, jax.numpy as jnp
        import numpy as np
        import math
        D_MODEL = 256
        D_STATE = 128
        EXPAND = 2
        HEADDIM = 64
        NGROUPS = 1
        ROPE_FRACTION = 0.5
        A_FLOOR = 0.0001
        D_INNER = EXPAND * D_MODEL
        NHEADS = D_INNER // HEADDIM
        SPLIT = int(D_STATE * ROPE_FRACTION)
        R = SPLIT // 2
        D_IN_PROJ = 2 * D_INNER + 2 * D_STATE * NGROUPS + 3 * NHEADS + R
        BATCH = 1
        SEQLEN = 256

        def _mamba3_forward(u, w_in, w_out, dt_bias, D):
            b, l, _ = u.shape
            proj = u @ w_in.T
            sizes = [D_INNER, D_INNER, D_STATE * NGROUPS, D_STATE * NGROUPS, NHEADS, NHEADS, NHEADS, R]
            idx = np.cumsum(sizes)[:-1]
            z, x, B, C, dd_dt, dd_A, trap, angles = jnp.split(proj, idx, axis=-1)
            A = jnp.minimum(-jax.nn.softplus(dd_A), -A_FLOOR)
            dt = jax.nn.softplus(dd_dt + dt_bias)
            tr = jax.nn.sigmoid(trap)
            theta = jnp.cumsum(jnp.tanh(angles)[:, :, None, :] * dt[..., None] * jnp.pi, axis=1)
            x_h = x.reshape(b, l, NHEADS, HEADDIM)
            z_h = z.reshape(b, l, NHEADS, HEADDIM)
            B_h = B.reshape(b, l, NGROUPS, D_STATE)[:, :, 0, :]
            C_h = C.reshape(b, l, NGROUPS, D_STATE)[:, :, 0, :]

            def step(carry, inp):
                sr, si, px = carry
                dt_t, A_t, tr_t, th, bt, ct, xt = inp
                alpha = jnp.exp(A_t * dt_t)[:, :, None, None]
                beta = ((1.0 - tr_t) * dt_t)[:, :, None, None] * alpha
                gamma = (tr_t * dt_t)[:, :, None, None]
                base = bt[:, None, None, :] * (px[..., None] * beta + xt[..., None] * gamma)
                rc = jnp.cos(th)[:, :, None, :]
                rs = jnp.sin(th)[:, :, None, :]
                sr = sr * alpha + jnp.concatenate([base[..., :R] * rc, base[..., R:]], axis=-1)
                si = si * alpha + base[..., :R] * rs
                ctb = ct[:, None, None, :]
                y = jnp.sum((sr[..., :R] * rc + si * rs) * ctb[..., :R], axis=-1) + jnp.sum(sr[..., R:] * ctb[..., R:], axis=-1)
                return ((sr, si, xt), y)
            sr0 = jnp.zeros((b, NHEADS, HEADDIM, D_STATE), u.dtype)
            si0 = jnp.zeros((b, NHEADS, HEADDIM, R), u.dtype)
            px0 = jnp.zeros((b, NHEADS, HEADDIM), u.dtype)
            xs = (jnp.moveaxis(dt, 1, 0), jnp.moveaxis(A, 1, 0), jnp.moveaxis(tr, 1, 0), jnp.moveaxis(theta, 1, 0), jnp.moveaxis(B_h, 1, 0), jnp.moveaxis(C_h, 1, 0), jnp.moveaxis(x_h, 1, 0))
            _, ys = jax.lax.scan(step, (sr0, si0, px0), xs)
            y = jnp.moveaxis(ys, 0, 1) + D[None, None, :, None] * x_h
            out = y * jax.nn.silu(z_h)
            return out.reshape(b, l, D_INNER) @ w_out.T
        key = jax.random.key(seed)
        k0, k1, k2, k3 = jax.random.split(key, 4)
        u = jax.random.normal(k0, (BATCH, SEQLEN, D_MODEL), jnp.float32)
        w_in = jax.random.normal(k1, (D_IN_PROJ, D_MODEL), jnp.float32) * D_MODEL ** (-0.5)
        w_out = jax.random.normal(k2, (D_MODEL, D_INNER), jnp.float32) * D_INNER ** (-0.5)
        dt = jnp.exp(jax.random.uniform(k3, (NHEADS,), jnp.float32) * (math.log(0.1) - math.log(0.001)) + math.log(0.001))
        dt = jnp.maximum(dt, 0.0001)
        dt_bias = dt + jnp.log(-jnp.expm1(-dt))
        D = jnp.ones((NHEADS,), jnp.float32)
        return {'u': u, 'w_in': w_in, 'w_out': w_out, 'dt_bias': dt_bias, 'D': D}
    _L1_attn_all = _L1_attn_setup()
    _L1_attn_in = {k: v for k, v in _L1_attn_all.items() if k in ('w_in', 'w_out', 'dt_bias', 'D')}
    del _L1_attn_all

    def _L1_ffn_setup():
        import jax, jax.numpy as jnp
        import numpy as np
        INPUT_SIZE = 256
        OUTPUT_SIZE = 256
        key = jax.random.key(seed)
        kx, kt, kp, ktn, kpn = jax.random.split(key, 5)
        x = jax.random.normal(kx, (8, 512, INPUT_SIZE), dtype=jnp.float32)
        theta = jax.random.normal(kt, (INPUT_SIZE, OUTPUT_SIZE), dtype=jnp.float32) * 0.02
        phi = jax.random.normal(kp, (INPUT_SIZE, OUTPUT_SIZE), dtype=jnp.float32) * 0.02
        theta_noise = jax.random.normal(ktn, (INPUT_SIZE, OUTPUT_SIZE), dtype=jnp.float32) * 0.01
        phi_noise = jax.random.normal(kpn, (INPUT_SIZE, OUTPUT_SIZE), dtype=jnp.float32) * 0.01
        return {'x': x, 'theta': theta, 'phi': phi, 'theta_noise': theta_noise, 'phi_noise': phi_noise}
    _L1_ffn_all = _L1_ffn_setup()
    _L1_ffn_in = {k: v for k, v in _L1_ffn_all.items() if k in ('theta', 'phi', 'theta_noise', 'phi_noise')}
    del _L1_ffn_all
    return {'x': x, 'txt': txt, 'L0_tok_W1': _L0_tok_in['W1'], 'L0_tok_b1': _L0_tok_in['b1'], 'L0_tok_W2': _L0_tok_in['W2'], 'L0_tok_b2': _L0_tok_in['b2'], 'L0_attn_ema_delta': _L0_attn_in['ema_delta'], 'L0_attn_ema_alpha': _L0_attn_in['ema_alpha'], 'L0_attn_ema_beta': _L0_attn_in['ema_beta'], 'L0_attn_ema_gamma': _L0_attn_in['ema_gamma'], 'L0_attn_ema_omega': _L0_attn_in['ema_omega'], 'L0_attn_ln_w': _L0_attn_in['ln_w'], 'L0_attn_ln_b': _L0_attn_in['ln_b'], 'L0_attn_Wv': _L0_attn_in['Wv'], 'L0_attn_bv': _L0_attn_in['bv'], 'L0_attn_Wmx': _L0_attn_in['Wmx'], 'L0_attn_bmx': _L0_attn_in['bmx'], 'L0_attn_Wh': _L0_attn_in['Wh'], 'L0_attn_bh': _L0_attn_in['bh'], 'L0_attn_qk_gamma': _L0_attn_in['qk_gamma'], 'L0_attn_qk_beta': _L0_attn_in['qk_beta'], 'L0_attn_rot_alpha': _L0_attn_in['rot_alpha'], 'L0_attn_rot_beta': _L0_attn_in['rot_beta'], 'L0_ffn_router_w': _L0_ffn_in['router_w'], 'L0_ffn_w1': _L0_ffn_in['w1'], 'L0_ffn_w2': _L0_ffn_in['w2'], 'L0_ffn_shared_gate_up': _L0_ffn_in['shared_gate_up'], 'L0_ffn_shared_down': _L0_ffn_in['shared_down'], 'L0_ffn_shared_gate_w': _L0_ffn_in['shared_gate_w'], 'L1_attn_w_in': _L1_attn_in['w_in'], 'L1_attn_w_out': _L1_attn_in['w_out'], 'L1_attn_dt_bias': _L1_attn_in['dt_bias'], 'L1_attn_D': _L1_attn_in['D'], 'L1_ffn_theta': _L1_ffn_in['theta'], 'L1_ffn_phi': _L1_ffn_in['phi'], 'L1_ffn_theta_noise': _L1_ffn_in['theta_noise'], 'L1_ffn_phi_noise': _L1_ffn_in['phi_noise']}

def reference(x, txt, L0_tok_W1, L0_tok_b1, L0_tok_W2, L0_tok_b2, L0_attn_ema_delta, L0_attn_ema_alpha, L0_attn_ema_beta, L0_attn_ema_gamma, L0_attn_ema_omega, L0_attn_ln_w, L0_attn_ln_b, L0_attn_Wv, L0_attn_bv, L0_attn_Wmx, L0_attn_bmx, L0_attn_Wh, L0_attn_bh, L0_attn_qk_gamma, L0_attn_qk_beta, L0_attn_rot_alpha, L0_attn_rot_beta, L0_ffn_router_w, L0_ffn_w1, L0_ffn_w2, L0_ffn_shared_gate_up, L0_ffn_shared_down, L0_ffn_shared_gate_w, L1_attn_w_in, L1_attn_w_out, L1_attn_dt_bias, L1_attn_D, L1_ffn_theta, L1_ffn_phi, L1_ffn_theta_noise, L1_ffn_phi_noise):
    import jax
    import jax.numpy as jnp

    def _L0_tok_ref(x, W1, b1, W2, b2):
        import jax, jax.numpy as jnp
        import numpy as np
        P = 16
        C = 3
        D = 256

        def _patchify(x, p):
            B, Cc, H, W = x.shape
            gh, gw = (H // p, W // p)
            x = x.reshape(B, Cc, gh, p, gw, p)
            x = x.transpose(0, 2, 4, 1, 3, 5)
            return x.reshape(B, gh * gw, Cc * p * p)
        patches = _patchify(x, P)
        h = jax.nn.silu(jnp.einsum('blk,kd->bld', patches, W1) + b1)
        return jnp.einsum('bld,de->ble', h, W2) + b2

    def _L0_attn_ref(x, ema_delta, ema_alpha, ema_beta, ema_gamma, ema_omega, ln_w, ln_b, Wv, bv, Wmx, bmx, Wh, bh, qk_gamma, qk_beta, rot_alpha, rot_beta):
        import jax, jax.numpy as jnp
        import numpy as np
        import math
        L, B, D = (512, 4, 256)
        ZDIM, HDIM, NDIM = (128, 512, 16)

        def _laplace(x, mu=0.707107, sigma=0.282095):
            return 0.5 * (1.0 + jax.lax.erf((x - mu) / (sigma * math.sqrt(2.0))))

        def _ema(x, delta, alpha, beta, gamma, omega):
            seq_len = x.shape[0]
            scale = math.sqrt(1.0 / delta.shape[1])
            residual = x * omega
            xe = jnp.transpose(x, (1, 2, 0))
            p = jax.nn.sigmoid(delta)
            q = 1.0 - p * jax.nn.sigmoid(alpha)
            vander = jnp.arange(seq_len, dtype=x.dtype)[None, None, :] * jnp.log(q)
            kern = jnp.einsum('dnl,dn->dl', p * beta * jnp.exp(vander), gamma * scale)
            n = 2 * seq_len
            out = jnp.fft.irfft(jnp.fft.rfft(xe, n=n) * jnp.fft.rfft(kern, n=n), n=n)[..., :seq_len]
            out = jnp.transpose(out, (2, 0, 1)).astype(x.dtype)
            return jax.nn.silu(out + residual)

        def _rotary_bias(seq_len, zdim, alpha, beta):
            half = zdim // 2
            freqs = jnp.exp(jnp.arange(half, dtype=jnp.float32) * (-math.log(10000.0) / half))
            ang = jnp.arange(seq_len, dtype=jnp.float32)[:, None] * freqs[None, :]
            sin, cos = (jnp.sin(ang), jnp.cos(ang))

            def rot(v):
                v = jnp.broadcast_to(v, (seq_len, zdim))
                v1, v2 = (v[:, :half], v[:, half:])
                return jnp.concatenate([v1 * cos - v2 * sin, v2 * cos + v1 * sin], axis=1)
            return rot(alpha) @ rot(beta).T
        seq_len = x.shape[0]
        residual = x
        mean = jnp.mean(x, -1, keepdims=True)
        var = jnp.var(x, -1, keepdims=True)
        xn = (x - mean) * jax.lax.rsqrt(var + 1e-05) * ln_w + ln_b
        v = jax.nn.silu(xn @ Wv.T + bv)
        mx = _ema(xn, ema_delta, ema_alpha, ema_beta, ema_gamma, ema_omega)
        base = mx @ Wmx.T + bmx
        u = jax.nn.sigmoid(base[..., :D])
        zr = jax.nn.silu(base[..., D:D + ZDIM + HDIM])
        hx = base[..., D + ZDIM + HDIM:]
        z, r = (zr[..., :ZDIM], zr[..., ZDIM:])
        z2 = z[..., None, :] * qk_gamma + qk_beta
        q = jnp.transpose(z2[:, :, 0], (1, 0, 2))
        k = jnp.transpose(z2[:, :, 1], (1, 0, 2))
        vb = jnp.transpose(v, (1, 0, 2))
        bias = _rotary_bias(seq_len, ZDIM, rot_alpha, rot_beta)
        qk = jnp.einsum('blz,bmz->blm', q, k) / seq_len + bias
        attn = _laplace(qk)
        h = jnp.einsum('blm,bmh->blh', attn, vb)
        h = jnp.transpose(h, (1, 0, 2))
        h = jax.nn.silu(hx + h * r @ Wh.T + bh)
        return residual + u * (h - residual)

    def _L0_ffn_ref(x, router_w, w1, w2, shared_gate_up, shared_down, shared_gate_w):
        import jax, jax.numpy as jnp
        import numpy as np
        D = 256
        F = 256
        E = 8
        K = 2
        B, T = (2, 512)

        def _moe_forward(x, router_w, w1, w2, shared_gate_up, shared_down, shared_gate_w):
            b, t, d = x.shape
            xf = x.reshape(-1, d)
            n = xf.shape[0]
            logits = xf @ router_w
            probs = jax.nn.softmax(logits, axis=-1)
            topw, topi = jax.lax.top_k(probs, K)
            combine = jnp.zeros((n, E), dtype=probs.dtype).at[jnp.arange(n)[:, None], topi].add(topw)
            h = jax.nn.silu(jnp.einsum('nd,edf->nef', xf, w1))
            ye = jnp.einsum('nef,efd->ned', h, w2)
            routed = jnp.einsum('ne,ned->nd', combine, ye)
            gu = xf @ shared_gate_up
            gate, up = (gu[:, :F], gu[:, F:])
            shared = jax.nn.silu(gate) * up @ shared_down
            shared = jax.nn.sigmoid(xf @ shared_gate_w) * shared
            return (routed + shared).reshape(b, t, d)
        return _moe_forward(x, router_w, w1, w2, shared_gate_up, shared_down, shared_gate_w)

    def _L1_attn_ref(u, w_in, w_out, dt_bias, D):
        import jax, jax.numpy as jnp
        import numpy as np
        import math
        D_MODEL = 256
        D_STATE = 128
        EXPAND = 2
        HEADDIM = 64
        NGROUPS = 1
        ROPE_FRACTION = 0.5
        A_FLOOR = 0.0001
        D_INNER = EXPAND * D_MODEL
        NHEADS = D_INNER // HEADDIM
        SPLIT = int(D_STATE * ROPE_FRACTION)
        R = SPLIT // 2
        D_IN_PROJ = 2 * D_INNER + 2 * D_STATE * NGROUPS + 3 * NHEADS + R
        BATCH = 1
        SEQLEN = 256

        def _mamba3_forward(u, w_in, w_out, dt_bias, D):
            b, l, _ = u.shape
            proj = u @ w_in.T
            sizes = [D_INNER, D_INNER, D_STATE * NGROUPS, D_STATE * NGROUPS, NHEADS, NHEADS, NHEADS, R]
            idx = np.cumsum(sizes)[:-1]
            z, x, B, C, dd_dt, dd_A, trap, angles = jnp.split(proj, idx, axis=-1)
            A = jnp.minimum(-jax.nn.softplus(dd_A), -A_FLOOR)
            dt = jax.nn.softplus(dd_dt + dt_bias)
            tr = jax.nn.sigmoid(trap)
            theta = jnp.cumsum(jnp.tanh(angles)[:, :, None, :] * dt[..., None] * jnp.pi, axis=1)
            x_h = x.reshape(b, l, NHEADS, HEADDIM)
            z_h = z.reshape(b, l, NHEADS, HEADDIM)
            B_h = B.reshape(b, l, NGROUPS, D_STATE)[:, :, 0, :]
            C_h = C.reshape(b, l, NGROUPS, D_STATE)[:, :, 0, :]

            def step(carry, inp):
                sr, si, px = carry
                dt_t, A_t, tr_t, th, bt, ct, xt = inp
                alpha = jnp.exp(A_t * dt_t)[:, :, None, None]
                beta = ((1.0 - tr_t) * dt_t)[:, :, None, None] * alpha
                gamma = (tr_t * dt_t)[:, :, None, None]
                base = bt[:, None, None, :] * (px[..., None] * beta + xt[..., None] * gamma)
                rc = jnp.cos(th)[:, :, None, :]
                rs = jnp.sin(th)[:, :, None, :]
                sr = sr * alpha + jnp.concatenate([base[..., :R] * rc, base[..., R:]], axis=-1)
                si = si * alpha + base[..., :R] * rs
                ctb = ct[:, None, None, :]
                y = jnp.sum((sr[..., :R] * rc + si * rs) * ctb[..., :R], axis=-1) + jnp.sum(sr[..., R:] * ctb[..., R:], axis=-1)
                return ((sr, si, xt), y)
            sr0 = jnp.zeros((b, NHEADS, HEADDIM, D_STATE), u.dtype)
            si0 = jnp.zeros((b, NHEADS, HEADDIM, R), u.dtype)
            px0 = jnp.zeros((b, NHEADS, HEADDIM), u.dtype)
            xs = (jnp.moveaxis(dt, 1, 0), jnp.moveaxis(A, 1, 0), jnp.moveaxis(tr, 1, 0), jnp.moveaxis(theta, 1, 0), jnp.moveaxis(B_h, 1, 0), jnp.moveaxis(C_h, 1, 0), jnp.moveaxis(x_h, 1, 0))
            _, ys = jax.lax.scan(step, (sr0, si0, px0), xs)
            y = jnp.moveaxis(ys, 0, 1) + D[None, None, :, None] * x_h
            out = y * jax.nn.silu(z_h)
            return out.reshape(b, l, D_INNER) @ w_out.T
        return _mamba3_forward(u, w_in, w_out, dt_bias, D)

    def _L1_ffn_ref(x, theta, phi, theta_noise, phi_noise):
        import jax, jax.numpy as jnp
        import numpy as np
        INPUT_SIZE = 256
        OUTPUT_SIZE = 256
        real = jnp.einsum('bti,io->bto', x, jnp.cos(theta + theta_noise))
        imag = jnp.einsum('bti,io->bto', x, jnp.sin(phi + phi_noise))
        return jnp.sqrt(real * real + imag * imag)
    h = _L0_tok_ref(x, L0_tok_W1, L0_tok_b1, L0_tok_W2, L0_tok_b2)
    h = jnp.concatenate([h, txt], axis=1)
    h = h + _L0_attn_ref(_layernorm(h, axis=-1), L0_attn_ema_delta, L0_attn_ema_alpha, L0_attn_ema_beta, L0_attn_ema_gamma, L0_attn_ema_omega, L0_attn_ln_w, L0_attn_ln_b, L0_attn_Wv, L0_attn_bv, L0_attn_Wmx, L0_attn_bmx, L0_attn_Wh, L0_attn_bh, L0_attn_qk_gamma, L0_attn_qk_beta, L0_attn_rot_alpha, L0_attn_rot_beta)
    h = h + _L0_ffn_ref(_layernorm(h, axis=-1), L0_ffn_router_w, L0_ffn_w1, L0_ffn_w2, L0_ffn_shared_gate_up, L0_ffn_shared_down, L0_ffn_shared_gate_w)
    h = h + _L1_attn_ref(_layernorm(h, axis=-1), L1_attn_w_in, L1_attn_w_out, L1_attn_dt_bias, L1_attn_D)
    h = h + _L1_ffn_ref(_layernorm(h, axis=-1), L1_ffn_theta, L1_ffn_phi, L1_ffn_theta_noise, L1_ffn_phi_noise)
    return h

_drawn_inputs = setup_inputs


def setup_inputs(seed=0):
    import zlib

    import numpy as np

    out = dict(_drawn_inputs(seed))
    spreads = {'L0_attn_ln_w': (1.0, 0.2),
     'L0_attn_ln_b': (0.0, 0.1),
     'L0_attn_bv': (0.0, 0.8),
     'L0_attn_bmx': (0.0, 0.1),
     'L0_attn_bh': (0.0, 0.1),
     'L0_attn_qk_beta': (0.0, 0.8),
     'L1_attn_D': (1.0, 0.2)}
    factors = {'L0_attn_ema_delta': 4.177,
     'L0_attn_ema_alpha': 3.49,
     'L0_attn_ema_beta': 8.0,
     'L0_attn_Wv': 8.0,
     'L0_attn_Wh': 8.0,
     'L0_attn_qk_gamma': 8.0,
     'L0_attn_rot_alpha': 8.0,
     'L0_attn_rot_beta': 8.0,
     'L0_ffn_shared_gate_w': 64.0,
     'L1_ffn_theta': 8.0,
     'L1_ffn_theta_noise': 8.0,
     'L0_ffn_router_w': 3.941,
     'L0_ffn_w1': 3.317,
     'L0_ffn_w2': 3.297,
     'L0_ffn_shared_gate_up': 4.351,
     'L0_ffn_shared_down': 4.427}
    for name, (base, spread) in spreads.items():
        noise = np.random.default_rng([zlib.crc32(name.encode()), seed]).standard_normal(out[name].shape)
        drawn = base * np.exp(spread * noise) if base else spread * noise
        out[name] = jnp.asarray(drawn.astype(out[name].dtype))
    for name, factor in factors.items():
        out[name] = (out[name] * factor).astype(out[name].dtype)
    return out
```

```python
from contextlib import ExitStack

import numpy as np

import concourse.bass as bass
from concourse import mybir

F32 = mybir.dt.float32
F32R = mybir.dt.float32r
ALU = mybir.AluOpType
ACT = mybir.ActivationFunctionType
AX = mybir.AxisListType

P = 128
IMGS, TOKS, D = 32, 324, 256
PATCHES, TEXT = 196, 128
KC = 768 // P
DC = D // P
HALF = PATCHES // 2
NSTATE = 16
GROUPS = D // 4
TC = TOKS // 3
EPS = 1e-5


class Stage:

    def __init__(self, nc, tag):
        self.nc, self.tag, self.ctx = nc, tag, ExitStack()

    def __enter__(self):
        self.ctx.__enter__()
        return self

    def __exit__(self, *e):
        return self.ctx.__exit__(*e)

    def sb(self, name, shape, dt=F32):
        return self.ctx.enter_context(self.nc.sbuf_tensor(f"{self.tag}_{name}", shape, dt))

    def ps(self, name, shape):
        return self.ctx.enter_context(self.nc.psum_tensor(f"{self.tag}_{name}", shape, F32))

    def sem(self, name):
        return self.ctx.enter_context(self.nc.semaphore(f"{self.tag}_{name}"))

    def block(self):
        return self.ctx.enter_context(self.nc.Block())


def taps_stage(nc, T, kpad):
    with Stage(nc, "taps") as s:
        par = s.sb("par", [P, 4, DC, NSTATE])
        om = s.sb("om", [P, DC, 1])
        sg = s.sb("sg", [P, 2, DC, NSTATE])
        q = s.sb("q", [P, 5, DC, NSTATE])
        w = s.sb("w", [P, DC, IMGS, NSTATE])
        tmp = s.sb("tmp", [P, 2, DC, NSTATE])
        kp = s.sb("kp", [P, DC, 2 * IMGS])
        loaded, tanhs, step, stored = s.sem("loaded"), s.sem("tanhs"), s.sem("step"), s.sem("stored")
        block = s.block()

        @block.sync
        def _(sp):
            for n, name in enumerate(("delta", "alpha", "beta", "gamma")):
                sp.dma_start(par[:, n], T[name].rearrange("(c p) n -> p c n", p=P)).then_inc(loaded, 16)
            sp.dma_start(om[:, :, 0], T["omega"]).then_inc(loaded, 16)
            sp.wait_ge(step, 17)
            for c in range(DC):
                sp.dma_start(kpad[c * P:(c + 1) * P].rearrange("p (r k) -> p r k", r=IMGS),
                             kp[:, c:c + 1, :].broadcast_to([P, IMGS, 2 * IMGS])).then_inc(stored, 16)
            sp.wait_ge(stored, 32)

        @block.scalar
        def _(act):
            act.wait_ge(loaded, 80)
            act.activation(sg[:], par[:, 0:2], ACT.Tanh, scale=0.5).then_inc(tanhs, 1)

        @block.vector
        def _(dve):
            n = 0

            def chain(ins):
                nonlocal n
                n += 1
                ins.then_inc(step, 1)
                dve.wait_ge(step, n)

            chain(dve.memset(kp[:], 0.0))
            dve.wait_ge(tanhs, 1)
            dve.wait_ge(loaded, 80)
            chain(dve.tensor_scalar(sg[:], sg[:], 0.5, 0.5, ALU.mult, ALU.add))
            chain(dve.tensor_tensor(tmp[:, 0], sg[:, 0], sg[:, 1], ALU.mult))
            chain(dve.tensor_tensor(tmp[:, 1], sg[:, 0], par[:, 2], ALU.mult))
            chain(dve.tensor_scalar(q[:, 0], tmp[:, 0], -1.0, 1.0, ALU.mult, ALU.add))
            chain(dve.scalar_tensor_tensor(w[:, :, 0, :], tmp[:, 1], 0.25, par[:, 3], ALU.mult, ALU.mult))
            for k in range(5):
                if k < 4:
                    chain(dve.tensor_tensor(q[:, k + 1], q[:, k], q[:, k], ALU.mult))
                m = 1 << k
                for c in range(DC):
                    ins = dve.tensor_tensor(w[:, c, m:2 * m, :], w[:, c, 0:m, :],
                                            q[:, k, c:c + 1, :].broadcast_to([P, m, NSTATE]), ALU.mult)
                chain(ins)
            chain(dve.tensor_reduce(kp[:, :, IMGS:], w[:], AX.X, ALU.add))
            chain(dve.tensor_tensor(kp[:, :, IMGS:IMGS + 1], kp[:, :, IMGS:IMGS + 1], om[:], ALU.add))


def embed_stage(nc, T, h0, xn_t):
    with Stage(nc, "emb") as s:
        w1 = s.sb("w1", [P, KC, D])
        w2 = s.sb("w2", [P, DC, D])
        b1 = s.sb("b1", [P, DC])
        b2 = s.sb("b2", [P, 1, D])
        lnw, lnb = s.sb("lnw", [P, DC]), s.sb("lnb", [P, DC])
        ident = s.sb("ident", [P, P])
        xt = s.sb("xt", [P, KC * PATCHES])
        g = s.sb("g", [P, DC, PATCHES])
        ht = s.sb("ht", [P, 3, D])
        st, mv = s.sb("st", [P, 3, 6]), s.sb("mv", [P, 3, 2])
        neg = s.sb("neg", [P, 3])
        eps = s.sb("eps", [P, 3])
        hold = s.sb("hold", [P, 1])
        ln = s.sb("ln", [P, 6, 3])
        xn = s.sb("xn", [P, 3, D])
        xnt = s.sb("xnt", [P, DC, TOKS])
        hid = s.ps("hid", [P, DC, PATCHES])
        emb = s.ps("emb", [P, 2, D])
        tr = [s.ps(f"tr{c}", [P, 512]) for c in range(DC)]
        (weights, patches_in, text_in, hid_done, hid_silu, emb_done, ht_ready, init, stats, aggr, rstd, pool_step,
         normed, tr_done, xnt_ready, h0_out, xnt_out) = [s.sem(n) for n in (
            "weights", "patches_in", "text_in", "hid_done", "hid_silu", "emb_done", "ht_ready", "init", "stats", "aggr",
            "rstd", "pool_step", "normed", "tr_done", "xnt_ready", "h0_out", "xnt_out")]
        block = s.block()
        rows = (HALF, HALF, TEXT)
        col = (0, HALF, PATCHES)
        LOADS = 8

        @block.sync
        def _(sp):
            for dst, src in ((w1[:], T["tok_W1"].rearrange("(k p) n -> p k n", p=P)),
                             (w2[:], T["tok_W2"].rearrange("(k p) n -> p k n", p=P)),
                             (b1[:], T["tok_b1"]),
                             (b2[:, 0, :], T["tok_b2"].rearrange("(a d) -> a d", a=1).broadcast_to([P, D])),
                             (lnw[:], T["ln_w"]),
                             (lnb[:], T["ln_b"]),
                             (ident[:], T["ident"])):
                sp.dma_start(dst, src).then_inc(weights, 16)
            sp.wait_ge(init, 4)
            with sp.Fori(0, IMGS) as i:
                sp.wait_ge(hid_done, i + 1)
                sp.dma_start(xt[:], T["patches"][i]).then_inc(patches_in, 16)
                sp.wait_ge(normed, 3 * i + 3)
                sp.wait_ge(h0_out, 32 * i + 32)
                sp.dma_start(ht[:, 2, :], T["txt"][i]).then_inc(text_in, 16)
            sp.wait_ge(h0_out, 32 * IMGS + 32)
            sp.wait_ge(xnt_out, 16 * IMGS + 16)

        @block.tensor
        def _(pe):
            pe.wait_ge(weights, 16 * 7)

            def hidden(i):
                pe.wait_ge(patches_in, 16 * i + 16)
                pe.wait_ge(hid_silu, 2 * i + 2)
                for f in range(DC):
                    for k in range(KC):
                        mm = pe.matmul(hid[:, f, :], w1[:, k, f * P:(f + 1) * P],
                                       xt[:, k * PATCHES:(k + 1) * PATCHES], start=k == 0, stop=k == KC - 1)
                mm.then_inc(hid_done, 1)

            def embedding(i):
                pe.wait_ge(hid_silu, 2 * i + 4)
                pe.wait_ge(ht_ready, i + 1)
                for j in range(2):
                    for f in range(DC):
                        mm = pe.matmul(emb[0:HALF, j, :], g[:, f, j * HALF:(j + 1) * HALF], w2[:, f, :],
                                       start=f == 0, stop=f == DC - 1)
                mm.then_inc(emb_done, 1)

            def turn(n):
                pe.wait_ge(normed, 3 * n)
                pe.wait_ge(xnt_ready, 2 * n - 2)
                for c in range(DC):
                    for j in range(3):
                        mm = pe.transpose(tr[c][:, col[j]:col[j] + rows[j]], xn[0:rows[j], j, c * P:(c + 1) * P],
                                          ident[0:rows[j], 0:rows[j]])
                mm.then_inc(tr_done, 1)

            for i in range(2):
                hidden(i)
                embedding(i)
            with pe.Fori(2, IMGS) as i:
                hidden(i)
                turn(i)
                embedding(i)
            turn(IMGS)
            turn(IMGS + 1)

        @block.scalar
        def _(act):
            act.sem_inc(hid_silu, 2)
            act.sem_inc(xnt_ready, 2)
            act.sem_inc(h0_out, 32)
            act.sem_inc(xnt_out, 16)
            act.wait_ge(weights, 16 * 7)

            def silu(i):
                act.wait_ge(hid_done, i + 2)
                act.wait_ge(emb_done, i + 1)
                for f in range(DC):
                    act.activation(g[:, f, :], hid[:, f, :], ACT.Silu, bias=b1[:, f:f + 1]).then_inc(hid_silu, 1)

            def store_rows(i):
                act.wait_ge(ht_ready, i + 2)
                act.wait_ge(text_in, 16 * i + 16)
                act.dma_start(h0[i, 0:PATCHES, :].rearrange("(j p) d -> p j d", j=2),
                              ht[0:HALF, 0:2, :]).then_inc(h0_out, 16)
                act.dma_start(h0[i, PATCHES:TOKS, :], ht[:, 2, :]).then_inc(h0_out, 16)

            def affine(n):
                act.wait_ge(tr_done, n)
                act.wait_ge(xnt_out, 16 * n - 16)
                for c in range(DC):
                    act.activation(xnt[:, c, :], tr[c][:, 0:TOKS], ACT.Identity, bias=lnb[:, c:c + 1],
                                   scale=lnw[:, c:c + 1]).then_inc(xnt_ready, 1)
                act.wait_ge(xnt_ready, 2 * n)
                act.dma_start(xn_t[:, n - 2, :].rearrange("(c p) b -> p c b", p=P), xnt[:]).then_inc(xnt_out, 16)

            for i in range(2):
                silu(i)
                store_rows(i)
            with act.Fori(2, IMGS) as i:
                silu(i)
                affine(i)
                store_rows(i)
            affine(IMGS)
            affine(IMGS + 1)

        @block.vector
        def _(dve):
            dve.memset(ht[:], 0.0).then_inc(init, 1)
            dve.memset(neg[:], -0.5).then_inc(init, 1)
            dve.memset(eps[:], EPS).then_inc(init, 1)
            dve.sem_inc(init, 1)
            dve.sem_inc(ht_ready, 1)
            dve.sem_inc(normed, 3)
            dve.wait_ge(weights, 16 * 7)
            dve.wait_ge(init, 4)
            with dve.Fori(0, IMGS) as i:
                dve.wait_ge(emb_done, i + 2)
                dve.wait_ge(h0_out, 32 * i + 32)
                dve.wait_ge(normed, 3 * i + 3)
                dve.tensor_tensor(ht[0:HALF, 0:2, :], emb[0:HALF], b2[0:HALF].broadcast_to([HALF, 2, D]),
                                  ALU.add).then_inc(ht_ready, 1)
                dve.wait_ge(ht_ready, i + 2)
                dve.wait_ge(text_in, 16 * i + 16)
                for j in range(3):
                    dve.bn_stats(st[:, j, :], ht[:, j, :]).then_inc(stats, 1)
                dve.wait_ge(rstd, i + 1)
                dve.wait_ge(stats, 3 * i + 3)
                dve.memset(hold[:], 0.0)
                for j in range(3):
                    dve.bn_aggr(mv[:, j, :], st[:, j, :]).then_inc(aggr, 1)
                dve.wait_ge(rstd, i + 2)
                dve.wait_ge(tr_done, i + 1)
                for j in range(3):
                    dve.tensor_scalar(xn[:, j, :], ht[:, j, :], mv[:, j, 0:1], ln[:, 5, j:j + 1],
                                      ALU.subtract, ALU.mult).then_inc(normed, 1)

        @block.gpsimd
        def _(pool):
            pool.sem_inc(rstd, 1)
            pool.sem_inc(hid_done, 1)
            pool.sem_inc(emb_done, 1)
            pool.sem_inc(tr_done, 1)
            pool.wait_ge(init, 4)
            with pool.Fori(0, IMGS) as i:
                pool.wait_ge(aggr, 3 * i + 3)
                pool.wait_ge(normed, 3 * i + 3)
                norm_chain(pool, mv, neg, eps, ln, pool_step, 6 * i).then_inc(rstd, 1)


def norm_chain(pool, mv, neg, eps, ln, step, base):
    var = mv[:, :, 1]
    pool.tensor_tensor(ln[:, 0, :], var, eps[:], ALU.add).then_inc(step, 1)
    pool.wait_ge(step, base + 1)
    pool.tensor_tensor(ln[:, 1, :], ln[:, 0, :], neg[:], ALU.pow).then_inc(step, 1)
    pool.wait_ge(step, base + 2)
    pool.tensor_tensor(ln[:, 2, :], ln[:, 1, :], ln[:, 1, :], ALU.mult).then_inc(step, 1)
    pool.wait_ge(step, base + 3)
    pool.tensor_tensor(ln[:, 3, :], ln[:, 2, :], var, ALU.mult).then_inc(step, 1)
    pool.wait_ge(step, base + 4)
    pool.tensor_tensor(ln[:, 3, :], ln[:, 3, :], eps[:], ALU.add).then_inc(step, 1)
    pool.wait_ge(step, base + 5)
    pool.tensor_tensor(ln[:, 4, :], ln[:, 3, :], neg[:], ALU.pow).then_inc(step, 1)
    pool.wait_ge(step, base + 6)
    return pool.tensor_tensor(ln[:, 5, :], ln[:, 4, :], ln[:, 1, :], ALU.mult)


def ema_stage(nc, T, kpad, xn_t, mx):
    QD = 4
    GQ = GROUPS // QD
    with Stage(nc, "ema") as s:
        x = s.sb("x", [P, GROUPS, TOKS])
        toep = s.sb("toep", [P, GROUPS, P])
        o = s.sb("o", [TC, 2, IMGS, P])
        banks = [s.ps(f"bank{k}", [P, 4, P]) for k in range(4)]
        cleared, toep_in, stored = s.sem("cleared"), s.sem("toep_in"), [s.sem(f"stored{k}") for k in range(2)]
        x_in = [s.sem(f"x_in{q}") for q in range(QD)]
        conv_done, silu_done = s.sem("conv_done"), s.sem("silu_done")
        block = s.block()
        work = [(dh, bc, k) for dh in range(2) for bc in range(3) for k in range(8)]

        @block.sync
        def _(sp):
            view = xn_t.rearrange("(g j) s b -> (j s) g b", j=4)
            for q in range(QD):
                sp.dma_start(x[:, q * GQ:(q + 1) * GQ, :], view[:, q * GQ:(q + 1) * GQ, :]).then_inc(x_in[q], 16)
            for t in range(6):
                dh, bc = divmod(t, 3)
                sp.wait_ge(silu_done, 8 * t + 8)
                sp.dma_start(mx[bc * TC:(bc + 1) * TC, :, dh * P:(dh + 1) * P],
                             o[:, t % 2]).then_inc(stored[t % 2], 16)
            for k in range(2):
                sp.wait_ge(stored[k], 48)

        @block.gpsimd
        def _(pool):
            pool.memset(toep[:], 0.0).then_inc(cleared, 1)

        @block.scalar
        def _(act):
            act.wait_ge(cleared, 1)
            for j in range(4):
                rows = kpad.rearrange("(g j) k -> j g k", j=4)[j, :, IMGS:IMGS + IMGS * 63]
                act.dma_start(toep[IMGS * j:IMGS * (j + 1), :, IMGS * j:IMGS * (j + 1)],
                              rows.rearrange("g (s k) -> s g k", k=63)[:, :, 0:IMGS]).then_inc(toep_in, 16)
            for n, (dh, bc, k) in enumerate(work):
                t = n // 8
                act.wait_ge(conv_done, n + 1)
                if k == 0 and t >= 2:
                    act.wait_ge(stored[t % 2], 16 * (t // 2))
                act.activation(o[:, t % 2].rearrange("p t (k d) -> p k d t", k=8)[:, k],
                               banks[n % 4][0:TC].rearrange("p g (j t) -> p (g j) t", j=4), ACT.Silu).then_inc(silu_done, 1)

        @block.tensor
        def _(pe):
            pe.wait_ge(toep_in, 64)
            for n, (dh, bc, k) in enumerate(work):
                if bc == 0 and k % 4 == 0:
                    pe.wait_ge(x_in[2 * dh + k // 4], 16)
                if n >= 4:
                    pe.wait_ge(silu_done, n - 3)
                for m in range(4):
                    gr = 32 * dh + 4 * k + m
                    mm = pe.matmul(banks[n % 4][0:TC, m, :], x[:, gr, bc * TC:(bc + 1) * TC], toep[:, gr, :],
                                   start=True, stop=True)
                mm.then_inc(conv_done, 1)


ERF_P = (-2.72614225801306e-10, 2.77068142495902e-08, -2.10102402082508e-06, -5.69250639462346e-05,
         -7.34990630326855e-04, -2.95459980854025e-03, -1.60960333262415e-02)
ERF_Q = (-1.45660718464996e-05, -2.13374055278905e-04, -1.68282697438203e-03, -7.37332916720468e-03,
         -1.42647390514189e-02)
EXPERTS = 8
MU, SIGMA = 0.707107, 0.282095
ERF_SCALE = 1.0 / (SIGMA * 2.0 ** 0.5)
COLS = 12
GRP = TOKS // COLS
N = COLS * IMGS


class Chain:

    def __init__(self, eng, sem, base):
        self.eng, self.sem, self.at = eng, sem, base

    def __call__(self, ins):
        ins.then_inc(self.sem, 1)
        self.at = self.at + 1
        self.eng.wait_ge(self.sem, self.at)


def mix_stage(nc, T, h0, mx, h2):
    with Stage(nc, "mix") as s:
        ident = s.sb("ident", [P, P])
        lnw, lnb = s.sb("lnw", [P, DC]), s.sb("lnb", [P, DC])
        wv, wzr, wuh = s.sb("wv", [P, DC, 512]), s.sb("wzr", [P, DC, 640]), s.sb("wuh", [P, DC, 512])
        wh = s.sb("wh", [P, 4, D])
        bv, buh = s.sb("bv", [P, 512]), s.sb("buh", [P, 512])
        bzr = s.sb("bzr", [P, 5])
        bh = s.sb("bh", [P, D])
        qk = s.sb("qk", [P, 4])
        rot = s.sb("rot", [P, 4])
        trig = s.sb("trig", [P, 2, IMGS])
        rotated = s.sb("rotated", [P, 3, IMGS])
        rotb = s.sb("rotb", [P, 4, IMGS])
        biasc = s.sb("biasc", [P, 1, IMGS])
        w1 = s.sb("w1", [P, 2, EXPERTS + 2, DC, D], F32R)
        w2 = s.sb("w2", [P, 2, EXPERTS + 1, DC, D], F32R)
        raw = s.sb("raw", [P, 2, 2, DC, D])
        wr = s.sb("wr", [P, DC, EXPERTS + 1])
        lower = s.sb("lower", [P, 1, EXPERTS * EXPERTS])
        neg, eps, hold = s.sb("neg", [P, 3]), s.sb("eps", [P, 3]), s.sb("hold", [P, 1])
        ebase = s.sb("ebase", [P, 3 * EXPERTS])

        ht, mt = s.sb("ht", [P, 3, D]), s.sb("mt", [P, 3, D])
        st, mv, ln = s.sb("st", [P, 3, 6]), s.sb("mv", [P, 3, 2]), s.sb("ln", [P, 6, 3])
        x1, xn, hx = s.sb("x1", [P, 3, D]), s.sb("xn", [P, 3, D]), s.sb("hx", [P, 3, D])
        mxt, xnt = s.sb("mxt", [P, DC, N]), s.sb("xnt", [P, DC, N])
        zt, rt = s.sb("zt", [P, N]), s.sb("rt", [P, 4, N])
        qt, kt = s.sb("qt", [P, N]), s.sb("kt", [P, N])
        v = s.sb("v", [P, 3, 512])
        er = s.sb("er", [P, 5, 3 * IMGS])
        at = s.sb("at", [P, 3, P])
        hrt = s.sb("hrt", [P, 4, N])
        uh = s.sb("uh", [P, 3, 512])
        h1 = s.sb("h1", [P, 3, D])
        st2, mv2, ln2 = s.sb("st2", [P, 3, 6]), s.sb("mv2", [P, 3, 2]), s.sb("ln2", [P, 2, 3])
        xf = s.sb("xf", [P, 3, D])
        xft = s.sb("xft", [P, DC, N])
        lg = s.sb("lg", [P, 3, EXPERTS + 1])
        rs = s.sb("rs", [P, 3, 3])
        ex = s.sb("ex", [P, 2, 3, EXPERTS])
        pr = s.sb("pr", [P, 3, EXPERTS])
        cmp = s.sb("cmp", [P, 2, 3, EXPERTS * EXPERTS])
        rank = s.sb("rank", [P, 3, EXPERTS])
        gate = s.sb("gate", [P, 3, 1])
        comb = s.sb("comb", [P, 3, EXPERTS + 1])
        xfr = s.sb("xfr", [P, 2, DC, N], F32R)
        he = s.sb("he", [P, DC, N])
        her = s.sb("her", [P, 2, 2, DC, N], F32R)
        sg = s.sb("sg", [P, DC, N])
        acc = s.sb("acc", [P, 3, D])

        bank = [s.ps(f"bank{k}", [P, 512]) for k in range(4)]
        up = s.ps("up", [P, DC, 512])
        down = s.ps("down", [P, 2, 512])

        names = ("weights init rot_step bias_done ht_in mt_in stats aggr rstd pool_step x1_ready xn_ready hx_ready "
                 "mt_turned xn_turned mxt_ready xnt_ready zr_done zr_silu qk_ready sc_done erf_step at_ready v_done "
                 "vb_ready v_ready av_done hr_ready uh_done pre_ready uh_act comb_step h1_ready stats2 aggr2 rstd2 "
                 "pool_step2 xf_ready xft_done xft_ready rt_done gate_tanh route_step exp_done comb_ready up_done "
                 "eh_silu sh_mult down_done sum_done h2_out raw_high raw_used xft_high xft_low he_high he_low sh_high").split()
        (weights, init, rot_step, bias_done, ht_in, mt_in, stats, aggr, rstd, pool_step, x1_ready, xn_ready, hx_ready,
         mt_turned, xn_turned, mxt_ready, xnt_ready, zr_done, zr_silu, qk_ready, sc_done, erf_step, at_ready, v_done,
         vb_ready, v_ready, av_done, hr_ready, uh_done, pre_ready, uh_act, comb_step, h1_ready, stats2, aggr2, rstd2,
         pool_step2, xf_ready, xft_done, xft_ready, rt_done, gate_tanh, route_step, exp_done, comb_ready, up_done,
         eh_silu, sh_mult, down_done, sum_done, h2_out, raw_high, raw_used, xft_high, xft_low, he_high, he_low, sh_high) = [s.sem(x) for x in names]
        block = s.block()
        raw_in = [s.sem(f"raw_in{k}") for k in range(2)]
        NERF, NROUTE = 16, 11
        INIT = 7
        loads = [(ident[:], T["ident"]), (lnw[:], T["ln_w"]), (lnb[:], T["ln_b"]),
                 (wv[:], T["wv"].rearrange("(c p) n -> p c n", p=P)),
                 (wzr[:], T["wzr"].rearrange("(c p) n -> p c n", p=P)),
                 (wuh[:], T["wuh"].rearrange("(c p) n -> p c n", p=P)),
                 (wh[:], T["wh"].rearrange("(c p) n -> p c n", p=P)),
                 (bv[:], T["bv"].broadcast_to([P, 512])), (buh[:], T["buh"].broadcast_to([P, 512])),
                 (bh[:], T["bh"].broadcast_to([P, D])), (bzr[:], T["bzr"]), (qk[:], T["qk"]), (rot[:], T["rot"]),
                 (trig[:], T["trig"]),
                 (wr[:], T["wr"].rearrange("(c p) n -> p c n", p=P)),
                 (lower[:, 0, :], T["lower"].broadcast_to([P, EXPERTS * EXPERTS]))]
        LOADED = 16 * len(loads)
        pairs = [(w, e, 2, T[name][e:e + 2].rearrange("e (c p) n -> p e c n", p=P))
                 for w, name in ((w1, "w1"), (w2, "w2")) for e in range(0, EXPERTS, 2)]
        pairs += [(w1, EXPERTS, 2, T["wgu"].rearrange("(c p) (e n) -> p e c n", p=P, e=2)),
                  (w2, EXPERTS, 1, T["wsd"].rearrange("(c p) (e n) -> p e c n", p=P, e=1))]
        PARTS = ((1, 0), (0, 1), (0, 0))

        @block.sync
        def _(sp):
            for dst, src in loads:
                sp.dma_start(dst, src).then_inc(weights, 16)
            for k, (_, _, count, src) in enumerate(pairs):
                if k >= 2:
                    sp.wait_ge(raw_used, k - 1)
                sp.dma_start(raw[:, k % 2, 0:count], src).then_inc(raw_in[k % 2], 16)
            with sp.Fori(0, GRP) as n:
                sp.wait_ge(hx_ready, n + 1)
                for b in range(4):
                    sp.dma_start(ht[IMGS * b:IMGS * (b + 1)],
                                 h0.rearrange("t (g j b) d -> g b t j d", j=3, b=4)[n, b]
                                 ).then_inc(ht_in, 16)
                sp.wait_ge(mt_turned, n + 1)
                sp.dma_start(mt[:], mx.rearrange("(g j b) t d -> g (b t) j d", j=3, b=4)[n]
                             ).then_inc(mt_in, 16)
            sp.wait_ge(h2_out, 64 * GRP + 64)

        @block.tensor
        def _(pe):
            pe.wait_ge(weights, LOADED)

            def turn_in(n):
                pe.wait_ge(mt_in, 16 * n + 16)
                pe.wait_ge(xft_ready, 2 * n + 2)
                pe.wait_ge(hr_ready, 3 * n + 3)
                pe.wait_ge(route_step, NROUTE * n + 1)
                for c in range(DC):
                    for j in range(3):
                        mm = pe.transpose(bank[c][:, j * P:(j + 1) * P], mt[:, j, c * P:(c + 1) * P], ident[:])
                mm.then_inc(mt_turned, 1)
                pe.wait_ge(xn_ready, 3 * n + 3)
                pe.wait_ge(pre_ready, 3 * n + 3)
                for c in range(DC):
                    for j in range(3):
                        mm = pe.transpose(bank[2 + c][:, j * P:(j + 1) * P], xn[:, j, c * P:(c + 1) * P], ident[:])
                mm.then_inc(xn_turned, 1)

            def z_r(n, q):
                if q == 0:
                    pe.wait_ge(mxt_ready, 2 * n + 4)
                if q == 2:
                    pe.wait_ge(xnt_ready, 2 * n + 4)
                if q == 4:
                    pe.wait_ge(zr_silu, 5 * n + 1)
                for c in range(DC):
                    mm = pe.matmul(bank[q % 4][:, 0:N], wzr[:, c, q * P:(q + 1) * P], mxt[:, c, :],
                                   start=c == 0, stop=c == DC - 1)
                mm.then_inc(zr_done, 1)

            def scores(n):
                pe.wait_ge(qk_ready, 2 * n + 4)
                pe.wait_ge(zr_silu, 5 * n + 2)
                for j in range(3):
                    for b in range(4):
                        o = j * P + b * IMGS
                        mm = pe.matmul(bank[1][b * IMGS:(b + 1) * IMGS, j * IMGS:(j + 1) * IMGS],
                                       kt[:, o:o + IMGS], qt[:, o:o + IMGS], start=True, stop=True)
                mm.then_inc(sc_done, 1)

            def values(n):
                pe.wait_ge(zr_silu, 5 * n + 5)
                for j, k in enumerate((0, 2, 3)):
                    for c in range(DC):
                        mm = pe.matmul(bank[k][:, :], xnt[:, c, j * P:(j + 1) * P], wv[:, c, :],
                                       start=c == 0, stop=c == DC - 1)
                    mm.then_inc(v_done, 1)

            def attend(n):
                pe.wait_ge(at_ready, 4 * n + 4)
                pe.wait_ge(v_ready, 3 * n + 6)
                for j, k in enumerate((1, 0, 2)):
                    for f in range(4):
                        mm = pe.matmul(bank[k][:, f * P:(f + 1) * P], v[:, j, f * P:(f + 1) * P], at[:, j, :],
                                       start=True, stop=True)
                    mm.then_inc(av_done, 1)

            def update(n):
                for j, k in enumerate((3, 1, 0)):
                    pe.wait_ge(hr_ready, 3 * n + 6)
                    for c in range(DC):
                        pe.matmul(bank[k][:, :], mxt[:, c, j * P:(j + 1) * P], wuh[:, c, :], start=c == 0, stop=False,
                                  skip_group_check=True)
                    for f in range(4):
                        mm = pe.matmul(bank[k][:, D:], hrt[:, f, j * P:(j + 1) * P], wh[:, f, :],
                                       start=False, stop=f == 3, skip_group_check=True)
                    mm.then_inc(uh_done, 1)

            def turn_out(n):
                pe.wait_ge(xf_ready, 3 * n + 3)
                pe.wait_ge(pre_ready, 3 * n + 6)
                for c, k in enumerate((0, 2)):
                    for j in range(3):
                        mm = pe.transpose(bank[k][:, j * P:(j + 1) * P], xf[:, j, c * P:(c + 1) * P], ident[:])
                mm.then_inc(xft_done, 1)

            def router(n):
                pe.wait_ge(xft_ready, 2 * n + 4)
                for j in range(3):
                    for c in range(DC):
                        mm = pe.matmul(bank[1][:, 16 * j:16 * j + EXPERTS + 1], xft[:, c, j * P:(j + 1) * P],
                                       wr[:, c, :], start=c == 0, stop=c == DC - 1)
                mm.then_inc(rt_done, 1)

            def up_proj(m, e):
                if e == 0:
                    pe.wait_ge(sh_mult, m + 1)
                    pe.wait_ge(xft_low, m + 2)
                else:
                    pe.wait_ge(eh_silu, 9 * m + e)
                for f in range(DC):
                    for c in range(DC):
                        for a, b in PARTS:
                            mm = pe.matmul(up[:, f, 0:N], w1[:, a, e, c, f * P:(f + 1) * P], xfr[:, b, c, :],
                                           start=(a, c) == (1, 0), stop=(a, b, c) == (0, 0, DC - 1))
                mm.then_inc(up_done, 1)

            def down_proj(m, e):
                pe.wait_ge(he_low, 9 * m + e + 2)
                pe.wait_ge(sum_done, 27 * m + 3 * e + 27)
                for j in range(3):
                    for f in range(DC):
                        for a, b in PARTS:
                            mm = pe.matmul(down[:, j // 2, (j % 2) * D:(j % 2 + 1) * D],
                                           her[:, e % 2, b, f, j * P:(j + 1) * P], w2[:, a, e, f, :],
                                           start=(a, f) == (1, 0), stop=(a, b, f) == (0, 0, DC - 1))
                mm.then_inc(down_done, 1)

            def attention(n):
                turn_in(n)
                for q in range(5):
                    z_r(n, q)
                scores(n)
                values(n)
                attend(n)
                update(n)
                turn_out(n)

            def body(m, n):
                between = {}
                if n is not None:
                    between = {0: (lambda: turn_in(n),), 1: (lambda: z_r(n, 0), lambda: z_r(n, 1), lambda: z_r(n, 2)),
                               2: (lambda: z_r(n, 3), lambda: z_r(n, 4), lambda: scores(n)), 3: (lambda: values(n),),
                               4: (lambda: attend(n),), 5: (lambda: update(n),)}
                up_proj(m, 0)
                for e in range(EXPERTS):
                    for part in between.get(e, ()):
                        part()
                    up_proj(m, e + 1)
                    down_proj(m, e)
                up_proj(m, EXPERTS + 1)
                if n is not None:
                    turn_out(n)
                down_proj(m, EXPERTS)
                if n is not None:
                    router(n)

            pe.wait_ge(rot_step, 6)
            pe.matmul(bank[0][:, 0:IMGS], rotb[:, :, :].rearrange("p a b -> p (a b)"), rotated[:, 0, :],
                      start=True, stop=True).then_inc(bias_done, 1)
            pe.wait_ge(init, INIT)
            attention(0)
            router(0)
            with pe.Fori(0, GRP - 1) as m:
                body(m, m + 1)
            body(GRP - 1, None)

        @block.scalar
        def _(act):
            for k, (w, e, count, _) in enumerate(pairs):
                act.wait_ge(raw_in[k % 2], 16 * (k // 2) + 16)
                act.activation(w[:, 0, e:e + count], raw[:, k % 2, 0:count], ACT.Copy).then_inc(raw_high, 1)
            act.wait_ge(weights, LOADED)
            act.wait_ge(init, INIT)

            def evac_in(n):
                act.wait_ge(mt_turned, n + 2)
                act.wait_ge(uh_done, 3 * n + 3)
                for c in range(DC):
                    act.activation(mxt[:, c, :], bank[c][:, 0:N], ACT.Copy).then_inc(mxt_ready, 1)
                act.wait_ge(xn_turned, n + 2)
                act.wait_ge(v_done, 3 * n + 3)
                for c in range(DC):
                    act.activation(xnt[:, c, :], bank[2 + c][:, 0:N], ACT.Identity, bias=lnb[:, c:c + 1],
                                   scale=lnw[:, c:c + 1]).then_inc(xnt_ready, 1)

            def evac_zr(n, q):
                act.wait_ge(zr_done, 5 * n + q + 1)
                if q == 0:
                    act.wait_ge(qk_ready, 2 * n + 2)
                if q == 1:
                    act.wait_ge(hr_ready, 3 * n + 3)
                act.activation(zt[:] if q == 0 else rt[:, q - 1, :], bank[q % 4][:, 0:N], ACT.Silu,
                               bias=bzr[:, q:q + 1]).then_inc(zr_silu, 1)

            def silu_v(n):
                act.wait_ge(av_done, 3 * n + 3)
                for j in range(3):
                    act.wait_ge(vb_ready, 3 * n + j + 1)
                    act.activation(v[:, j, :], v[:, j, :], ACT.Silu).then_inc(v_ready, 1)

            def act_uh(n):
                for j in range(3):
                    act.wait_ge(pre_ready, 3 * n + j + 4)
                    act.activation(uh[:, j, 0:D], uh[:, j, 0:D], ACT.Tanh, scale=0.5).then_inc(uh_act, 1)
                    act.activation(uh[:, j, D:], uh[:, j, D:], ACT.Silu).then_inc(uh_act, 1)

            def evac_out(n):
                act.wait_ge(xft_done, n + 2)
                for c, k in enumerate((0, 2)):
                    act.activation(xft[:, c, :], bank[k][:, 0:N], ACT.Copy).then_inc(xft_ready, 1)
                act.wait_ge(xft_ready, 2 * n + 4)
                act.activation(xfr[:, 0], xft[:], ACT.Copy).then_inc(xft_high, 1)

            def tanh_gate(n):
                act.wait_ge(route_step, NROUTE * n + 2)
                act.wait_ge(comb_ready, n + 1)
                act.activation(gate[:], lg[:, :, EXPERTS:], ACT.Tanh,
                               scale=0.5).then_inc(gate_tanh, 1)

            def silu_e(m, e):
                act.wait_ge(up_done, 10 * m + e + 1)
                if e == EXPERTS:
                    act.wait_ge(sh_mult, m + 1)
                    act.activation(sg[:], up[:, :, 0:N], ACT.Silu).then_inc(eh_silu, 1)
                    return
                act.wait_ge(he_low, 9 * m + e + 1)
                act.activation(he[:], up[:, :, 0:N], ACT.Silu).then_inc(eh_silu, 1)
                act.wait_ge(eh_silu, 9 * m + e + 1)
                act.wait_ge(down_done, 9 * m + (2, 1)[e] if e < 2 else 9 * m + e + 1)
                act.activation(her[:, e % 2, 0], he[:], ACT.Copy).then_inc(he_high, 1)

            def store(m):
                act.wait_ge(sum_done, 27 * m + 54)
                for b in range(4):
                    act.dma_start(h2.rearrange("t (g j b) d -> g b t j d", j=3, b=4)[m, b],
                                  acc[IMGS * b:IMGS * (b + 1)]).then_inc(h2_out, 16)

            def attention(n):
                evac_in(n)
                for q in range(5):
                    evac_zr(n, q)
                silu_v(n)
                act_uh(n)
                evac_out(n)
                tanh_gate(n)

            def body(m, n):
                silu_e(m, 0)
                evac_in(n)
                silu_e(m, 1)
                for q in range(3):
                    evac_zr(n, q)
                silu_e(m, 2)
                for q in range(3, 5):
                    evac_zr(n, q)
                silu_e(m, 3)
                silu_v(n)
                silu_e(m, 4)
                silu_e(m, 5)
                act_uh(n)
                for e in range(6, EXPERTS + 1):
                    silu_e(m, e)
                evac_out(n)
                tanh_gate(n)
                store(m)

            attention(0)
            with act.Fori(0, GRP - 1) as m:
                body(m, m + 1)
            for e in range(9):
                silu_e(GRP - 1, e)
            store(GRP - 1)

        @block.gpsimd
        def _(pool):
            for sem, credit in ((hx_ready, 1), (mt_turned, 1), (xn_turned, 1), (uh_done, 3), (v_done, 3), (qk_ready, 2),
                                (hr_ready, 3), (av_done, 3), (comb_ready, 1), (down_done, 2), (he_low, 1), (xft_low, 1), (h1_ready, 1),
                                (xft_done, 1), (rstd, 1), (rstd2, 1), (xft_ready, 2), (pre_ready, 3), (gate_tanh, 1),
                                (route_step, 1), (sc_done, 1), (v_ready, 3), (uh_act, 6), (sum_done, 27), (sh_mult, 1),
                                (h2_out, 64), (mxt_ready, 2), (xnt_ready, 2), (exp_done, 1)):
                if credit:
                    pool.sem_inc(sem, credit)
            pool.memset(neg[:], -0.5).then_inc(init, 1)
            pool.memset(eps[:], EPS).then_inc(init, 1)
            pool.memset(ebase[:], float(np.float32(np.e))).then_inc(init, 1)
            pool.memset(at[:], 0.0).then_inc(init, 1)
            pool.sem_inc(init, 1)
            pool.wait_ge(init, INIT)

            def rsqrt1(n):
                pool.wait_ge(aggr, 3 * n + 3)
                pool.wait_ge(hx_ready, n + 1)
                norm_chain(pool, mv, neg, eps, ln, pool_step, 6 * n).then_inc(rstd, 1)

            def rsqrt2(n):
                pool.wait_ge(aggr2, 3 * n + 3)
                if not isinstance(n, int) or n > 0:
                    pool.wait_ge(xf_ready, 3 * n)
                pool.tensor_tensor(ln2[:, 0, :], mv2[:, :, 1], eps[:], ALU.add).then_inc(pool_step2, 1)
                pool.wait_ge(pool_step2, n + 1)
                pool.tensor_tensor(ln2[:, 1, :], ln2[:, 0, :], neg[:], ALU.pow).then_inc(rstd2, 1)

            def exps(n):
                pool.wait_ge(route_step, NROUTE * n + 4)
                pool.tensor_tensor(ex[:, 1].rearrange("p j e -> p (j e)"), ebase[:],
                                   ex[:, 0].rearrange("p j e -> p (j e)"), ALU.pow).then_inc(exp_done, 1)

            rsqrt1(0)
            rsqrt2(0)
            rsqrt1(1)
            exps(0)
            with pool.Fori(1, GRP - 1) as n:
                rsqrt2(n)
                rsqrt1(n + 1)
                exps(n)
            rsqrt2(GRP - 1)
            exps(GRP - 1)

        @block.vector
        def _(dve):
            for k, (w, e, count, _) in enumerate(pairs):
                dve.wait_ge(raw_high, k + 1)
                dve.tensor_tensor(w[:, 1, e:e + count], raw[:, k % 2, 0:count], w[:, 0, e:e + count], ALU.subtract
                                  ).then_inc(raw_used, 1)
            dve.wait_ge(weights, LOADED)
            one = Chain(dve, rot_step, 0)
            one(dve.tensor_scalar(rotated[:, 1, :], trig[:, 1, :], rot[:, 1:2], None, ALU.mult))
            one(dve.scalar_tensor_tensor(rotated[:, 0, :], trig[:, 0, :], rot[:, 0:1], rotated[:, 1, :],
                                         ALU.mult, ALU.add))
            one(dve.tensor_scalar(rotated[:, 1, :], trig[:, 1, :], rot[:, 3:4], None, ALU.mult))
            one(dve.scalar_tensor_tensor(rotated[:, 2, :], trig[:, 0, :], rot[:, 2:3], rotated[:, 1, :],
                                         ALU.mult, ALU.add))
            one(dve.tensor_copy(rotb[:], rotated[:, 2:3, :].broadcast_to([P, 4, IMGS])))
            one(dve.tensor_tensor(buh[:, D:], buh[:, D:], bh[:], ALU.add))
            dve.wait_ge(bias_done, 1)
            dve.tensor_scalar(biasc[:, 0, :], bank[0][:, 0:IMGS], ERF_SCALE, -MU * ERF_SCALE,
                              ALU.mult, ALU.add).then_inc(init, 1)
            dve.sem_inc(init, 1)
            dve.wait_ge(init, INIT)

            def stats_in(n):
                dve.wait_ge(ht_in, 64 * n + 64)
                for j in range(3):
                    dve.bn_stats(st[:, j, :], ht[:, j, :]).then_inc(stats, 1)
                dve.wait_ge(rstd, n + 1)
                dve.wait_ge(stats, 3 * n + 3)
                dve.memset(hold[:], 0.0)
                for j in range(3):
                    dve.bn_aggr(mv[:, j, :], st[:, j, :]).then_inc(aggr, 1)

            def norm_twice(n):
                dve.wait_ge(rstd, n + 2)
                dve.wait_ge(xn_turned, n + 1)
                for j in range(3):
                    dve.tensor_scalar(xn[:, j, :], ht[:, j, :], mv[:, j, 0:1], ln[:, 5, j:j + 1],
                                      ALU.subtract, ALU.mult).then_inc(xn_ready, 1)

            def norm_once(n):
                dve.wait_ge(h1_ready, n + 1)
                for j in range(3):
                    dve.tensor_scalar(x1[:, j, :], ht[:, j, :], mv[:, j, 0:1], ln[:, 1, j:j + 1],
                                      ALU.subtract, ALU.mult).then_inc(x1_ready, 1)
                dve.wait_ge(x1_ready, 3 * n + 3)
                dve.tensor_tensor(hx[:], ht[:], x1[:], ALU.add).then_inc(hx_ready, 1)

            def make_qk(n):
                dve.wait_ge(zr_silu, 5 * n + 1)
                dve.wait_ge(sc_done, n + 1)
                dve.tensor_scalar(qt[:], zt[:], qk[:, 0:1], qk[:, 2:3], ALU.mult, ALU.add).then_inc(qk_ready, 1)
                dve.tensor_scalar(kt[:], zt[:], qk[:, 1:2], qk[:, 3:4], ALU.mult, ALU.add).then_inc(qk_ready, 1)

            def erf(n):
                dve.wait_ge(sc_done, n + 2)
                step = Chain(dve, erf_step, NERF * n)
                x, xx, p, q, iq = (er[:, k, :] for k in range(5))
                step(dve.scalar_tensor_tensor(x.rearrange("p (j l) -> p j l", j=3),
                                              bank[1][:, 0:3 * IMGS].rearrange("p (j l) -> p j l", j=3),
                                              ERF_SCALE / IMGS, biasc[:].broadcast_to([P, 3, IMGS]), ALU.mult, ALU.add))
                step(dve.tensor_scalar(x, x, -4.0, 4.0, ALU.max, ALU.min))
                step(dve.tensor_tensor(xx, x, x, ALU.mult))
                step(dve.tensor_scalar(p, xx, ERF_P[0], None, ALU.mult))
                for c in ERF_P[1:-1]:
                    step(dve.scalar_tensor_tensor(p, p, c, xx, ALU.add, ALU.mult))
                dve.scalar_tensor_tensor(p, p, ERF_P[-1], x, ALU.add, ALU.mult)
                step(dve.tensor_scalar(q, xx, ERF_Q[0], None, ALU.mult))
                for c in ERF_Q[1:-1]:
                    step(dve.scalar_tensor_tensor(q, q, c, xx, ALU.add, ALU.mult))
                step(dve.tensor_scalar(q, q, ERF_Q[-1], None, ALU.add))
                step(dve.reciprocal(iq, q))
                step(dve.scalar_tensor_tensor(p, p, 0.5, iq, ALU.mult, ALU.mult))
                dve.wait_ge(av_done, 3 * n + 3)
                for b in range(4):
                    rows = slice(IMGS * b, IMGS * (b + 1))
                    dve.tensor_scalar(at[rows, :, IMGS * b:IMGS * (b + 1)],
                                      p.rearrange("p (j l) -> p j l", j=3)[rows], 0.5, None,
                                      ALU.add).then_inc(at_ready, 1)

            def bias_v(n):
                dve.wait_ge(av_done, 3 * n + 3)
                for j, k in enumerate((0, 2, 3)):
                    dve.wait_ge(v_done, 3 * n + j + 4)
                    dve.tensor_tensor(v[:, j, :], bank[k][:, :], bv[:], ALU.add).then_inc(vb_ready, 1)

            def times_r(n):
                dve.wait_ge(uh_done, 3 * n + 3)
                for j, k in enumerate((1, 0, 2)):
                    dve.wait_ge(av_done, 3 * n + j + 4)
                    dve.tensor_tensor(hrt[:, :, j * P:(j + 1) * P], bank[k][:, :].rearrange("p (f l) -> p f l", f=4),
                                      rt[:, :, j * P:(j + 1) * P], ALU.mult).then_inc(hr_ready, 1)

            def bias_uh(n):
                dve.wait_ge(h1_ready, n + 1)
                for j, k in enumerate((3, 1, 0)):
                    dve.wait_ge(uh_done, 3 * n + j + 4)
                    dve.tensor_tensor(uh[:, j, :], bank[k][:, :], buh[:], ALU.add).then_inc(pre_ready, 1)

            def combine(n):
                dve.wait_ge(uh_act, 6 * n + 12)
                dve.wait_ge(sum_done, 27 * n + 3)
                u, c = uh[:, :, 0:D], uh[:, :, D:]
                step = Chain(dve, comb_step, 2 * n)
                step(dve.tensor_tensor(c, c, x1[:], ALU.subtract))
                step(dve.scalar_tensor_tensor(c, u, 1.0, c, ALU.add, ALU.mult))
                dve.scalar_tensor_tensor(h1[:], c, 0.5, hx[:], ALU.mult, ALU.add).then_inc(h1_ready, 1)

            def stats_out(n):
                dve.wait_ge(h1_ready, n + 2)
                for j in range(3):
                    dve.bn_stats(st2[:, j, :], h1[:, j, :]).then_inc(stats2, 1)
                dve.wait_ge(stats2, 3 * n + 3)
                dve.memset(hold[:], 0.0)
                for j in range(3):
                    dve.bn_aggr(mv2[:, j, :], st2[:, j, :]).then_inc(aggr2, 1)

            def norm_out(n):
                dve.wait_ge(rstd2, n + 2)
                dve.wait_ge(xft_done, n + 1)
                for j in range(3):
                    dve.tensor_scalar(xf[:, j, :], h1[:, j, :], mv2[:, j, 0:1], ln2[:, 1, j:j + 1],
                                      ALU.subtract, ALU.mult).then_inc(xf_ready, 1)

            def route(n):
                dve.wait_ge(rt_done, n + 1)
                step = Chain(dve, route_step, NROUTE * n + 1)
                E3 = [P, 3, EXPERTS]
                dve.wait_ge(gate_tanh, n + 1)
                step(dve.tensor_copy(lg[:], bank[1][:, 0:48].rearrange("p (j x) -> p j x", j=3)[:, :, 0:EXPERTS + 1]))
                step(dve.tensor_reduce(rs[:, 0, :], lg[:, :, 0:EXPERTS], AX.X, ALU.max))
                step(dve.tensor_tensor(ex[:, 0], lg[:, :, 0:EXPERTS], rs[:, 0, :].unsqueeze(2).broadcast_to(E3), ALU.subtract))
                dve.wait_ge(exp_done, n + 2)
                step(dve.tensor_reduce(rs[:, 1, :], ex[:, 1], AX.X, ALU.add))
                step(dve.reciprocal(rs[:, 2, :], rs[:, 1, :]))
                step(dve.tensor_tensor(pr[:], ex[:, 1], rs[:, 2, :].unsqueeze(2).broadcast_to(E3), ALU.mult))
                EE = [P, 3, EXPERTS, EXPERTS]
                other = pr[:].unsqueeze(2).broadcast_to(EE)
                own = pr[:].unsqueeze(3).broadcast_to(EE)
                gt, eq = (cmp[:, k].rearrange("p j (a b) -> p j a b", a=EXPERTS) for k in range(2))
                dve.tensor_tensor(gt, other, own, ALU.is_gt)
                step(dve.tensor_tensor(eq, other, own, ALU.is_equal))
                step(dve.tensor_tensor(cmp[:, 1], cmp[:, 1], lower[:].broadcast_to([P, 3, EXPERTS * EXPERTS]), ALU.mult))
                step(dve.tensor_tensor(cmp[:, 0], cmp[:, 0], cmp[:, 1], ALU.add))
                step(dve.tensor_reduce(rank[:], gt, AX.X, ALU.add))
                dve.wait_ge(sum_done, 27 * n + 27)
                step(dve.scalar_tensor_tensor(comb[:, :, 0:EXPERTS], rank[:], 1.5, pr[:], ALU.is_lt, ALU.mult))
                dve.wait_ge(gate_tanh, n + 2)
                dve.tensor_scalar(comb[:, :, EXPERTS:], gate[:], 0.5, 0.5, ALU.mult, ALU.add).then_inc(comb_ready, 1)

            def add_expert(m, e):
                dve.wait_ge(down_done, 9 * m + e + 3)
                if e == 0:
                    dve.wait_ge(comb_ready, m + 2)
                    dve.wait_ge(h2_out, 64 * m + 64)
                else:
                    dve.wait_ge(sum_done, 27 * m + 3 * e + 27)
                for j in range(3):
                    dve.scalar_tensor_tensor(acc[:, j, :], down[:, j // 2, (j % 2) * D:(j % 2 + 1) * D],
                                             comb[:, j, e:e + 1], (h1 if e == 0 else acc)[:, j, :],
                                             ALU.mult, ALU.add).then_inc(sum_done, 1)

            def gate_shared(m):
                dve.wait_ge(up_done, 10 * m + 10)
                dve.wait_ge(eh_silu, 9 * m + 9)
                dve.wait_ge(he_low, 9 * m + 9)
                dve.tensor_tensor(he[:], sg[:], up[:, :, 0:N], ALU.mult).then_inc(sh_mult, 1)
                dve.wait_ge(sh_mult, m + 2)
                dve.wait_ge(down_done, 9 * m + 9)
                dve.tensor_copy(her[:, 0, 0], he[:]).then_inc(sh_high, 1)
                dve.wait_ge(sh_high, m + 1)
                dve.tensor_tensor(her[:, 0, 1], he[:], her[:, 0, 0], ALU.subtract).then_inc(he_low, 1)

            def low_e(m, e):
                dve.wait_ge(he_high, 8 * m + e + 1)
                dve.tensor_tensor(her[:, e % 2, 1], he[:], her[:, e % 2, 0], ALU.subtract).then_inc(he_low, 1)

            def low_xft(n):
                dve.wait_ge(xft_high, n + 1)
                dve.tensor_tensor(xfr[:, 1], xft[:], xfr[:, 0], ALU.subtract).then_inc(xft_low, 1)

            def attention(n):
                stats_in(n)
                norm_twice(n)
                norm_once(n)
                make_qk(n)
                erf(n)
                bias_v(n)
                times_r(n)
                bias_uh(n)
                combine(n)
                stats_out(n)
                norm_out(n)
                stats_in(n + 1)
                low_xft(n)
                route(n)

            def body(m, n, after):
                norm_twice(n)
                low_e(m, 0)
                norm_once(n)
                low_e(m, 1)
                add_expert(m, 0)
                make_qk(n)
                low_e(m, 2)
                add_expert(m, 1)
                low_e(m, 3)
                add_expert(m, 2)
                erf(n)
                bias_v(n)
                low_e(m, 4)
                add_expert(m, 3)
                times_r(n)
                low_e(m, 5)
                add_expert(m, 4)
                bias_uh(n)
                low_e(m, 6)
                add_expert(m, 5)
                low_e(m, 7)
                combine(n)
                add_expert(m, 6)
                stats_out(n)
                norm_out(n)
                add_expert(m, 7)
                gate_shared(m)
                if after is not None:
                    stats_in(after)
                add_expert(m, 8)
                low_xft(n)
                route(n)

            attention(0)
            with dve.Fori(0, GRP - 2) as m:
                body(m, m + 1, m + 2)
            body(GRP - 2, GRP - 1, None)
            for e in range(EXPERTS):
                low_e(GRP - 1, e)
                add_expert(GRP - 1, e)
            gate_shared(GRP - 1)
            add_expert(GRP - 1, EXPERTS)


HEADS, HD, R = 8, 64, 32
INNER = HEADS * HD
NSH = P - R
KL = 7
WIDTHS = [TOKS - TC * j for j in range(3)]
OFFS = [0, 324, 540]
SPAN = sum(WIDTHS)
TURN = 6.283185
ROUND = 1.5 * 2.0 ** 23
PREP = "tA0 tA1 gates ang x0 x1 x2 dd Csh Bsh d0 d1 d2 d3 lt Ga Gb C B z0 z1 z2".split()
AHEAD = ((2,), (3,), (4, 5), (6,), (7,), (), (), (), ())
TAIL = "og0 og1 og2 og3 wo0 wo1 wo2 xe0 xe1 re0 re1 re2".split()


class Signal:
    every = []

    def __init__(self, stage, name, per):
        self.sem, self.per = stage.sem(name), per
        Signal.every.append(self)

    def now(self, n, k=None):
        return self.per * (n + 1) + (self.per if k is None else k)

    def before(self, n, k=None):
        return self.per * n + (self.per if k is None else k)


class Ring:

    def __init__(self, stage, tag, names, banks):
        self.names, self.banks, k = names, banks, len(banks)
        assert len(names) % k == 0
        self.full = [Signal(stage, f"{tag}_full{b}", len(names) // k) for b in range(k)]
        self.read = [Signal(stage, f"{tag}_read{b}", len(names) // k) for b in range(k)]

    def at(self, name):
        i, k = self.names.index(name), len(self.banks)
        return self.banks[i % k], self.full[i % k], self.read[i % k], i // k + 1


def scan_stage(nc, T, h2, lam_d, out):
    with Stage(nc, "scan") as s:
        ident = s.sb("ident", [P, P])
        wg, wx, wz = s.sb("wg", [P, DC, 24]), s.sb("wx", [P, DC, INNER]), s.sb("wz", [P, DC, INNER])
        wrep = s.sb("wrep", [P, DC, 3, P])
        wsh = s.sb("wsh", [P, DC, 2, NSH])
        wo = s.sb("wo", [P, 4, D])
        ff = s.sb("ff", [P, 3, DC, 2 * D])
        gbias = s.sb("gbias", [P, 1, 16])
        drep = s.sb("drep", [P, 1, INNER])
        sel = s.sb("sel", [16, 4, P])
        phase = s.sb("phase", [P, 2])
        negmask = s.sb("negmask", [TC, TC])
        ones = s.sb("ones", [P, TOKS])
        neg, eps, hold = s.sb("neg", [P, 3]), s.sb("eps", [P, 3]), s.sb("hold", [P, 1])

        ht, res = s.sb("ht", [TC, 3, D]), s.sb("res", [TC, 3, D])
        st, mv, ln = s.sb("st", [TC, 3, 6]), s.sb("mv", [TC, 3, 2]), s.sb("ln", [TC, 2, 3])
        xn, xnt = s.sb("xn", [TC, 3, D]), s.sb("xnt", [P, DC, TOKS])
        gl, trt = s.sb("gl", [TC, 3, 24]), s.sb("trt", [TC, 3, 8])
        gx = s.sb("gx", [TC, 8, 3, 16])
        dd = s.sb("dd", [TC, 3, 16])
        gb = s.sb("gb", [TC, 4, 3, 8])
        al = s.sb("al", [TC, 3, 8])
        ddt, cs16 = s.sb("ddt", [16, TOKS]), s.sb("cs16", [16, TOKS])
        ta, thi = s.sb("ta", [P, TOKS]), s.sb("thi", [P, TOKS])
        th = s.sb("th", [P, 3, 4, TOKS])
        cs = s.sb("cs", [P, 4, TOKS])
        qr, kr = s.sb("qr", [P, 4, TOKS]), s.sb("kr", [P, 4, TOKS])
        csh, bsh = s.sb("csh", [NSH, TOKS]), s.sb("bsh", [NSH, TOKS])
        gsh = s.sb("gsh", [TC, SPAN])
        lam, nlam = s.sb("lam", [TC, 3, 8]), s.sb("nlam", [TC, 3, 8])
        lb = s.sb("lb", [TC, HEADS, TOKS])
        ld = s.sb("ld", [TC, HEADS, 3, TC])
        ee = s.sb("ee", [TC, HEADS, SPAN])
        mm_ = s.sb("m", [TC, 2, SPAN])
        x, xs = s.sb("x", [TC, 3, INNER]), s.sb("xs", [TC, 3, INNER])
        xg = s.sb("xg", [TC, 3, INNER])
        xb, xd, u = s.sb("xb", [TC, 3, INNER]), s.sb("xd", [TC, 3, INNER]), s.sb("u", [TC, 3, INNER])
        zs = s.sb("zs", [TC, 3, INNER])
        og, ogt = s.sb("og", [TC, 3, INNER]), s.sb("ogt", [P, 4, TOKS])
        h3, ob = s.sb("h3", [TC, 3, D]), s.sb("ob", [TC, 3, D])
        st2, mv2, ln2 = s.sb("st2", [TC, 3, 6]), s.sb("mv2", [TC, 3, 2]), s.sb("ln2", [TC, 2, 3])
        xe, xet = s.sb("xe", [TC, 3, D]), s.sb("xet", [P, DC, TOKS])
        sq = s.sb("sq", [TC, 3, 2 * D])
        ss = ff[0:TC, 1].rearrange("p c n -> p (c n)")[:, 0:3 * D].rearrange("p (j d) -> p j d", j=3)

        rot = s.ps("rot", [P, 2, 512])
        y = [s.ps(f"y{j}", [P, 512]) for j in range(3)]
        xbank = [s.ps(f"x{k}", [P, 512]) for k in range(2)]
        tbank = [s.ps("tail", [P, 512])]

        Signal.every = []
        prep, tail = Ring(s, "prep", PREP, xbank), Ring(s, "tail", TAIL, tbank)
        NG = KL + 16
        sigs = dict(ht_in=16, stats=3, aggr=3, rs_step=1, rstd=1, xn_ready=3, gate_tanh=1, g_step=NG, u_exp=1, al_exp=1,
                    scanned=1, d_step=4, turns=4, angles=1, r_step=1, sin_done=1, lam_step=1, lam_ready=1, lam_out=16, lb_in=16,
                    shifted=32, xb_ready=1, ug_ready=1, u_ready=1, xd_ready=1, ld_ready=24, e_done=40, rot_done=8,
                    a_done=8, m_ready=8, y_done=8, y_read=3, og_ready=3, res_in=16, h3_ready=3, stats2=3, aggr2=3,
                    rs_step2=1, rstd2=1, xe_ready=3, ss_ready=1, root=1, h4_ready=1, stored=16)
        S = {k: Signal(s, k, per) for k, per in sigs.items()}
        weights, init, ffs = s.sem("weights"), s.sem("init"), s.sem("ffs")
        block = s.block()
        INIT = 7

        def wait(eng, name, value):
            eng.wait_ge(S[name].sem, value)

        def now(eng, name, n, k=None):
            eng.wait_ge(S[name].sem, S[name].now(n, k))

        def before(eng, name, n, k=None):
            eng.wait_ge(S[name].sem, S[name].before(n, k))

        def filled(eng, ring, n, name):
            bank, full, read, k = ring.at(name)
            eng.wait_ge(full.sem, full.now(n, k))
            return bank, read.sem

        def was_read(eng, ring, n, name):
            _, _, read, k = ring.at(name)
            eng.wait_ge(read.sem, read.now(n, k))

        def read_before(eng, ring, n, name):
            _, _, read, k = ring.at(name)
            eng.wait_ge(read.sem, read.before(n, k))

        def used_before(eng, ring, n, name):
            _, full, _, k = ring.at(name)
            eng.wait_ge(full.sem, full.before(n, k))

        loads = [(ident[:], T["ident"]), (wg[:], T["wg"].rearrange("(c p) n -> p c n", p=P)),
                 (wx[:], T["wx"].rearrange("(c p) n -> p c n", p=P)),
                 (wz[:], T["wz"].rearrange("(c p) n -> p c n", p=P)),
                 (wrep[:], T["wrep"].rearrange("(c p) k n -> p c k n", p=P)),
                 (wsh[:], T["wsh"].rearrange("(c p) k n -> p c k n", p=P)),
                 (wo[:], T["wo"].rearrange("(c p) n -> p c n", p=P)),
                 (ff[:, 0], T["ff"].rearrange("(c p) n -> p c n", p=P)),
                 (ff[:, 1], T["ffn"].rearrange("(c p) n -> p c n", p=P)),
                 (gbias[:, 0, :], T["gbias"].broadcast_to([P, 16])),
                 (drep[:, 0, :], T["drep"].broadcast_to([P, INNER])),
                 (sel[:], T["sel"]), (phase[:], T["phase"]), (negmask[:], T["negmask"])]
        LOADED = 16 * len(loads)

        def run(eng, body):
            body(0, None, None, None)
            body(1, 0, None, None)
            body(2, 1, 0, None)
            with eng.Fori(2, IMGS - 1) as i:
                body(i + 1, i, i - 1, i - 2)
            body(None, IMGS - 1, IMGS - 2, IMGS - 3)
            body(None, None, IMGS - 1, IMGS - 2)
            body(None, None, None, IMGS - 1)

        @block.sync
        def _(sp):
            for dst, src in loads:
                sp.dma_start(dst, src).then_inc(weights, 16)

            def load(n):
                before(sp, "xn_ready", n)
                sp.dma_start(ht[:], h2[n].rearrange("(j p) d -> p j d", p=TC)).then_inc(S["ht_in"].sem, 16)

            def shift(n):
                was_read(sp, prep, n, "x2")
                before(sp, "xb_ready", n)
                sp.dma_start(xs[1:TC], x[0:TC - 1]).then_inc(S["shifted"].sem, 16)
                sp.dma_start(xs[0:1, 1:3, :], x[TC - 1:TC, 0:2, :]).then_inc(S["shifted"].sem, 16)

            def spread(n):
                now(sp, "scanned", n)
                before(sp, "lb_in", n)
                sp.dma_start(lam_d[n], cs16[8:16, :]).then_inc(S["lam_out"].sem, 16)
                now(sp, "lam_out", n)
                before(sp, "e_done", n)
                sp.dma_start(lb[:], lam_d[n].rearrange("(a h) t -> a h t", a=1).broadcast_to([TC, HEADS, TOKS])
                             ).then_inc(S["lb_in"].sem, 16)

            def load_res(t):
                before(sp, "h3_ready", t)
                sp.dma_start(res[:], h2[t].rearrange("(j p) d -> p j d", p=TC)).then_inc(S["res_in"].sem, 16)

            def store(t):
                now(sp, "h4_ready", t)
                sp.dma_start(out[t].rearrange("(j p) d -> p j d", p=TC), ob[:]).then_inc(S["stored"].sem, 16)

            def body(n, i, t, f):
                if t is not None:
                    load_res(t)
                if n is not None:
                    load(n)
                if f is not None:
                    store(f)
                if n is not None:
                    shift(n)
                    spread(n)

            sp.wait_ge(init, INIT)
            run(sp, body)
            sp.wait_ge(S["stored"].sem, S["stored"].before(IMGS))

        @block.tensor
        def _(pe):
            pe.wait_ge(weights, LOADED)
            pe.wait_ge(init, INIT)
            pe.wait_ge(ffs, 5)

            def fill(ring, n, name, matmuls, after=()):
                bank, full, read, k = ring.at(name)
                latest = {read: k - 1}
                for piece in after:
                    _, _, other, m = ring.at(piece)
                    latest[other] = max(latest.get(other, 0), m)
                for signal, m in latest.items():
                    pe.wait_ge(signal.sem, signal.now(n, m))
                matmuls(bank).then_inc(full.sem, 1)

            def turn_x(n, c):
                now(pe, "xn_ready", n)

                def mms(bank):
                    for j in range(3):
                        mm = pe.transpose(bank[:, j * TC:(j + 1) * TC], xn[:, j, c * P:(c + 1) * P], ident[0:TC, 0:TC])
                    return mm
                fill(prep, n, f"tA{c}", mms)

            def rows_of(n, name, w, width):
                def mms(bank):
                    for j in range(3):
                        for c in range(DC):
                            mm = pe.matmul(bank[0:TC, width * j:width * (j + 1)], xnt[:, c, j * TC:(j + 1) * TC],
                                           w[:, c, :], start=c == 0, stop=c == DC - 1)
                    return mm
                fill(prep, n, name, mms, after=("tA0", "tA1"))

            def tile_of(n, name, w, j):
                def mms(bank):
                    for c in range(DC):
                        mm = pe.matmul(bank[0:TC, :], xnt[:, c, j * TC:(j + 1) * TC], w[:, c, :],
                                       start=c == 0, stop=c == DC - 1)
                    return mm
                fill(prep, n, name, mms)

            def chans_of(n, name, w, m):
                def mms(bank):
                    for c in range(DC):
                        mm = pe.matmul(bank[0:m, 0:TOKS], w[:, c], xnt[:, c, :], start=c == 0, stop=c == DC - 1)
                    return mm
                fill(prep, n, name, mms)

            def turn_dd(n):
                now(pe, "g_step", n, NG - 4)

                def mms(bank):
                    for j in range(3):
                        mm = pe.transpose(bank[0:16, j * TC:(j + 1) * TC], dd[:, j, :], ident[0:TC, 0:TC])
                    return mm
                fill(prep, n, "dd", mms)

            def spread_dt(n, q):
                fill(prep, n, f"d{q}", lambda bank: pe.matmul(bank[:, 0:TOKS], sel[:, q, :], ddt[:],
                                                              start=True, stop=True), after=("dd",))

            def turn_lam(n):
                now(pe, "scanned", n)

                def mms(bank):
                    for j in range(3):
                        mm = pe.matmul(bank[0:TC, 16 * j:16 * (j + 1)], cs16[:, j * TC:(j + 1) * TC], ident[0:16, 0:16],
                                       start=True, stop=True)
                    return mm
                fill(prep, n, "lt", mms)

            def shared(n, name, tiles):
                def mms(bank):
                    for j in tiles:
                        o = OFFS[j] - OFFS[tiles[0]]
                        mm = pe.matmul(bank[0:TC, o:o + WIDTHS[j]], bsh[:, j * TC:(j + 1) * TC], csh[:, j * TC:],
                                       start=True, stop=True)
                    return mm
                fill(prep, n, name, mms, after=("Csh", "Bsh"))

            def scores(i, h):
                if h == 0:
                    was_read(pe, prep, i, "C")
                    was_read(pe, prep, i, "B")
                wait(pe, "a_done", 8 * i + 8 + h)
                r = slice(64 * (h % 2), 64 * (h % 2) + 64)
                for j in range(3):
                    o = 0 if j < 2 else WIDTHS[1]
                    mm = pe.matmul(rot[0:TC, min(j, 1), o:o + WIDTHS[j]], kr[r, h // 2, j * TC:(j + 1) * TC],
                                   qr[r, h // 2, j * TC:], start=True, stop=True)
                mm.then_inc(S["rot_done"].sem, 1)

            def apply(i, h):
                now(pe, "m_ready", i, h + 1)
                if h == 0:
                    now(pe, "u_ready", i)
                    before(pe, "y_read", i)
                for jt in range(3):
                    for js in range(jt + 1):
                        o = OFFS[js] + (jt - js) * TC
                        mm = pe.matmul(y[jt][0:TC, h * HD:(h + 1) * HD], mm_[:, h % 2, o:o + TC],
                                       u[:, js, h * HD:(h + 1) * HD], start=js == 0, stop=js == jt)
                mm.then_inc(S["y_done"].sem, 1)

            def turn_og(t, f):
                now(pe, "og_ready", t)

                def mms(bank):
                    for j in range(3):
                        mm = pe.transpose(bank[:, j * TC:(j + 1) * TC], og[:, j, f * P:(f + 1) * P], ident[0:TC, 0:TC])
                    return mm
                fill(tail, t, f"og{f}", mms)

            def project(t, j):
                def mms(bank):
                    for f in range(4):
                        mm = pe.matmul(bank[0:TC, 0:D], ogt[:, f, j * TC:(j + 1) * TC], wo[:, f, :],
                                       start=f == 0, stop=f == 3)
                    return mm
                fill(tail, t, f"wo{j}", mms, after=("og3",))

            def turn_xe(t, c):
                now(pe, "xe_ready", t)

                def mms(bank):
                    for j in range(3):
                        mm = pe.transpose(bank[:, j * TC:(j + 1) * TC], xe[:, j, c * P:(c + 1) * P], ident[0:TC, 0:TC])
                    return mm
                fill(tail, t, f"xe{c}", mms)

            def real_imag(t, j):
                def mms(bank):
                    for c in range(DC):
                        mm = pe.matmul(bank[0:TC, :], xet[:, c, j * TC:(j + 1) * TC], ff[:, 0, c, :],
                                       start=c == 0, stop=c == DC - 1)
                    return mm
                fill(tail, t, f"re{j}", mms, after=("xe1",))

            def body(n, i, t, f):
                for slot in range(9):
                    if n is not None and slot == 5:
                        turn_dd(n)
                    if i is not None and slot < 8:
                        scores(i, slot)
                    if i is not None and slot > 0:
                        apply(i, slot - 1)
                    if i is not None and slot == 0:
                        tile_of(i, "z1", wz, 1)
                    if t is not None and slot in (0, 1):
                        turn_og(t, 2 * slot)
                    if i is not None and slot == 0:
                        tile_of(i, "z2", wz, 2)
                    if n is not None:
                        if slot == 1:
                            turn_x(n, 0)
                            turn_x(n, 1)
                        if slot == 2:
                            rows_of(n, "gates", wg, 24)
                            chans_of(n, "ang", wrep[:, :, 0], P)
                        if slot == 3:
                            tile_of(n, "x0", wx, 0)
                            tile_of(n, "x1", wx, 1)
                        if slot == 4:
                            tile_of(n, "x2", wx, 2)
                    if t is not None:
                        if slot in (0, 1):
                            turn_og(t, 2 * slot + 1)
                        if slot in (2, 3, 4):
                            project(t, slot - 2)
                    if n is not None:
                        if slot == 5:
                            chans_of(n, "Csh", wsh[:, :, 0], NSH)
                            chans_of(n, "Bsh", wsh[:, :, 1], NSH)
                            spread_dt(n, 0)
                            spread_dt(n, 1)
                        if slot == 6:
                            spread_dt(n, 2)
                            spread_dt(n, 3)
                    if t is not None and slot in (6, 7):
                        turn_xe(t, slot - 6)
                    if n is not None and slot == 6:
                        turn_lam(n)
                    if n is not None and slot == 7:
                        shared(n, "Ga", (0,))
                    if t is not None and slot == 7:
                        real_imag(t, 0)
                    if n is not None and slot == 7:
                        shared(n, "Gb", (1, 2))
                        chans_of(n, "C", wrep[:, :, 1], P)
                    if t is not None and slot == 7:
                        real_imag(t, 1)
                    if n is not None and slot == 8:
                        chans_of(n, "B", wrep[:, :, 2], P)
                    if t is not None and slot == 8:
                        real_imag(t, 2)
                    if n is not None and slot == 8:
                        tile_of(n, "z0", wz, 0)

            run(pe, body)

        @block.scalar
        def _(act):
            act.wait_ge(ffs, 4)
            act.activation(ff[:, 0], ff[:, 2], ACT.Sin, scale=TURN).then_inc(ffs, 1)
            act.wait_ge(init, INIT)

            def copy_turned(n, c):
                bank, read = filled(act, prep, n, f"tA{c}")
                act.activation(xnt[:, c, :], bank[:, 0:TOKS], ACT.Copy).then_inc(read, 1)

            def tanh_gate(n):
                now(act, "g_step", n, 1)
                before(act, "g_step", n)
                act.activation(trt[:], gl[:, :, 16:24], ACT.Tanh, scale=0.5).then_inc(S["gate_tanh"].sem, 1)

            def exp_abs(n):
                now(act, "g_step", n, 3)
                act.activation(gx[:, 2], gx[:, 1], ACT.Exp).then_inc(S["u_exp"].sem, 1)

            def exp_da(n):
                now(act, "g_step", n, NG - 4)
                before(act, "g_step", n)
                act.activation(al[:], dd[:, :, 8:16], ACT.Exp).then_inc(S["al_exp"].sem, 1)

            def tanh_angle(n):
                before(act, "d_step", n)
                bank, read = filled(act, prep, n, "ang")
                act.activation(ta[:], bank[:, 0:TOKS], ACT.Tanh).then_inc(read, 1)

            def copy_x(n, j):
                if j == 0:
                    before(act, "ug_ready", n)
                    before(act, "xd_ready", n)
                    before(act, "shifted", n)
                bank, read = filled(act, prep, n, f"x{j}")
                act.activation(x[:, j, :], bank[0:TC, :], ACT.Copy).then_inc(read, 1)

            def copy_shared(n, name, dst):
                bank, read = filled(act, prep, n, name)
                act.activation(dst[:], bank[0:NSH, 0:TOKS], ACT.Copy).then_inc(read, 1)

            def copy_g(n, name, o, w):
                bank, read = filled(act, prep, n, name)
                before(act, "a_done", n)
                act.activation(gsh[:, o:o + w], bank[0:TC, 0:w], ACT.Copy).then_inc(read, 1)

            def sines(n):
                now(act, "angles", n)
                before(act, "sin_done", n)
                read_before(act, prep, n, "C")
                read_before(act, prep, n, "B")
                act.activation(cs[:], th[:, 2], ACT.Sin, scale=TURN).then_inc(S["sin_done"].sem, 1)

            def silu_z(n, j):
                before(act, "og_ready", n, j + 1)
                bank, read = filled(act, prep, n, f"z{j}")
                act.activation(zs[:, j, :], bank[0:TC, :], ACT.Silu).then_inc(read, 1)

            def decays(i, h):
                now(act, "ld_ready", i, 3 * h + 3)
                before(act, "m_ready", i, h + 1)
                for j in range(3):
                    act.activation(ee[:, h, OFFS[j]:OFFS[j] + TC], ld[:, h, j, :], ACT.Exp,
                                   bias=nlam[:, j, h:h + 1]).then_inc(S["e_done"].sem, 1)
                    if j < 2:
                        act.activation(ee[:, h, OFFS[j] + TC:OFFS[j] + WIDTHS[j]], lb[:, h, (j + 1) * TC:], ACT.Exp,
                                       bias=nlam[:, j, h:h + 1]).then_inc(S["e_done"].sem, 1)

            def copy_tail(t, name, dst):
                bank, read = filled(act, tail, t, name)
                act.activation(dst, bank[:, 0:TOKS], ACT.Copy).then_inc(read, 1)

            def squares(t, j):
                if j == 0:
                    before(act, "ss_ready", t)
                bank, read = filled(act, tail, t, f"re{j}")
                act.activation(sq[:, j, :], bank[0:TC, :], ACT.Square).then_inc(read, 1)

            def roots(t):
                now(act, "ss_ready", t)
                act.activation(ss[:], ss[:], ACT.Sqrt).then_inc(S["root"].sem, 1)

            def body(n, i, t, f):
                for slot in range(9):
                    if i is not None and slot == 0:
                        silu_z(i, 1)
                    if t is not None and slot in (0, 1):
                        copy_tail(t, f"og{2 * slot}", ogt[:, 2 * slot, :])
                    if i is not None and slot == 0:
                        silu_z(i, 2)
                    if n is not None:
                        if slot == 1:
                            copy_turned(n, 0)
                            copy_turned(n, 1)
                        if slot == 2:
                            tanh_gate(n)
                            tanh_angle(n)
                            exp_abs(n)
                        if slot == 3:
                            copy_x(n, 0)
                            copy_x(n, 1)
                            exp_da(n)
                        if slot == 4:
                            copy_x(n, 2)
                        if slot == 5:
                            copy_shared(n, "Csh", csh)
                            copy_shared(n, "Bsh", bsh)
                    if t is not None:
                        if slot in (0, 1):
                            copy_tail(t, f"og{2 * slot + 1}", ogt[:, 2 * slot + 1, :])
                        if slot in (6, 7):
                            copy_tail(t, f"xe{slot - 6}", xet[:, slot - 6, :])
                    if i is not None:
                        for h in AHEAD[slot]:
                            decays(i, h)
                    if n is not None and slot == 7:
                        copy_g(n, "Ga", 0, WIDTHS[0])
                    if t is not None and slot == 7:
                        squares(t, 0)
                    if n is not None and slot == 7:
                        copy_g(n, "Gb", WIDTHS[0], SPAN - WIDTHS[0])
                        decays(n, 0)
                        decays(n, 1)
                        sines(n)
                    if t is not None:
                        if slot == 7:
                            squares(t, 1)
                        if slot == 8:
                            squares(t, 2)
                            roots(t)
                    if n is not None and slot == 8:
                        silu_z(n, 0)

            run(act, body)

        @block.gpsimd
        def _(pool):
            for sig in Signal.every:
                pool.sem_inc(sig.sem, sig.per)
            pool.memset(neg[:], -0.5).then_inc(init, 1)
            pool.memset(eps[:], EPS).then_inc(init, 1)
            pool.memset(ones[:], 1.0).then_inc(init, 1)
            pool.memset(xs[:], 0.0).then_inc(init, 1)
            pool.sem_inc(init, 1)
            pool.wait_ge(init, INIT)

            def rsqrt(n, aggr, used, mv_, ln_, step, rstd):
                now(pool, aggr, n)
                before(pool, used, n)
                pool.tensor_tensor(ln_[:, 0, :], mv_[:, :, 1], eps[0:TC], ALU.add).then_inc(S[step].sem, 1)
                now(pool, step, n)
                pool.tensor_tensor(ln_[:, 1, :], ln_[:, 0, :], neg[0:TC], ALU.pow).then_inc(S[rstd].sem, 1)

            def beta_x(n):
                now(pool, "shifted", n)
                now(pool, "g_step", n)
                before(pool, "u_ready", n)
                pool.tensor_tensor(xb[:].rearrange("p j (h d) -> p (j h) d", d=HD),
                                   xs[:].rearrange("p j (h d) -> p (j h) d", d=HD),
                                   gb[:, 3].rearrange("p j h -> p (j h)").unsqueeze(2).broadcast_to([TC, 24, HD]),
                                   ALU.mult).then_inc(S["xb_ready"].sem, 1)

            def gamma_x(n):
                was_read(pool, prep, n, "x1")
                was_read(pool, prep, n, "x2")
                pool.tensor_tensor(xg[:].rearrange("p j (h d) -> p (j h) d", d=HD),
                                   x[:].rearrange("p j (h d) -> p (j h) d", d=HD),
                                   gb[:, 1].rearrange("p j h -> p (j h)").unsqueeze(2).broadcast_to([TC, 24, HD]),
                                   ALU.mult).then_inc(S["ug_ready"].sem, 1)

            def d_x(n):
                before(pool, "y_read", n)
                was_read(pool, prep, n, "x1")
                was_read(pool, prep, n, "x2")
                pool.tensor_tensor(xd[:], x[:], drep[0:TC].broadcast_to([TC, 3, INNER]), ALU.mult
                                   ).then_inc(S["xd_ready"].sem, 1)

            def body(n, i, t, f):
                if n is not None:
                    rsqrt(n, "aggr", "xn_ready", mv, ln, "rs_step", "rstd")
                if t is not None:
                    rsqrt(t, "aggr2", "xe_ready", mv2, ln2, "rs_step2", "rstd2")
                if n is not None:
                    beta_x(n)
                    gamma_x(n)
                    d_x(n)

            run(pool, body)

        @block.vector
        def _(dve):
            dve.wait_ge(weights, LOADED)
            one = Chain(dve, ffs, 0)
            one(dve.tensor_tensor(ff[:, 2], ff[:, 0], ff[:, 1], ALU.add))
            dve.tensor_scalar(ff[:, 0, :, 0:D], ff[:, 2, :, 0:D], 1.0 / (2.0 * np.pi), 0.25, ALU.mult, ALU.add)
            one(dve.tensor_scalar(ff[:, 0, :, D:], ff[:, 2, :, D:], 1.0 / (2.0 * np.pi), None, ALU.mult))
            one(dve.tensor_scalar(ff[:, 1], ff[:, 0], ROUND, ROUND, ALU.add, ALU.subtract))
            one(dve.tensor_tensor(ff[:, 2], ff[:, 0], ff[:, 1], ALU.subtract))
            dve.sem_inc(init, 2)
            dve.wait_ge(init, INIT)

            def stats_of(n, src, st_, mv_, stats, aggr, rstd):
                before(dve, rstd, n)
                for j in range(3):
                    dve.bn_stats(st_[:, j, :], src[:, j, :]).then_inc(S[stats].sem, 1)
                now(dve, stats, n)
                dve.memset(hold[:], 0.0)
                for j in range(3):
                    dve.bn_aggr(mv_[:, j, :], st_[:, j, :]).then_inc(S[aggr].sem, 1)

            def norm(n, src, dst, mv_, ln_, rstd, ready):
                now(dve, rstd, n)
                for j in range(3):
                    dve.tensor_scalar(dst[:, j, :], src[:, j, :], mv_[:, j, 0:1], ln_[:, 1, j:j + 1],
                                      ALU.subtract, ALU.mult).then_inc(S[ready].sem, 1)

            def gates(n):
                before(dve, "al_exp", n)
                before(dve, "gate_tanh", n)
                bank, _ = filled(dve, prep, n, "gates")
                step = Chain(dve, S["g_step"].sem, NG * n + NG)
                gv = bank[0:TC, 0:72].rearrange("p (j g) -> p j g", g=24)
                _, _, read, _ = prep.at("gates")
                step(dve.tensor_copy(gl[:], gv))
                dve.sem_inc(read.sem, 1)
                a, na, w, b, r, s_, s2, p = (gx[:, k] for k in range(8))
                step(dve.tensor_tensor(a, gl[:, :, 0:16], gbias[0:TC].broadcast_to([TC, 3, 16]), ALU.add))
                step(dve.scalar_tensor_tensor(na, a, -1.0, a, ALU.mult, ALU.min))

            def softplus(n):
                a, _, w, b, r, s_, s2, p = (gx[:, k] for k in range(8))
                step = Chain(dve, S["g_step"].sem, NG * n + NG + 3)
                now(dve, "u_exp", n)
                step(dve.tensor_scalar(b, w, 2.0, None, ALU.add))
                step(dve.reciprocal(r, b))
                step(dve.tensor_tensor(s_, w, r, ALU.mult))
                step(dve.tensor_tensor(s2, s_, s_, ALU.mult))
                step(dve.tensor_scalar(p, s2, 1.0 / (2 * KL + 1), None, ALU.mult))
                for k in range(KL - 1, 0, -1):
                    step(dve.scalar_tensor_tensor(p, p, 1.0 / (2 * k + 1), s2, ALU.add, ALU.mult))
                step(dve.scalar_tensor_tensor(p, p, 1.0, s_, ALU.add, ALU.mult))
                step(dve.tensor_scalar(b, a, 0.0, None, ALU.max))
                step(dve.scalar_tensor_tensor(p, p, 2.0, b, ALU.mult, ALU.add))
                dve.tensor_copy(dd[:, :, 0:8], p[:, :, 0:8])
                step(dve.tensor_scalar(r[:, :, 0:8], p[:, :, 8:16], -1.0, -1e-4, ALU.mult, ALU.min))
                step(dve.tensor_tensor(dd[:, :, 8:16], r[:, :, 0:8], p[:, :, 0:8], ALU.mult))

            def mixes(n):
                tr, ga, be, bb = (gb[:, k] for k in range(4))
                step = Chain(dve, S["g_step"].sem, NG * n + NG + NG - 4)
                before(dve, "ug_ready", n)
                now(dve, "gate_tanh", n)
                step(dve.tensor_scalar(tr, trt[:], 0.5, 0.5, ALU.mult, ALU.add))
                step(dve.tensor_tensor(ga, tr, dd[:, :, 0:8], ALU.mult))
                step(dve.tensor_tensor(be, dd[:, :, 0:8], ga, ALU.subtract))
                now(dve, "al_exp", n)
                step(dve.tensor_tensor(bb, be, al[:], ALU.mult))

            def cumulate(n):
                bank, read = filled(dve, prep, n, "dd")
                dve.tensor_copy(ddt[:], bank[0:16, 0:TOKS]).then_inc(read, 1)
                was_read(dve, prep, n, "dd")
                before(dve, "lam_out", n)
                dve.tensor_tensor_scan(cs16[:], ones[0:16, :], ddt[:], 0.0, ALU.mult, ALU.add
                                       ).then_inc(S["scanned"].sem, 1)

            def angle(n, q):
                if q == 0:
                    before(dve, "angles", n)
                    before(dve, "sin_done", n)
                    was_read(dve, prep, n, "ang")
                wait(dve, "turns", 4 * n + 4 + q)
                bank, _ = filled(dve, prep, n, f"d{q}")
                dve.tensor_tensor(thi[:], ta[:], bank[:, 0:TOKS], ALU.mult).then_inc(S["d_step"].sem, 1)
                now(dve, "d_step", n, q + 1)
                dve.sem_inc(prep.at(f"d{q}")[2].sem, 1)
                dve.tensor_tensor_scan(th[:, 0, q, :], ones[:], thi[:], phase[:, 0:1], ALU.mult, ALU.add
                                       ).then_inc(S["turns"].sem, 1)

            def reduce_angles(n):
                now(dve, "turns", n)
                dve.tensor_scalar(th[:, 1], th[:, 0], ROUND, ROUND, ALU.add, ALU.subtract).then_inc(S["r_step"].sem, 1)
                now(dve, "r_step", n)
                dve.tensor_tensor(th[:, 2], th[:, 0], th[:, 1], ALU.subtract).then_inc(S["angles"].sem, 1)

            def copy_lam(n):
                bank, _ = filled(dve, prep, n, "lt")
                before(dve, "e_done", n)
                lv = bank[0:TC, 0:48].rearrange("p (j g) -> p j g", g=16)[:, :, 8:16]
                dve.tensor_copy(lam[:], lv).then_inc(S["lam_step"].sem, 1)
                now(dve, "lam_step", n)
                dve.sem_inc(prep.at("lt")[2].sem, 1)
                dve.tensor_scalar(nlam[:], lam[:], -1.0, None, ALU.mult).then_inc(S["lam_ready"].sem, 1)

            def turn_qk(n, name, dst):
                now(dve, "sin_done", n)
                bank, read = filled(dve, prep, n, name)
                before(dve, "rot_done", n)
                dve.tensor_tensor(dst[:], cs[:], bank[:, 0:TOKS].unsqueeze(1).broadcast_to([P, 4, TOKS]),
                                  ALU.mult).then_inc(read, 1)

            def make_u(n):
                before(dve, "y_done", n)
                now(dve, "ug_ready", n)
                dve.tensor_tensor(u[:], xg[:], xb[:], ALU.add).then_inc(S["u_ready"].sem, 1)

            def diagonal(i, h):
                if h == 0:
                    now(dve, "lb_in", i)
                    now(dve, "lam_ready", i)
                before(dve, "e_done", i, 5 * h + 5)
                for j in range(3):
                    dve.scalar_tensor_tensor(ld[:, h, j, :], lb[:, h, j * TC:(j + 1) * TC], lam[:, j, h:h + 1],
                                             negmask[:], ALU.min, ALU.add).then_inc(S["ld_ready"].sem, 1)

            def decay(i, h):
                now(dve, "rot_done", i, h + 1)
                wait(dve, "y_done", 8 * i + h + 7)
                if h == 0:
                    was_read(dve, prep, i, "Ga")
                    was_read(dve, prep, i, "Gb")
                m = mm_[:, h % 2, :]
                dve.tensor_tensor(m.rearrange("p (a b) -> p a b", a=2), rot[0:TC, :, 0:WIDTHS[0]],
                                  gsh[:].rearrange("p (a b) -> p a b", a=2), ALU.add).then_inc(S["a_done"].sem, 1)
                now(dve, "a_done", i, h + 1)
                now(dve, "e_done", i, 5 * h + 5)
                dve.tensor_tensor(m, m, ee[:, h, :], ALU.mult).then_inc(S["m_ready"].sem, 1)

            def add_dx(i):
                now(dve, "y_done", i)
                now(dve, "xd_ready", i)
                used_before(dve, tail, i, "og3")
                for j in range(3):
                    dve.tensor_tensor(og[:, j, :], y[j][0:TC, :], xd[:, j, :], ALU.add).then_inc(S["y_read"].sem, 1)

            def gate_y(i):
                was_read(dve, prep, i, "z1")
                was_read(dve, prep, i, "z2")
                for j in range(3):
                    now(dve, "y_read", i, j + 1)
                    dve.tensor_tensor(og[:, j, :], og[:, j, :], zs[:, j, :], ALU.mult).then_inc(S["og_ready"].sem, 1)

            def residual(t, j):
                if j == 0:
                    now(dve, "res_in", t)
                    before(dve, "h4_ready", t)
                bank, _ = filled(dve, tail, t, f"wo{j}")
                dve.tensor_tensor(h3[:, j, :], bank[0:TC, 0:D], res[:, j, :], ALU.add).then_inc(S["h3_ready"].sem, 1)
                now(dve, "h3_ready", t, j + 1)
                dve.sem_inc(tail.read[0].sem, 1)

            def sum_squares(t):
                was_read(dve, tail, t, "re2")
                before(dve, "h4_ready", t)
                dve.tensor_tensor(ss[:], sq[:, :, 0:D], sq[:, :, D:], ALU.add).then_inc(S["ss_ready"].sem, 1)

            def finish(t):
                now(dve, "root", t)
                before(dve, "stored", t)
                dve.tensor_tensor(ob[:], h3[:], ss[:], ALU.add).then_inc(S["h4_ready"].sem, 1)

            def body(n, i, t, f):
                for slot in range(9):
                    if i is not None:
                        for h in AHEAD[slot]:
                            diagonal(i, h)
                    if n is not None:
                        if slot == 5:
                            cumulate(n)
                        if slot == 6:
                            angle(n, 0)
                            angle(n, 1)
                        if slot == 7:
                            diagonal(n, 0)
                            diagonal(n, 1)
                    if n is not None and slot == 0:
                        now(dve, "ht_in", n)
                        stats_of(n, ht, st, mv, "stats", "aggr", "rstd")
                    if i is not None and slot < 8:
                        decay(i, slot)
                    if n is not None:
                        if slot == 0:
                            used_before(dve, prep, n, "tA1")
                            norm(n, ht, xn, mv, ln, "rstd", "xn_ready")
                        if slot == 2:
                            gates(n)
                        if slot == 3:
                            softplus(n)
                        if slot == 4:
                            mixes(n)
                        if slot == 6:
                            angle(n, 2)
                            angle(n, 3)
                            reduce_angles(n)
                            copy_lam(n)
                    if t is not None:
                        if slot in (2, 3, 4):
                            residual(t, slot - 2)
                        if slot == 4:
                            stats_of(t, h3, st2, mv2, "stats2", "aggr2", "rstd2")
                        if slot == 5:
                            used_before(dve, tail, t, "xe1")
                            norm(t, h3, xe, mv2, ln2, "rstd2", "xe_ready")
                    if f is not None and slot == 0:
                        finish(f)
                    if n is not None and slot == 8:
                        turn_qk(n, "C", qr)
                    if i is not None and slot == 8:
                        add_dx(i)
                    if n is not None and slot == 8:
                        turn_qk(n, "B", kr)
                    if t is not None and slot == 8:
                        sum_squares(t)
                    if i is not None and slot == 8:
                        gate_y(i)
                    if n is not None and slot == 8:
                        make_u(n)

            run(dve, body)


def program(nc, T, out):
    h0 = nc.dram_tensor("h0", [IMGS, TOKS, D], F32).ap()
    kpad = nc.dram_tensor("kpad", [D, IMGS * 2 * IMGS], F32).ap()
    xn_t = nc.dram_tensor("xn_t", [D, IMGS, TOKS], F32).ap()
    mx = nc.dram_tensor("mx", [TOKS, IMGS, D], F32).ap()
    taps_stage(nc, T, kpad)
    embed_stage(nc, T, h0, xn_t)
    ema_stage(nc, T, kpad, xn_t, mx)
    h2 = nc.dram_tensor("h2", [IMGS, TOKS, D], F32).ap()
    mix_stage(nc, T, h0, mx, h2)
    lam_d = nc.dram_tensor("lam_d", [IMGS, HEADS, TOKS], F32).ap()
    scan_stage(nc, T, h2, lam_d, out)


def laid_out(inputs):
    a = {k: np.asarray(v) for k, v in inputs.items()}
    x = a["x"].reshape(IMGS, 3, 14, 16, 14, 16).transpose(0, 1, 3, 5, 2, 4).reshape(IMGS, KC, P, PATCHES)
    def cols(v):
        return v.reshape(-1, P).T

    T = {"patches": x.transpose(0, 2, 1, 3).reshape(IMGS, P, KC * PATCHES), "txt": a["txt"],
         "tok_W1": a["L0_tok_W1"], "tok_b1": cols(a["L0_tok_b1"]), "tok_W2": a["L0_tok_W2"], "tok_b2": a["L0_tok_b2"],
         "delta": a["L0_attn_ema_delta"][:, :, 0], "alpha": a["L0_attn_ema_alpha"][:, :, 0],
         "beta": a["L0_attn_ema_beta"][:, :, 0], "gamma": a["L0_attn_ema_gamma"], "omega": cols(a["L0_attn_ema_omega"]),
         "ln_w": cols(a["L0_attn_ln_w"]), "ln_b": cols(a["L0_attn_ln_b"]), "ident": np.eye(P, dtype=np.float32)}
    wmx, bmx = a["L0_attn_Wmx"].T, a["L0_attn_bmx"]
    half = np.arange(P // 2, dtype=np.float32)
    ang = np.arange(IMGS, dtype=np.float32)[None, :] * np.exp(half * np.float32(-np.log(10000.0) / (P // 2)))[:, None]
    cos, sin = np.cos(ang), np.sin(ang)
    ra, rb = a["L0_attn_rot_alpha"][0], a["L0_attn_rot_beta"][0]
    e = np.arange(EXPERTS)
    T.update({
        "wv": a["L0_attn_Wv"].T, "wzr": wmx[:, D:D + 640], "wuh": np.concatenate([wmx[:, :D], wmx[:, D + 640:]], 1),
        "wh": a["L0_attn_Wh"].T, "bv": a["L0_attn_bv"][None], "bh": a["L0_attn_bh"][None],
        "buh": np.concatenate([bmx[:D], bmx[D + 640:]])[None], "bzr": cols(bmx[D:D + 640]),
        "qk": np.concatenate([a["L0_attn_qk_gamma"], a["L0_attn_qk_beta"]]).T,
        "rot": np.stack([ra, np.roll(ra, 64), rb, np.roll(rb, 64)], 1),
        "trig": np.stack([np.concatenate([cos, cos]), np.concatenate([-sin, sin])], 1).astype(np.float32),
        "w1": a["L0_ffn_w1"], "w2": a["L0_ffn_w2"], "wgu": a["L0_ffn_shared_gate_up"], "wsd": a["L0_ffn_shared_down"],
        "wr": np.concatenate([a["L0_ffn_router_w"], a["L0_ffn_shared_gate_w"]], 1),
        "lower": (e[None, :] < e[:, None]).astype(np.float32).reshape(1, -1)})
    win = a["L1_attn_w_in"].T
    z0, x0, b0, c0, g0, a0 = 0, INNER, 2 * INNER, 2 * INNER + P, 2 * INNER + 2 * P, 2 * INNER + 2 * P + 24
    head = np.arange(P) // 64
    sel = np.zeros((16, 4, P), np.float32)
    for q in range(4):
        sel[2 * q + head, q, np.arange(P)] = 0.5
    cosine = (np.arange(P) // R) % 2 == 0
    pos = np.arange(TC)
    T.update({
        "wg": win[:, g0:a0], "wx": win[:, x0:b0], "wz": win[:, z0:x0],
        "wrep": np.stack([np.tile(win[:, o:o + R], 4) for o in (a0, c0, b0)], 1),
        "wsh": np.stack([win[:, c0 + R:g0], win[:, b0 + R:c0]], 1),
        "wo": a["L1_attn_w_out"].T, "ff": np.concatenate([a["L1_ffn_theta"], a["L1_ffn_phi"]], 1),
        "ffn": np.concatenate([a["L1_ffn_theta_noise"], a["L1_ffn_phi_noise"]], 1),
        "gbias": np.concatenate([a["L1_attn_dt_bias"], np.zeros(8, np.float32)])[None],
        "drep": np.repeat(a["L1_attn_D"], HD)[None], "sel": sel,
        "phase": np.stack([np.where(cosine, 0.25, 0.0), np.zeros(P)], 1).astype(np.float32),
        "negmask": np.where(pos[None, :] < pos[:, None], -1e30, 0.0).astype(np.float32)})
    return {k: np.ascontiguousarray(v) for k, v in T.items()}


def kernel(**inputs):
    import concourse.bacc as _bacc
    from concourse.bass_utils import run_bass_kernel_spmd as _run

    nc = _bacc.Bacc("TRN2", target_bir_lowering=False, num_devices=1)
    arrays = laid_out(inputs)
    T = {k: nc.dram_tensor(f"in_{k}", v.shape, mybir.dt.from_np(v.dtype), kind="ExternalInput").ap()
         for k, v in arrays.items()}
    out = nc.dram_tensor("out_0", (IMGS, TOKS, D), F32, kind="ExternalOutput").ap()
    program(nc, T, out)
    r = _run(nc, [{f"in_{k}": v for k, v in arrays.items()}], core_ids=[0])
    return r.results[0]["out_0"]
```

```python
from contextlib import ExitStack

import numpy as np

import concourse.bass as bass
from concourse import mybir

F32 = mybir.dt.float32
F32R = mybir.dt.float32r
ALU = mybir.AluOpType
ACT = mybir.ActivationFunctionType
AX = mybir.AxisListType

P = 128
IMGS, TOKS, D = 32, 324, 256
PATCHES, TEXT = 196, 128
KC = 768 // P
DC = D // P
HALF = PATCHES // 2
NSTATE = 16
GROUPS = D // 4
TC = TOKS // 3
EPS = 1e-5


class Stage:

    def __init__(self, nc, tag):
        self.nc, self.tag, self.ctx = nc, tag, ExitStack()

    def __enter__(self):
        self.ctx.__enter__()
        return self

    def __exit__(self, *e):
        return self.ctx.__exit__(*e)

    def sb(self, name, shape, dt=F32):
        return self.ctx.enter_context(self.nc.sbuf_tensor(f"{self.tag}_{name}", shape, dt))

    def ps(self, name, shape):
        return self.ctx.enter_context(self.nc.psum_tensor(f"{self.tag}_{name}", shape, F32))

    def sem(self, name):
        return self.ctx.enter_context(self.nc.semaphore(f"{self.tag}_{name}"))

    def block(self):
        return self.ctx.enter_context(self.nc.Block())


def taps_stage(nc, T, kpad):
    with Stage(nc, "taps") as s:
        par = s.sb("par", [P, 4, DC, NSTATE])
        om = s.sb("om", [P, DC, 1])
        sg = s.sb("sg", [P, 2, DC, NSTATE])
        q = s.sb("q", [P, 5, DC, NSTATE])
        w = s.sb("w", [P, DC, IMGS, NSTATE])
        tmp = s.sb("tmp", [P, 2, DC, NSTATE])
        kp = s.sb("kp", [P, DC, 2 * IMGS])
        loaded, tanhs, step, stored = s.sem("loaded"), s.sem("tanhs"), s.sem("step"), s.sem("stored")
        block = s.block()

        @block.sync
        def _(sp):
            for n, name in enumerate(("delta", "alpha", "beta", "gamma")):
                sp.dma_start(par[:, n], T[name].rearrange("(c p) n -> p c n", p=P)).then_inc(loaded, 16)
            sp.dma_start(om[:, :, 0], T["omega"]).then_inc(loaded, 16)
            sp.wait_ge(step, 17)
            for c in range(DC):
                sp.dma_start(kpad[c * P:(c + 1) * P].rearrange("p (r k) -> p r k", r=IMGS),
                             kp[:, c:c + 1, :].broadcast_to([P, IMGS, 2 * IMGS])).then_inc(stored, 16)
            sp.wait_ge(stored, 32)

        @block.scalar
        def _(act):
            act.wait_ge(loaded, 80)
            act.activation(sg[:], par[:, 0:2], ACT.Tanh, scale=0.5).then_inc(tanhs, 1)

        @block.vector
        def _(dve):
            n = 0

            def chain(ins):
                nonlocal n
                n += 1
                ins.then_inc(step, 1)
                dve.wait_ge(step, n)

            chain(dve.memset(kp[:], 0.0))
            dve.wait_ge(tanhs, 1)
            dve.wait_ge(loaded, 80)
            chain(dve.tensor_scalar(sg[:], sg[:], 0.5, 0.5, ALU.mult, ALU.add))
            chain(dve.tensor_tensor(tmp[:, 0], sg[:, 0], sg[:, 1], ALU.mult))
            chain(dve.tensor_tensor(tmp[:, 1], sg[:, 0], par[:, 2], ALU.mult))
            chain(dve.tensor_scalar(q[:, 0], tmp[:, 0], -1.0, 1.0, ALU.mult, ALU.add))
            chain(dve.scalar_tensor_tensor(w[:, :, 0, :], tmp[:, 1], 0.25, par[:, 3], ALU.mult, ALU.mult))
            for k in range(5):
                if k < 4:
                    chain(dve.tensor_tensor(q[:, k + 1], q[:, k], q[:, k], ALU.mult))
                m = 1 << k
                for c in range(DC):
                    ins = dve.tensor_tensor(w[:, c, m:2 * m, :], w[:, c, 0:m, :],
                                            q[:, k, c:c + 1, :].broadcast_to([P, m, NSTATE]), ALU.mult)
                chain(ins)
            chain(dve.tensor_reduce(kp[:, :, IMGS:], w[:], AX.X, ALU.add))
            chain(dve.tensor_tensor(kp[:, :, IMGS:IMGS + 1], kp[:, :, IMGS:IMGS + 1], om[:], ALU.add))


def embed_stage(nc, T, h0, xn_t):
    with Stage(nc, "emb") as s:
        w1 = s.sb("w1", [P, KC, D])
        w2 = s.sb("w2", [P, DC, D])
        b1 = s.sb("b1", [P, DC])
        b2 = s.sb("b2", [P, 1, D])
        lnw, lnb = s.sb("lnw", [P, DC]), s.sb("lnb", [P, DC])
        ident = s.sb("ident", [P, P])
        xt = s.sb("xt", [P, 2, KC * PATCHES])
        g = s.sb("g", [P, DC, PATCHES])
        ht = s.sb("ht", [P, 2, 3, D])
        st, mv = s.sb("st", [P, 3, 6]), s.sb("mv", [P, 3, 2])
        neg = s.sb("neg", [P, 3])
        eps = s.sb("eps", [P, 3])
        hold = s.sb("hold", [P, 1])
        ln = s.sb("ln", [P, 6, 3])
        xn = s.sb("xn", [P, 3, D])
        xnt = s.sb("xnt", [P, DC, TOKS])
        hid = s.ps("hid", [P, DC, PATCHES])
        emb = s.ps("emb", [P, 2, D])
        tr = [s.ps(f"tr{c}", [P, 512]) for c in range(DC)]
        patches_in, text_in, h0_out = ([s.sem(f"{n}{b}") for b in range(2)] for n in ("patches_in", "text_in", "h0_out"))
        (weights, hid_done, hid_silu, emb_done, ht_ready, init, stats, aggr, rstd, pool_step,
         normed, tr_done, xnt_ready, xnt_out) = [s.sem(n) for n in (
            "weights", "hid_done", "hid_silu", "emb_done", "ht_ready", "init", "stats", "aggr",
            "rstd", "pool_step", "normed", "tr_done", "xnt_ready", "xnt_out")]
        block = s.block()
        rows = (HALF, HALF, TEXT)
        col = (0, HALF, PATCHES)
        LOADS = 8

        @block.sync
        def _(sp):
            for dst, src in ((w1[:], T["tok_W1"].rearrange("(k p) n -> p k n", p=P)),
                             (w2[:], T["tok_W2"].rearrange("(k p) n -> p k n", p=P)),
                             (b1[:], T["tok_b1"]),
                             (b2[:, 0, :], T["tok_b2"].rearrange("(a d) -> a d", a=1).broadcast_to([P, D])),
                             (lnw[:], T["ln_w"]),
                             (lnb[:], T["ln_b"]),
                             (ident[:], T["ident"])):
                sp.dma_start(dst, src).then_inc(weights, 16)
            sp.wait_ge(init, 4)
            with sp.Fori(0, IMGS // 2) as h:
                for b in range(2):
                    i = 2 * h + b
                    sp.wait_ge(hid_done, i + 1)
                    sp.dma_start(xt[:, b], T["patches"][i]).then_inc(patches_in[b], 16)
                    sp.wait_ge(normed, 3 * i + 3)
                    sp.wait_ge(h0_out[b], 32 * h + 32)
                    sp.dma_start(ht[:, b, 2, :], T["txt"][i]).then_inc(text_in[b], 16)
            for b in range(2):
                sp.wait_ge(h0_out[b], 32 * (IMGS // 2) + 32)
            sp.wait_ge(xnt_out, 16 * IMGS + 16)

        @block.tensor
        def _(pe):
            pe.wait_ge(weights, 16 * 7)

            def hidden(h, b):
                i = 2 * h + b
                pe.wait_ge(patches_in[b], 16 * h + 16)
                pe.wait_ge(hid_silu, 2 * i + 2)
                for f in range(DC):
                    for k in range(KC):
                        mm = pe.matmul(hid[:, f, :], w1[:, k, f * P:(f + 1) * P],
                                       xt[:, b, k * PATCHES:(k + 1) * PATCHES], start=k == 0, stop=k == KC - 1)
                mm.then_inc(hid_done, 1)

            def embedding(i):
                pe.wait_ge(hid_silu, 2 * i + 4)
                pe.wait_ge(ht_ready, i + 1)
                for j in range(2):
                    for f in range(DC):
                        mm = pe.matmul(emb[0:HALF, j, :], g[:, f, j * HALF:(j + 1) * HALF], w2[:, f, :],
                                       start=f == 0, stop=f == DC - 1)
                mm.then_inc(emb_done, 1)

            def turn(n):
                pe.wait_ge(normed, 3 * n + 3)
                pe.wait_ge(xnt_ready, 2 * n - 2)
                for c in range(DC):
                    for j in range(3):
                        mm = pe.transpose(tr[c][:, col[j]:col[j] + rows[j]], xn[0:rows[j], j, c * P:(c + 1) * P],
                                          ident[0:rows[j], 0:rows[j]])
                mm.then_inc(tr_done, 1)

            for b in range(2):
                hidden(0, b)
                embedding(b)
            with pe.Fori(1, IMGS // 2) as h:
                for b in range(2):
                    hidden(h, b)
                    turn(2 * h + b)
                    embedding(2 * h + b)
            turn(IMGS)
            turn(IMGS + 1)

        @block.scalar
        def _(act):
            act.sem_inc(hid_silu, 2)
            act.sem_inc(xnt_ready, 2)
            act.sem_inc(h0_out[0], 32)
            act.sem_inc(h0_out[1], 32)
            act.sem_inc(xnt_out, 16)
            act.wait_ge(weights, 16 * 7)

            def silu(i):
                act.wait_ge(hid_done, i + 3)
                act.wait_ge(emb_done, i + 1)
                for f in range(DC):
                    act.activation(g[:, f, :], hid[:, f, :], ACT.Silu, bias=b1[:, f:f + 1]).then_inc(hid_silu, 1)

            def store_rows(h, b):
                i = 2 * h + b
                act.wait_ge(ht_ready, i + 2)
                act.wait_ge(text_in[b], 16 * h + 16)
                act.dma_start(h0[i, 0:PATCHES, :].rearrange("(j p) d -> p j d", j=2),
                              ht[0:HALF, b, 0:2, :]).then_inc(h0_out[b], 16)
                act.dma_start(h0[i, PATCHES:TOKS, :], ht[:, b, 2, :]).then_inc(h0_out[b], 16)

            def affine(n):
                act.wait_ge(tr_done, n)
                act.wait_ge(xnt_out, 16 * n - 16)
                for c in range(DC):
                    act.activation(xnt[:, c, :], tr[c][:, 0:TOKS], ACT.Identity, bias=lnb[:, c:c + 1],
                                   scale=lnw[:, c:c + 1]).then_inc(xnt_ready, 1)
                act.wait_ge(xnt_ready, 2 * n)
                act.dma_start(xn_t[:, n - 2, :].rearrange("(c p) b -> p c b", p=P), xnt[:]).then_inc(xnt_out, 16)

            for b in range(2):
                silu(b)
                store_rows(0, b)
            with act.Fori(1, IMGS // 2) as h:
                for b in range(2):
                    silu(2 * h + b)
                    affine(2 * h + b)
                    store_rows(h, b)
            affine(IMGS)
            affine(IMGS + 1)

        @block.vector
        def _(dve):
            dve.memset(ht[:], 0.0).then_inc(init, 1)
            dve.memset(neg[:], -0.5).then_inc(init, 1)
            dve.memset(eps[:], EPS).then_inc(init, 1)
            dve.sem_inc(init, 1)
            dve.sem_inc(ht_ready, 1)
            dve.sem_inc(normed, 6)
            dve.wait_ge(weights, 16 * 7)
            dve.wait_ge(init, 4)
            def rows_in(h, b):
                i = 2 * h + b
                dve.wait_ge(emb_done, i + 2)
                dve.wait_ge(h0_out[b], 32 * h + 32)
                dve.wait_ge(normed, 3 * i + 3)
                dve.tensor_tensor(ht[0:HALF, b, 0:2, :], emb[0:HALF], b2[0:HALF].broadcast_to([HALF, 2, D]),
                                  ALU.add).then_inc(ht_ready, 1)
                dve.wait_ge(ht_ready, i + 2)
                dve.wait_ge(text_in[b], 16 * h + 16)
                for j in range(3):
                    dve.bn_stats(st[:, j, :], ht[:, b, j, :]).then_inc(stats, 1)
                dve.wait_ge(rstd, i + 1)
                dve.wait_ge(normed, 3 * i + 6)
                dve.wait_ge(stats, 3 * i + 3)
                dve.memset(hold[:], 0.0)
                for j in range(3):
                    dve.bn_aggr(mv[:, j, :], st[:, j, :]).then_inc(aggr, 1)
                dve.wait_ge(rstd, i + 2)
                dve.wait_ge(tr_done, i + 1)
                for j in range(3):
                    dve.tensor_scalar(xn[:, j, :], ht[:, b, j, :], mv[:, j, 0:1], ln[:, 5, j:j + 1],
                                      ALU.subtract, ALU.mult).then_inc(normed, 1)

            with dve.Fori(0, IMGS // 2) as h:
                for b in range(2):
                    rows_in(h, b)

        @block.gpsimd
        def _(pool):
            pool.sem_inc(rstd, 1)
            pool.sem_inc(hid_done, 2)
            pool.sem_inc(emb_done, 1)
            pool.sem_inc(tr_done, 1)
            pool.wait_ge(init, 4)
            with pool.Fori(0, IMGS) as i:
                pool.wait_ge(aggr, 3 * i + 3)
                pool.wait_ge(normed, 3 * i + 6)
                norm_chain(pool, mv, neg, eps, ln, pool_step, 6 * i).then_inc(rstd, 1)


def norm_chain(pool, mv, neg, eps, ln, step, base):
    var = mv[:, :, 1]
    pool.tensor_tensor(ln[:, 0, :], var, eps[:], ALU.add).then_inc(step, 1)
    pool.wait_ge(step, base + 1)
    pool.tensor_tensor(ln[:, 1, :], ln[:, 0, :], neg[:], ALU.pow).then_inc(step, 1)
    pool.wait_ge(step, base + 2)
    pool.tensor_tensor(ln[:, 2, :], ln[:, 1, :], ln[:, 1, :], ALU.mult).then_inc(step, 1)
    pool.wait_ge(step, base + 3)
    pool.tensor_tensor(ln[:, 3, :], ln[:, 2, :], var, ALU.mult).then_inc(step, 1)
    pool.wait_ge(step, base + 4)
    pool.tensor_tensor(ln[:, 3, :], ln[:, 3, :], eps[:], ALU.add).then_inc(step, 1)
    pool.wait_ge(step, base + 5)
    pool.tensor_tensor(ln[:, 4, :], ln[:, 3, :], neg[:], ALU.pow).then_inc(step, 1)
    pool.wait_ge(step, base + 6)
    return pool.tensor_tensor(ln[:, 5, :], ln[:, 4, :], ln[:, 1, :], ALU.mult)


def ema_stage(nc, T, kpad, xn_t, mx):
    QD = 4
    GQ = GROUPS // QD
    with Stage(nc, "ema") as s:
        x = s.sb("x", [P, GROUPS, TOKS])
        toep = s.sb("toep", [P, GROUPS, P])
        o = s.sb("o", [TC, 2, IMGS, P])
        banks = [s.ps(f"bank{k}", [P, 4, P]) for k in range(4)]
        cleared, toep_in, stored = s.sem("cleared"), s.sem("toep_in"), [s.sem(f"stored{k}") for k in range(2)]
        x_in = [s.sem(f"x_in{q}") for q in range(QD)]
        conv_done, silu_done = s.sem("conv_done"), s.sem("silu_done")
        block = s.block()
        work = [(dh, bc, k) for dh in range(2) for bc in range(3) for k in range(8)]

        @block.sync
        def _(sp):
            view = xn_t.rearrange("(g j) s b -> (j s) g b", j=4)
            for q in range(QD):
                sp.dma_start(x[:, q * GQ:(q + 1) * GQ, :], view[:, q * GQ:(q + 1) * GQ, :]).then_inc(x_in[q], 16)
            for t in range(6):
                dh, bc = divmod(t, 3)
                sp.wait_ge(silu_done, 8 * t + 8)
                sp.dma_start(mx[bc * TC:(bc + 1) * TC, :, dh * P:(dh + 1) * P],
                             o[:, t % 2]).then_inc(stored[t % 2], 16)
            for k in range(2):
                sp.wait_ge(stored[k], 48)

        @block.gpsimd
        def _(pool):
            pool.memset(toep[:], 0.0).then_inc(cleared, 1)

        @block.scalar
        def _(act):
            act.wait_ge(cleared, 1)
            for j in range(4):
                rows = kpad.rearrange("(g j) k -> j g k", j=4)[j, :, IMGS:IMGS + IMGS * 63]
                act.dma_start(toep[IMGS * j:IMGS * (j + 1), :, IMGS * j:IMGS * (j + 1)],
                              rows.rearrange("g (s k) -> s g k", k=63)[:, :, 0:IMGS]).then_inc(toep_in, 16)
            for n, (dh, bc, k) in enumerate(work):
                t = n // 8
                act.wait_ge(conv_done, n + 1)
                if k == 0 and t >= 2:
                    act.wait_ge(stored[t % 2], 16 * (t // 2))
                act.activation(o[:, t % 2].rearrange("p t (k d) -> p k d t", k=8)[:, k],
                               banks[n % 4][0:TC].rearrange("p g (j t) -> p (g j) t", j=4), ACT.Silu).then_inc(silu_done, 1)

        @block.tensor
        def _(pe):
            pe.wait_ge(toep_in, 64)
            for n, (dh, bc, k) in enumerate(work):
                if bc == 0 and k % 4 == 0:
                    pe.wait_ge(x_in[2 * dh + k // 4], 16)
                if n >= 4:
                    pe.wait_ge(silu_done, n - 3)
                for m in range(4):
                    gr = 32 * dh + 4 * k + m
                    mm = pe.matmul(banks[n % 4][0:TC, m, :], x[:, gr, bc * TC:(bc + 1) * TC], toep[:, gr, :],
                                   start=True, stop=True)
                mm.then_inc(conv_done, 1)


ERF_P = (-2.72614225801306e-10, 2.77068142495902e-08, -2.10102402082508e-06, -5.69250639462346e-05,
         -7.34990630326855e-04, -2.95459980854025e-03, -1.60960333262415e-02)
ERF_Q = (-1.45660718464996e-05, -2.13374055278905e-04, -1.68282697438203e-03, -7.37332916720468e-03,
         -1.42647390514189e-02)
EXPERTS = 8
MU, SIGMA = 0.707107, 0.282095
ERF_SCALE = 1.0 / (SIGMA * 2.0 ** 0.5)
COLS = 12
GRP = TOKS // COLS
N = COLS * IMGS


class Chain:

    def __init__(self, eng, sem, base):
        self.eng, self.sem, self.at = eng, sem, base

    def __call__(self, ins):
        ins.then_inc(self.sem, 1)
        self.at = self.at + 1
        self.eng.wait_ge(self.sem, self.at)


def mix_stage(nc, T, h0, mx, h2):
    with Stage(nc, "mix") as s:
        ident = s.sb("ident", [P, P])
        lnw, lnb = s.sb("lnw", [P, DC]), s.sb("lnb", [P, DC])
        wv, wzr, wuh = s.sb("wv", [P, DC, 512]), s.sb("wzr", [P, DC, 640]), s.sb("wuh", [P, DC, 512])
        wh = s.sb("wh", [P, 4, D])
        bv, buh = s.sb("bv", [P, 512]), s.sb("buh", [P, 512])
        bzr = s.sb("bzr", [P, 5])
        bh = s.sb("bh", [P, D])
        qk = s.sb("qk", [P, 4])
        rot = s.sb("rot", [P, 4])
        trig = s.sb("trig", [P, 2, IMGS])
        rotated = s.sb("rotated", [P, 3, IMGS])
        rotb = s.sb("rotb", [P, 4, IMGS])
        biasc = s.sb("biasc", [P, 1, IMGS])
        w1 = s.sb("w1", [P, 2, EXPERTS + 2, DC, D], F32R)
        w2 = s.sb("w2", [P, 2, EXPERTS + 1, DC, D], F32R)
        raw = s.sb("raw", [P, 2, 2, DC, D])
        wr = s.sb("wr", [P, DC, EXPERTS + 1])
        lower = s.sb("lower", [P, 1, EXPERTS * EXPERTS])
        neg, eps, hold = s.sb("neg", [P, 3]), s.sb("eps", [P, 3]), s.sb("hold", [P, 1])
        ebase = s.sb("ebase", [P, 3 * EXPERTS])

        ht, mt = s.sb("ht", [P, 3, D]), s.sb("mt", [P, 3, D])
        st, mv, ln = s.sb("st", [P, 3, 6]), s.sb("mv", [P, 3, 2]), s.sb("ln", [P, 6, 3])
        x1, xn, hx = s.sb("x1", [P, 3, D]), s.sb("xn", [P, 3, D]), s.sb("hx", [P, 3, D])
        mxt, xnt = s.sb("mxt", [P, DC, N]), s.sb("xnt", [P, DC, N])
        zt, rt = s.sb("zt", [P, N]), s.sb("rt", [P, 4, N])
        qt, kt = s.sb("qt", [P, N]), s.sb("kt", [P, N])
        v = s.sb("v", [P, 3, 512])
        er = s.sb("er", [P, 5, 3 * IMGS])
        at = s.sb("at", [P, 3, P])
        hrt = s.sb("hrt", [P, 4, N])
        uh = s.sb("uh", [P, 3, 512])
        h1 = s.sb("h1", [P, 3, D])
        st2, mv2, ln2 = s.sb("st2", [P, 3, 6]), s.sb("mv2", [P, 3, 2]), s.sb("ln2", [P, 2, 3])
        xf = s.sb("xf", [P, 3, D])
        xft = s.sb("xft", [P, DC, N])
        lg = s.sb("lg", [P, 3, EXPERTS + 1])
        rs = s.sb("rs", [P, 3, 3])
        ex = s.sb("ex", [P, 2, 3, EXPERTS])
        pr = s.sb("pr", [P, 3, EXPERTS])
        cmp = s.sb("cmp", [P, 2, 3, EXPERTS * EXPERTS])
        rank = s.sb("rank", [P, 3, EXPERTS])
        gate = s.sb("gate", [P, 3, 1])
        comb = s.sb("comb", [P, 3, EXPERTS + 1])
        xfr = s.sb("xfr", [P, 2, DC, N], F32R)
        he = s.sb("he", [P, DC, N])
        her = s.sb("her", [P, 2, 2, DC, N], F32R)
        sg = s.sb("sg", [P, DC, N])
        acc = s.sb("acc", [P, 3, D])

        bank = [s.ps(f"bank{k}", [P, 512]) for k in range(4)]
        up = s.ps("up", [P, DC, 512])
        down = s.ps("down", [P, 2, 512])

        names = ("weights init rot_step bias_done ht_in mt_in stats aggr rstd pool_step x1_ready xn_ready hx_ready "
                 "mt_turned xn_turned mxt_ready xnt_ready zr_done zr_silu qk_ready sc_done erf_step at_ready v_done "
                 "vb_ready v_ready av_done hr_ready uh_done pre_ready uh_act comb_step h1_ready stats2 aggr2 rstd2 "
                 "pool_step2 xf_ready xft_done xft_ready rt_done gate_tanh route_step exp_done comb_ready up_done "
                 "eh_silu sh_mult down_done sum_done h2_out raw_high raw_used xft_high xft_low he_high he_low sh_high").split()
        (weights, init, rot_step, bias_done, ht_in, mt_in, stats, aggr, rstd, pool_step, x1_ready, xn_ready, hx_ready,
         mt_turned, xn_turned, mxt_ready, xnt_ready, zr_done, zr_silu, qk_ready, sc_done, erf_step, at_ready, v_done,
         vb_ready, v_ready, av_done, hr_ready, uh_done, pre_ready, uh_act, comb_step, h1_ready, stats2, aggr2, rstd2,
         pool_step2, xf_ready, xft_done, xft_ready, rt_done, gate_tanh, route_step, exp_done, comb_ready, up_done,
         eh_silu, sh_mult, down_done, sum_done, h2_out, raw_high, raw_used, xft_high, xft_low, he_high, he_low, sh_high) = [s.sem(x) for x in names]
        block = s.block()
        raw_in = [s.sem(f"raw_in{k}") for k in range(2)]
        NERF, NROUTE = 16, 11
        INIT = 7
        loads = [(ident[:], T["ident"]), (lnw[:], T["ln_w"]), (lnb[:], T["ln_b"]),
                 (wv[:], T["wv"].rearrange("(c p) n -> p c n", p=P)),
                 (wzr[:], T["wzr"].rearrange("(c p) n -> p c n", p=P)),
                 (wuh[:], T["wuh"].rearrange("(c p) n -> p c n", p=P)),
                 (wh[:], T["wh"].rearrange("(c p) n -> p c n", p=P)),
                 (bv[:], T["bv"].broadcast_to([P, 512])), (buh[:], T["buh"].broadcast_to([P, 512])),
                 (bh[:], T["bh"].broadcast_to([P, D])), (bzr[:], T["bzr"]), (qk[:], T["qk"]), (rot[:], T["rot"]),
                 (trig[:], T["trig"]),
                 (wr[:], T["wr"].rearrange("(c p) n -> p c n", p=P)),
                 (lower[:, 0, :], T["lower"].broadcast_to([P, EXPERTS * EXPERTS]))]
        LOADED = 16 * len(loads)
        pairs = [(w, e, 2, T[name][e:e + 2].rearrange("e (c p) n -> p e c n", p=P))
                 for w, name in ((w1, "w1"), (w2, "w2")) for e in range(0, EXPERTS, 2)]
        pairs += [(w1, EXPERTS, 2, T["wgu"].rearrange("(c p) (e n) -> p e c n", p=P, e=2)),
                  (w2, EXPERTS, 1, T["wsd"].rearrange("(c p) (e n) -> p e c n", p=P, e=1))]
        PARTS = ((1, 0), (0, 1), (0, 0))

        @block.sync
        def _(sp):
            for dst, src in loads:
                sp.dma_start(dst, src).then_inc(weights, 16)
            with sp.Fori(0, GRP) as n:
                sp.wait_ge(hx_ready, n + 1)
                for b in range(4):
                    sp.dma_start(ht[IMGS * b:IMGS * (b + 1)],
                                 h0.rearrange("t (g j b) d -> g b t j d", j=3, b=4)[n, b]
                                 ).then_inc(ht_in, 16)
                sp.wait_ge(mt_turned, n + 1)
                sp.dma_start(mt[:], mx.rearrange("(g j b) t d -> g (b t) j d", j=3, b=4)[n]
                             ).then_inc(mt_in, 16)
            sp.wait_ge(h2_out, 64 * GRP + 64)

        @block.tensor
        def _(pe):
            pe.wait_ge(weights, LOADED)

            def turn_in(n):
                pe.wait_ge(mt_in, 16 * n + 16)
                pe.wait_ge(xft_ready, 2 * n + 2)
                pe.wait_ge(hr_ready, 3 * n + 3)
                pe.wait_ge(route_step, NROUTE * n + 1)
                for c in range(DC):
                    for j in range(3):
                        mm = pe.transpose(bank[c][:, j * P:(j + 1) * P], mt[:, j, c * P:(c + 1) * P], ident[:])
                mm.then_inc(mt_turned, 1)
                pe.wait_ge(xn_ready, 3 * n + 3)
                pe.wait_ge(pre_ready, 3 * n + 3)
                for c in range(DC):
                    for j in range(3):
                        mm = pe.transpose(bank[2 + c][:, j * P:(j + 1) * P], xn[:, j, c * P:(c + 1) * P], ident[:])
                mm.then_inc(xn_turned, 1)

            def z_r(n, q):
                if q == 0:
                    pe.wait_ge(mxt_ready, 2 * n + 4)
                if q == 2:
                    pe.wait_ge(xnt_ready, 2 * n + 4)
                if q == 4:
                    pe.wait_ge(zr_silu, 5 * n + 1)
                for c in range(DC):
                    mm = pe.matmul(bank[q % 4][:, 0:N], wzr[:, c, q * P:(q + 1) * P], mxt[:, c, :],
                                   start=c == 0, stop=c == DC - 1)
                mm.then_inc(zr_done, 1)

            def scores(n):
                pe.wait_ge(qk_ready, 2 * n + 4)
                pe.wait_ge(zr_silu, 5 * n + 2)
                for j in range(3):
                    for b in range(4):
                        o = j * P + b * IMGS
                        mm = pe.matmul(bank[1][b * IMGS:(b + 1) * IMGS, j * IMGS:(j + 1) * IMGS],
                                       kt[:, o:o + IMGS], qt[:, o:o + IMGS], start=True, stop=True)
                mm.then_inc(sc_done, 1)

            def values(n):
                pe.wait_ge(zr_silu, 5 * n + 5)
                for j, k in enumerate((0, 2, 3)):
                    for c in range(DC):
                        mm = pe.matmul(bank[k][:, :], xnt[:, c, j * P:(j + 1) * P], wv[:, c, :],
                                       start=c == 0, stop=c == DC - 1)
                    mm.then_inc(v_done, 1)

            def attend(n):
                pe.wait_ge(at_ready, 4 * n + 4)
                pe.wait_ge(v_ready, 3 * n + 6)
                for j, k in enumerate((1, 0, 2)):
                    for f in range(4):
                        mm = pe.matmul(bank[k][:, f * P:(f + 1) * P], v[:, j, f * P:(f + 1) * P], at[:, j, :],
                                       start=True, stop=True)
                    mm.then_inc(av_done, 1)

            def update(n):
                for j, k in enumerate((3, 1, 0)):
                    pe.wait_ge(hr_ready, 3 * n + 6)
                    for c in range(DC):
                        pe.matmul(bank[k][:, :], mxt[:, c, j * P:(j + 1) * P], wuh[:, c, :], start=c == 0, stop=False,
                                  skip_group_check=True)
                    for f in range(4):
                        mm = pe.matmul(bank[k][:, D:], hrt[:, f, j * P:(j + 1) * P], wh[:, f, :],
                                       start=False, stop=f == 3, skip_group_check=True)
                    mm.then_inc(uh_done, 1)

            def turn_out(n):
                pe.wait_ge(xf_ready, 3 * n + 3)
                pe.wait_ge(pre_ready, 3 * n + 6)
                for c, k in enumerate((0, 2)):
                    for j in range(3):
                        mm = pe.transpose(bank[k][:, j * P:(j + 1) * P], xf[:, j, c * P:(c + 1) * P], ident[:])
                mm.then_inc(xft_done, 1)

            def router(n):
                pe.wait_ge(xft_ready, 2 * n + 4)
                for j in range(3):
                    for c in range(DC):
                        mm = pe.matmul(bank[1][:, 16 * j:16 * j + EXPERTS + 1], xft[:, c, j * P:(j + 1) * P],
                                       wr[:, c, :], start=c == 0, stop=c == DC - 1)
                mm.then_inc(rt_done, 1)

            def up_proj(m, e):
                if e == 0:
                    pe.wait_ge(sh_mult, m + 1)
                    pe.wait_ge(xft_low, m + 2)
                else:
                    pe.wait_ge(eh_silu, 9 * m + e)
                for f in range(DC):
                    for c in range(DC):
                        for a, b in PARTS:
                            mm = pe.matmul(up[:, f, 0:N], w1[:, a, e, c, f * P:(f + 1) * P], xfr[:, b, c, :],
                                           start=(a, c) == (1, 0), stop=(a, b, c) == (0, 0, DC - 1))
                mm.then_inc(up_done, 1)

            def down_proj(m, e):
                pe.wait_ge(he_low, 9 * m + e + 2)
                pe.wait_ge(sum_done, 27 * m + 3 * e + 27)
                for j in range(3):
                    for f in range(DC):
                        for a, b in PARTS:
                            mm = pe.matmul(down[:, j // 2, (j % 2) * D:(j % 2 + 1) * D],
                                           her[:, e % 2, b, f, j * P:(j + 1) * P], w2[:, a, e, f, :],
                                           start=(a, f) == (1, 0), stop=(a, b, f) == (0, 0, DC - 1))
                mm.then_inc(down_done, 1)

            def attention(n):
                turn_in(n)
                for q in range(5):
                    z_r(n, q)
                scores(n)
                values(n)
                attend(n)
                update(n)
                turn_out(n)

            def body(m, n):
                between = {}
                if n is not None:
                    between = {0: (lambda: turn_in(n),), 1: (lambda: z_r(n, 0), lambda: z_r(n, 1), lambda: z_r(n, 2)),
                               2: (lambda: z_r(n, 3), lambda: z_r(n, 4), lambda: scores(n)), 3: (lambda: values(n),),
                               4: (lambda: attend(n),), 5: (lambda: update(n),)}
                up_proj(m, 0)
                for e in range(EXPERTS):
                    for part in between.get(e, ()):
                        part()
                    up_proj(m, e + 1)
                    down_proj(m, e)
                up_proj(m, EXPERTS + 1)
                if n is not None:
                    turn_out(n)
                    router(n)
                down_proj(m, EXPERTS)

            pe.wait_ge(rot_step, 6)
            pe.matmul(bank[0][:, 0:IMGS], rotb[:, :, :].rearrange("p a b -> p (a b)"), rotated[:, 0, :],
                      start=True, stop=True).then_inc(bias_done, 1)
            pe.wait_ge(init, INIT)
            attention(0)
            router(0)
            pe.wait_ge(raw_used, len(pairs))
            with pe.Fori(0, GRP - 1) as m:
                body(m, m + 1)
            body(GRP - 1, None)

        @block.scalar
        def _(act):
            act.wait_ge(weights, LOADED)
            act.wait_ge(init, INIT)

            def high_weights(*ks):
                for k in ks:
                    w, e, count, _ = pairs[k]
                    act.wait_ge(raw_in[k % 2], 16 * (k // 2) + 16)
                    act.activation(w[:, 0, e:e + count], raw[:, k % 2, 0:count], ACT.Copy).then_inc(raw_high, 1)

            def evac_in(n):
                act.wait_ge(mt_turned, n + 2)
                act.wait_ge(uh_done, 3 * n + 3)
                for c in range(DC):
                    act.activation(mxt[:, c, :], bank[c][:, 0:N], ACT.Copy).then_inc(mxt_ready, 1)
                act.wait_ge(xn_turned, n + 2)
                act.wait_ge(v_done, 3 * n + 3)
                for c in range(DC):
                    act.activation(xnt[:, c, :], bank[2 + c][:, 0:N], ACT.Identity, bias=lnb[:, c:c + 1],
                                   scale=lnw[:, c:c + 1]).then_inc(xnt_ready, 1)

            def evac_zr(n, q):
                act.wait_ge(zr_done, 5 * n + q + 1)
                if q == 0:
                    act.wait_ge(qk_ready, 2 * n + 2)
                if q == 1:
                    act.wait_ge(hr_ready, 3 * n + 3)
                act.activation(zt[:] if q == 0 else rt[:, q - 1, :], bank[q % 4][:, 0:N], ACT.Silu,
                               bias=bzr[:, q:q + 1]).then_inc(zr_silu, 1)

            def silu_v(n):
                act.wait_ge(av_done, 3 * n + 3)
                for j in range(3):
                    act.wait_ge(vb_ready, 3 * n + j + 1)
                    act.activation(v[:, j, :], v[:, j, :], ACT.Silu).then_inc(v_ready, 1)

            def act_uh(n):
                for j in range(3):
                    act.wait_ge(pre_ready, 3 * n + j + 4)
                    act.activation(uh[:, j, 0:D], uh[:, j, 0:D], ACT.Tanh, scale=0.5).then_inc(uh_act, 1)
                    act.activation(uh[:, j, D:], uh[:, j, D:], ACT.Silu).then_inc(uh_act, 1)

            def evac_out(n):
                act.wait_ge(xft_done, n + 2)
                for c, k in enumerate((0, 2)):
                    act.activation(xft[:, c, :], bank[k][:, 0:N], ACT.Copy).then_inc(xft_ready, 1)
                act.wait_ge(xft_ready, 2 * n + 4)
                act.activation(xfr[:, 0], xft[:], ACT.Copy).then_inc(xft_high, 1)

            def tanh_gate(n):
                act.wait_ge(route_step, NROUTE * n + NROUTE + 1)
                act.wait_ge(comb_ready, n + 1)
                act.activation(gate[:], lg[:, :, EXPERTS:], ACT.Tanh,
                               scale=0.5).then_inc(gate_tanh, 1)

            def silu_e(m, e):
                act.wait_ge(up_done, 10 * m + e + 1)
                if e == EXPERTS:
                    act.wait_ge(sh_mult, m + 1)
                    act.activation(sg[:], up[:, :, 0:N], ACT.Silu).then_inc(eh_silu, 1)
                    return
                act.wait_ge(he_low, 9 * m + e + 1)
                act.activation(he[:], up[:, :, 0:N], ACT.Silu).then_inc(eh_silu, 1)
                act.wait_ge(eh_silu, 9 * m + e + 1)
                act.wait_ge(down_done, 9 * m + (2, 1)[e] if e < 2 else 9 * m + e + 1)
                act.activation(her[:, e % 2, 0], he[:], ACT.Copy).then_inc(he_high, 1)

            def store(m):
                act.wait_ge(sum_done, 27 * m + 54)
                for b in range(4):
                    act.dma_start(h2.rearrange("t (g j b) d -> g b t j d", j=3, b=4)[m, b],
                                  acc[IMGS * b:IMGS * (b + 1)]).then_inc(h2_out, 16)

            def first_attention():
                evac_in(0)
                high_weights(0, 1)
                for q in range(5):
                    evac_zr(0, q)
                high_weights(2, 3)
                silu_v(0)
                high_weights(4, 5, 6)
                act_uh(0)
                high_weights(7, 8, 9)
                evac_out(0)
                tanh_gate(0)

            def body(m, n):
                silu_e(m, 0)
                evac_in(n)
                silu_e(m, 1)
                for q in range(3):
                    evac_zr(n, q)
                silu_e(m, 2)
                for q in range(3, 5):
                    evac_zr(n, q)
                silu_e(m, 3)
                silu_v(n)
                silu_e(m, 4)
                silu_e(m, 5)
                act_uh(n)
                for e in range(6, EXPERTS + 1):
                    silu_e(m, e)
                evac_out(n)
                tanh_gate(n)
                store(m)

            first_attention()
            with act.Fori(0, GRP - 1) as m:
                body(m, m + 1)
            for e in range(9):
                silu_e(GRP - 1, e)
            store(GRP - 1)

        @block.gpsimd
        def _(pool):
            for sem, credit in ((hx_ready, 1), (mt_turned, 1), (xn_turned, 1), (uh_done, 3), (v_done, 3), (qk_ready, 2),
                                (hr_ready, 3), (av_done, 3), (comb_ready, 1), (down_done, 2), (he_low, 1), (xft_low, 1), (h1_ready, 1),
                                (xft_done, 1), (rstd, 1), (rstd2, 1), (xft_ready, 2), (pre_ready, 3), (gate_tanh, 1),
                                (route_step, NROUTE), (sc_done, 1), (v_ready, 3), (uh_act, 6), (sum_done, 27), (sh_mult, 1),
                                (h2_out, 64), (mxt_ready, 2), (xnt_ready, 2), (exp_done, 1)):
                if credit:
                    pool.sem_inc(sem, credit)
            pool.memset(neg[:], -0.5).then_inc(init, 1)
            pool.memset(eps[:], EPS).then_inc(init, 1)
            pool.memset(ebase[:], float(np.float32(np.e))).then_inc(init, 1)
            pool.memset(at[:], 0.0).then_inc(init, 1)
            pool.sem_inc(init, 1)
            pool.wait_ge(init, INIT)

            def rsqrt1(n):
                pool.wait_ge(aggr, 3 * n + 3)
                pool.wait_ge(hx_ready, n + 1)
                norm_chain(pool, mv, neg, eps, ln, pool_step, 6 * n).then_inc(rstd, 1)

            def rsqrt2(n):
                pool.wait_ge(aggr2, 3 * n + 3)
                if not isinstance(n, int) or n > 0:
                    pool.wait_ge(xf_ready, 3 * n)
                pool.tensor_tensor(ln2[:, 0, :], mv2[:, :, 1], eps[:], ALU.add).then_inc(pool_step2, 1)
                pool.wait_ge(pool_step2, n + 1)
                pool.tensor_tensor(ln2[:, 1, :], ln2[:, 0, :], neg[:], ALU.pow).then_inc(rstd2, 1)

            def exps(n):
                pool.wait_ge(route_step, NROUTE * n + NROUTE + 3)
                pool.tensor_tensor(ex[:, 1].rearrange("p j e -> p (j e)"), ebase[:],
                                   ex[:, 0].rearrange("p j e -> p (j e)"), ALU.pow).then_inc(exp_done, 1)

            def load_weights(k):
                if k >= 2:
                    pool.wait_ge(raw_used, k - 1)
                pool.dma_start(raw[:, k % 2, 0:pairs[k][2]], pairs[k][3]).then_inc(raw_in[k % 2], 16)

            load_weights(0)
            load_weights(1)
            rsqrt1(0)
            for k in range(2, len(pairs)):
                load_weights(k)
            rsqrt2(0)
            rsqrt1(1)
            exps(0)
            with pool.Fori(1, GRP - 1) as n:
                rsqrt2(n)
                rsqrt1(n + 1)
                exps(n)
            rsqrt2(GRP - 1)
            exps(GRP - 1)

        @block.vector
        def _(dve):
            dve.wait_ge(weights, LOADED)
            one = Chain(dve, rot_step, 0)
            one(dve.tensor_scalar(rotated[:, 1, :], trig[:, 1, :], rot[:, 1:2], None, ALU.mult))
            one(dve.scalar_tensor_tensor(rotated[:, 0, :], trig[:, 0, :], rot[:, 0:1], rotated[:, 1, :],
                                         ALU.mult, ALU.add))
            one(dve.tensor_scalar(rotated[:, 1, :], trig[:, 1, :], rot[:, 3:4], None, ALU.mult))
            one(dve.scalar_tensor_tensor(rotated[:, 2, :], trig[:, 0, :], rot[:, 2:3], rotated[:, 1, :],
                                         ALU.mult, ALU.add))
            one(dve.tensor_copy(rotb[:], rotated[:, 2:3, :].broadcast_to([P, 4, IMGS])))
            one(dve.tensor_tensor(buh[:, D:], buh[:, D:], bh[:], ALU.add))
            dve.wait_ge(bias_done, 1)
            dve.tensor_scalar(biasc[:, 0, :], bank[0][:, 0:IMGS], ERF_SCALE, -MU * ERF_SCALE,
                              ALU.mult, ALU.add).then_inc(init, 1)
            dve.sem_inc(init, 1)
            dve.wait_ge(init, INIT)

            def low_weights(*ks):
                for k in ks:
                    w, e, count, _ = pairs[k]
                    dve.wait_ge(raw_high, k + 1)
                    dve.tensor_tensor(w[:, 1, e:e + count], raw[:, k % 2, 0:count], w[:, 0, e:e + count], ALU.subtract
                                      ).then_inc(raw_used, 1)

            def stats_in(n):
                dve.wait_ge(ht_in, 64 * n + 64)
                for j in range(3):
                    dve.bn_stats(st[:, j, :], ht[:, j, :]).then_inc(stats, 1)
                dve.wait_ge(rstd, n + 1)
                dve.wait_ge(stats, 3 * n + 3)
                dve.memset(hold[:], 0.0)
                for j in range(3):
                    dve.bn_aggr(mv[:, j, :], st[:, j, :]).then_inc(aggr, 1)

            def norm_twice(n):
                dve.wait_ge(rstd, n + 2)
                dve.wait_ge(xn_turned, n + 1)
                for j in range(3):
                    dve.tensor_scalar(xn[:, j, :], ht[:, j, :], mv[:, j, 0:1], ln[:, 5, j:j + 1],
                                      ALU.subtract, ALU.mult).then_inc(xn_ready, 1)

            def norm_once(n):
                dve.wait_ge(h1_ready, n + 1)
                for j in range(3):
                    dve.tensor_scalar(x1[:, j, :], ht[:, j, :], mv[:, j, 0:1], ln[:, 1, j:j + 1],
                                      ALU.subtract, ALU.mult).then_inc(x1_ready, 1)
                dve.wait_ge(x1_ready, 3 * n + 3)
                dve.tensor_tensor(hx[:], ht[:], x1[:], ALU.add).then_inc(hx_ready, 1)

            def make_qk(n):
                dve.wait_ge(zr_silu, 5 * n + 1)
                dve.wait_ge(sc_done, n + 1)
                dve.tensor_scalar(qt[:], zt[:], qk[:, 0:1], qk[:, 2:3], ALU.mult, ALU.add).then_inc(qk_ready, 1)
                dve.tensor_scalar(kt[:], zt[:], qk[:, 1:2], qk[:, 3:4], ALU.mult, ALU.add).then_inc(qk_ready, 1)

            def erf(n):
                dve.wait_ge(sc_done, n + 2)
                step = Chain(dve, erf_step, NERF * n)
                x, xx, p, q, iq = (er[:, k, :] for k in range(5))
                step(dve.scalar_tensor_tensor(x.rearrange("p (j l) -> p j l", j=3),
                                              bank[1][:, 0:3 * IMGS].rearrange("p (j l) -> p j l", j=3),
                                              ERF_SCALE / IMGS, biasc[:].broadcast_to([P, 3, IMGS]), ALU.mult, ALU.add))
                step(dve.tensor_scalar(x, x, -4.0, 4.0, ALU.max, ALU.min))
                step(dve.tensor_tensor(xx, x, x, ALU.mult))
                step(dve.tensor_scalar(p, xx, ERF_P[0], None, ALU.mult))
                for c in ERF_P[1:-1]:
                    step(dve.scalar_tensor_tensor(p, p, c, xx, ALU.add, ALU.mult))
                dve.scalar_tensor_tensor(p, p, ERF_P[-1], x, ALU.add, ALU.mult)
                step(dve.tensor_scalar(q, xx, ERF_Q[0], None, ALU.mult))
                for c in ERF_Q[1:-1]:
                    step(dve.scalar_tensor_tensor(q, q, c, xx, ALU.add, ALU.mult))
                step(dve.tensor_scalar(q, q, ERF_Q[-1], None, ALU.add))
                step(dve.reciprocal(iq, q))
                step(dve.scalar_tensor_tensor(p, p, 0.5, iq, ALU.mult, ALU.mult))
                dve.wait_ge(av_done, 3 * n + 3)
                for b in range(4):
                    rows = slice(IMGS * b, IMGS * (b + 1))
                    dve.tensor_scalar(at[rows, :, IMGS * b:IMGS * (b + 1)],
                                      p.rearrange("p (j l) -> p j l", j=3)[rows], 0.5, None,
                                      ALU.add).then_inc(at_ready, 1)

            def bias_v(n):
                dve.wait_ge(av_done, 3 * n + 3)
                for j, k in enumerate((0, 2, 3)):
                    dve.wait_ge(v_done, 3 * n + j + 4)
                    dve.tensor_tensor(v[:, j, :], bank[k][:, :], bv[:], ALU.add).then_inc(vb_ready, 1)

            def times_r(n):
                dve.wait_ge(uh_done, 3 * n + 3)
                for j, k in enumerate((1, 0, 2)):
                    dve.wait_ge(av_done, 3 * n + j + 4)
                    dve.tensor_tensor(hrt[:, :, j * P:(j + 1) * P], bank[k][:, :].rearrange("p (f l) -> p f l", f=4),
                                      rt[:, :, j * P:(j + 1) * P], ALU.mult).then_inc(hr_ready, 1)

            def bias_uh(n):
                dve.wait_ge(h1_ready, n + 1)
                for j, k in enumerate((3, 1, 0)):
                    dve.wait_ge(uh_done, 3 * n + j + 4)
                    dve.tensor_tensor(uh[:, j, :], bank[k][:, :], buh[:], ALU.add).then_inc(pre_ready, 1)

            def combine(n):
                dve.wait_ge(uh_act, 6 * n + 12)
                dve.wait_ge(sum_done, 27 * n + 3)
                u, c = uh[:, :, 0:D], uh[:, :, D:]
                step = Chain(dve, comb_step, 2 * n)
                step(dve.tensor_tensor(c, c, x1[:], ALU.subtract))
                step(dve.scalar_tensor_tensor(c, u, 1.0, c, ALU.add, ALU.mult))
                dve.scalar_tensor_tensor(h1[:], c, 0.5, hx[:], ALU.mult, ALU.add).then_inc(h1_ready, 1)

            def stats_out(n):
                dve.wait_ge(h1_ready, n + 2)
                for j in range(3):
                    dve.bn_stats(st2[:, j, :], h1[:, j, :]).then_inc(stats2, 1)
                dve.wait_ge(stats2, 3 * n + 3)
                dve.memset(hold[:], 0.0)
                for j in range(3):
                    dve.bn_aggr(mv2[:, j, :], st2[:, j, :]).then_inc(aggr2, 1)

            def norm_out(n):
                dve.wait_ge(rstd2, n + 2)
                dve.wait_ge(xft_done, n + 1)
                for j in range(3):
                    dve.tensor_scalar(xf[:, j, :], h1[:, j, :], mv2[:, j, 0:1], ln2[:, 1, j:j + 1],
                                      ALU.subtract, ALU.mult).then_inc(xf_ready, 1)

            def route(n):
                dve.wait_ge(rt_done, n + 1)
                step = Chain(dve, route_step, NROUTE * n + NROUTE)
                E3 = [P, 3, EXPERTS]
                dve.wait_ge(gate_tanh, n + 1)
                step(dve.tensor_copy(lg[:], bank[1][:, 0:48].rearrange("p (j x) -> p j x", j=3)[:, :, 0:EXPERTS + 1]))
                step(dve.tensor_reduce(rs[:, 0, :], lg[:, :, 0:EXPERTS], AX.X, ALU.max))
                step(dve.tensor_tensor(ex[:, 0], lg[:, :, 0:EXPERTS], rs[:, 0, :].unsqueeze(2).broadcast_to(E3), ALU.subtract))

            def weigh(n):
                E3 = [P, 3, EXPERTS]
                step = Chain(dve, route_step, NROUTE * n + NROUTE + 3)
                dve.wait_ge(exp_done, n + 2)
                step(dve.tensor_reduce(rs[:, 1, :], ex[:, 1], AX.X, ALU.add))
                step(dve.reciprocal(rs[:, 2, :], rs[:, 1, :]))
                step(dve.tensor_tensor(pr[:], ex[:, 1], rs[:, 2, :].unsqueeze(2).broadcast_to(E3), ALU.mult))
                EE = [P, 3, EXPERTS, EXPERTS]
                other = pr[:].unsqueeze(2).broadcast_to(EE)
                own = pr[:].unsqueeze(3).broadcast_to(EE)
                gt, eq = (cmp[:, k].rearrange("p j (a b) -> p j a b", a=EXPERTS) for k in range(2))
                dve.tensor_tensor(gt, other, own, ALU.is_gt)
                step(dve.tensor_tensor(eq, other, own, ALU.is_equal))
                step(dve.tensor_tensor(cmp[:, 1], cmp[:, 1], lower[:].broadcast_to([P, 3, EXPERTS * EXPERTS]), ALU.mult))
                step(dve.tensor_tensor(cmp[:, 0], cmp[:, 0], cmp[:, 1], ALU.add))
                step(dve.tensor_reduce(rank[:], gt, AX.X, ALU.add))
                dve.wait_ge(sum_done, 27 * n + 27)
                step(dve.scalar_tensor_tensor(comb[:, :, 0:EXPERTS], rank[:], 1.5, pr[:], ALU.is_lt, ALU.mult))
                dve.wait_ge(gate_tanh, n + 2)
                dve.tensor_scalar(comb[:, :, EXPERTS:], gate[:], 0.5, 0.5, ALU.mult, ALU.add).then_inc(comb_ready, 1)

            def add_expert(m, e):
                dve.wait_ge(down_done, 9 * m + e + 3)
                if e == 0:
                    dve.wait_ge(comb_ready, m + 2)
                    dve.wait_ge(h2_out, 64 * m + 64)
                else:
                    dve.wait_ge(sum_done, 27 * m + 3 * e + 27)
                for j in range(3):
                    dve.scalar_tensor_tensor(acc[:, j, :], down[:, j // 2, (j % 2) * D:(j % 2 + 1) * D],
                                             comb[:, j, e:e + 1], (h1 if e == 0 else acc)[:, j, :],
                                             ALU.mult, ALU.add).then_inc(sum_done, 1)

            def gate_shared(m):
                dve.wait_ge(up_done, 10 * m + 10)
                dve.wait_ge(eh_silu, 9 * m + 9)
                dve.wait_ge(he_low, 9 * m + 9)
                dve.tensor_tensor(he[:], sg[:], up[:, :, 0:N], ALU.mult).then_inc(sh_mult, 1)
                dve.wait_ge(sh_mult, m + 2)
                dve.wait_ge(down_done, 9 * m + 9)
                dve.tensor_copy(her[:, 0, 0], he[:]).then_inc(sh_high, 1)
                dve.wait_ge(sh_high, m + 1)
                dve.tensor_tensor(her[:, 0, 1], he[:], her[:, 0, 0], ALU.subtract).then_inc(he_low, 1)

            def low_e(m, e):
                dve.wait_ge(he_high, 8 * m + e + 1)
                dve.tensor_tensor(her[:, e % 2, 1], he[:], her[:, e % 2, 0], ALU.subtract).then_inc(he_low, 1)

            def low_xft(n):
                dve.wait_ge(xft_high, n + 1)
                dve.tensor_tensor(xfr[:, 1], xft[:], xfr[:, 0], ALU.subtract).then_inc(xft_low, 1)

            def first_attention():
                stats_in(0)
                norm_twice(0)
                norm_once(0)
                low_weights(0, 1)
                make_qk(0)
                low_weights(2, 3)
                erf(0)
                bias_v(0)
                low_weights(4, 5, 6)
                times_r(0)
                bias_uh(0)
                low_weights(7, 8, 9)
                combine(0)
                stats_out(0)
                norm_out(0)
                stats_in(1)
                low_xft(0)
                route(0)

            def body(m, n, after):
                norm_twice(n)
                low_e(m, 0)
                weigh(m)
                norm_once(n)
                low_e(m, 1)
                add_expert(m, 0)
                make_qk(n)
                low_e(m, 2)
                add_expert(m, 1)
                erf(n)
                low_e(m, 3)
                add_expert(m, 2)
                bias_v(n)
                low_e(m, 4)
                add_expert(m, 3)
                times_r(n)
                low_e(m, 5)
                add_expert(m, 4)
                bias_uh(n)
                combine(n)
                low_e(m, 6)
                add_expert(m, 5)
                stats_out(n)
                low_e(m, 7)
                add_expert(m, 6)
                norm_out(n)
                add_expert(m, 7)
                gate_shared(m)
                low_xft(n)
                if after is not None:
                    stats_in(after)
                add_expert(m, 8)
                route(n)

            first_attention()
            with dve.Fori(0, GRP - 2) as m:
                body(m, m + 1, m + 2)
            body(GRP - 2, GRP - 1, None)
            weigh(GRP - 1)
            for e in range(EXPERTS):
                low_e(GRP - 1, e)
                add_expert(GRP - 1, e)
            gate_shared(GRP - 1)
            add_expert(GRP - 1, EXPERTS)


HEADS, HD, R = 8, 64, 32
INNER = HEADS * HD
NSH = P - R
KL = 7
WIDTHS = [TOKS - TC * j for j in range(3)]
OFFS = [0, 324, 540]
SPAN = sum(WIDTHS)
TURN = 6.283185
ROUND = 1.5 * 2.0 ** 23
PREP = "tA0 tA1 gates ang x0 x1 x2 dd Csh Bsh d0 d1 d2 d3 lt Ga Gb C B z0 z1 z2".split()
RING = 4
AHEAD = ((), (2, 3), (4, 5), (6,), (7,), (), (), (), ())
TAIL = "og0 og1 og2 og3 wo0 wo1 wo2 xe0 xe1 re0 re1 re2".split()


class Signal:
    every = []

    def __init__(self, stage, name, per):
        self.sem, self.per = stage.sem(name), per
        Signal.every.append(self)

    def now(self, n, k=None):
        return self.per * (n + 1) + (self.per if k is None else k)

    def before(self, n, k=None):
        return self.per * n + (self.per if k is None else k)


class Ring:

    def __init__(self, stage, tag, names, banks):
        self.names, self.banks, k = names, banks, len(banks)
        assert len(names) % k == 0
        self.full = [Signal(stage, f"{tag}_full{b}", len(names) // k) for b in range(k)]
        self.read = [Signal(stage, f"{tag}_read{b}", len(names) // k) for b in range(k)]

    def at(self, name):
        i, k = self.names.index(name), len(self.banks)
        return self.banks[i % k], self.full[i % k], self.read[i % k], i // k + 1


def scan_stage(nc, T, h2, lam_d, out):
    with Stage(nc, "scan") as s:
        ident = s.sb("ident", [P, P])
        wg, wx, wz = (s.sb(name, [P, 2, DC, w], F32R) for name, w in (("wg", 24), ("wx", INNER), ("wz", INNER)))
        wrep = s.sb("wrep", [P, 2, DC, 3 * P], F32R)
        wsh = s.sb("wsh", [P, 2, DC, 2 * NSH], F32R)
        wo = s.sb("wo", [P, 4, D])
        ff = s.sb("ff", [P, 2, DC, 2 * D])
        ffr = s.sb("ffr", [P, 2, DC, 2 * D], F32R)
        gbias = s.sb("gbias", [P, 1, 16])
        drep = s.sb("drep", [P, 1, INNER])
        sel = s.sb("sel", [16, 4, P])
        phase = s.sb("phase", [P, 2])
        negmask = s.sb("negmask", [TC, TC])
        ones = s.sb("ones", [P, TOKS])
        neg, eps, hold = s.sb("neg", [P, 3]), s.sb("eps", [P, 3]), s.sb("hold", [P, 1])

        ht, res = s.sb("ht", [TC, 3, D]), s.sb("res", [TC, 3, D])
        st, mv, ln = s.sb("st", [TC, 3, 6]), s.sb("mv", [TC, 3, 2]), s.sb("ln", [TC, 2, 3])
        xn, xnt = s.sb("xn", [TC, 3, D]), s.sb("xnt", [P, 2, DC, TOKS], F32R)
        gl, trt = s.sb("gl", [TC, 3, 24]), s.sb("trt", [TC, 3, 8])
        gx = s.sb("gx", [TC, 8, 3, 16])
        dd = s.sb("dd", [TC, 3, 16])
        gb = s.sb("gb", [TC, 4, 3, 8])
        al = s.sb("al", [TC, 3, 8])
        ddt, cs16 = s.sb("ddt", [16, TOKS]), s.sb("cs16", [16, TOKS])
        ta, thi = s.sb("ta", [P, TOKS]), s.sb("thi", [P, TOKS])
        th = s.sb("th", [P, 2, 4, TOKS])
        cs = s.sb("cs", [P, 4, TOKS])
        qr, kr = s.sb("qr", [P, 4, TOKS]), s.sb("kr", [P, 4, TOKS])
        csh, bsh = s.sb("csh", [NSH, TOKS]), s.sb("bsh", [NSH, TOKS])
        gsh = s.sb("gsh", [TC, SPAN])
        lam, nlam = s.sb("lam", [TC, 3, 8]), s.sb("nlam", [TC, 3, 8])
        lb = s.sb("lb", [TC, HEADS, TOKS])
        ld = s.sb("ld", [TC, RING, 3, TC])
        ee = s.sb("ee", [TC, RING, SPAN])
        mm_ = s.sb("m", [TC, 2, SPAN])
        x, xs = s.sb("x", [TC, 3, INNER]), s.sb("xs", [TC, 3, INNER])
        xg = s.sb("xg", [TC, 3, INNER])
        xb, xd, u = s.sb("xb", [TC, 3, INNER]), s.sb("xd", [TC, 3, INNER]), s.sb("u", [TC, 3, INNER])
        zs = s.sb("zs", [TC, 3, INNER])
        og, ogt = s.sb("og", [TC, 3, INNER]), s.sb("ogt", [P, 4, TOKS])
        h3 = s.sb("h3", [TC, 3, D])
        st2, mv2, ln2 = s.sb("st2", [TC, 3, 6]), s.sb("mv2", [TC, 3, 2]), s.sb("ln2", [TC, 2, 3])
        xe, xet = s.sb("xe", [TC, 3, D]), s.sb("xet", [P, 2, DC, TOKS], F32R)
        sq = s.sb("sq", [TC, 3, 2 * D])
        ob, ss = (ff[0:TC, k].rearrange("p c n -> p (c n)")[:, 0:3 * D].rearrange("p (j d) -> p j d", j=3)
                  for k in range(2))

        rot = s.ps("rot", [P, 2, 512])
        y = [s.ps(f"y{j}", [P, 512]) for j in range(3)]
        xbank = [s.ps(f"x{k}", [P, 512]) for k in range(2)]
        tbank = [s.ps("tail", [P, 512])]

        Signal.every = []
        prep, tail = Ring(s, "prep", PREP, xbank), Ring(s, "tail", TAIL, tbank)
        NG = KL + 16
        sigs = dict(ht_in=16, stats=3, aggr=3, rs_step=1, rstd=1, xn_ready=3, gate_tanh=1, g_step=NG, u_exp=1, al_exp=1,
                    scanned=1, d_step=4, turns=4, angles=1, r_step=1, sin_done=1, lam_step=1, lam_ready=1, lam_out=16, lb_in=16,
                    shifted=32, xb_ready=1, ug_ready=1, u_ready=1, xd_ready=1, ld_ready=24, e_done=40, rot_done=8,
                    a_done=8, m_ready=8, y_done=8, y_read=3, og_ready=3, res_in=16, h3_ready=3, stats2=3, aggr2=3,
                    rs_step2=1, rstd2=1, xe_ready=3, ss_ready=1, root=1, xn_high=2, xe_high=2, h4_ready=1, stored=16)
        S = {k: Signal(s, k, per) for k, per in sigs.items()}
        weights, init, ffs = s.sem("weights"), s.sem("init"), s.sem("ffs")
        block = s.block()
        INIT = 7

        def wait(eng, name, value):
            eng.wait_ge(S[name].sem, value)

        def now(eng, name, n, k=None):
            eng.wait_ge(S[name].sem, S[name].now(n, k))

        def before(eng, name, n, k=None):
            eng.wait_ge(S[name].sem, S[name].before(n, k))

        def reused(eng, name, i, h, k):
            if h >= RING:
                now(eng, name, i, k * (h - RING + 1))
            else:
                before(eng, name, i, k * (h + HEADS - RING + 1))

        def filled(eng, ring, n, name):
            bank, full, read, k = ring.at(name)
            eng.wait_ge(full.sem, full.now(n, k))
            return bank, read.sem

        def was_read(eng, ring, n, name):
            _, _, read, k = ring.at(name)
            eng.wait_ge(read.sem, read.now(n, k))

        def read_before(eng, ring, n, name):
            _, _, read, k = ring.at(name)
            eng.wait_ge(read.sem, read.before(n, k))

        def used_before(eng, ring, n, name):
            _, full, _, k = ring.at(name)
            eng.wait_ge(full.sem, full.before(n, k))

        def lent(buf, w):
            return buf.rearrange("p a b -> p (a b)")[:, 0:DC * w].rearrange("p (c n) -> p c n", c=DC)

        whole = {"wg": (wg, lent(th[:, 0], 24)), "wx": (wx, lent(qr[:], INNER)), "wz": (wz, lent(kr[:], INNER)),
                 "wrep": (wrep, lent(cs[:], 3 * P)), "wsh": (wsh, lent(th[:, 1], 2 * NSH))}
        loads = [(ident[:], T["ident"]),
                 *((buf, T[name].rearrange("(c p) n -> p c n", p=P)) for name, (_, buf) in whole.items()),
                 (wo[:], T["wo"].rearrange("(c p) n -> p c n", p=P)),
                 (ff[:, 0], T["ff"].rearrange("(c p) n -> p c n", p=P)),
                 (ff[:, 1], T["ffn"].rearrange("(c p) n -> p c n", p=P)),
                 (gbias[:, 0, :], T["gbias"].broadcast_to([P, 16])),
                 (drep[:, 0, :], T["drep"].broadcast_to([P, INNER])),
                 (sel[:], T["sel"]), (phase[:], T["phase"]), (negmask[:], T["negmask"])]
        LOADED = 16 * len(loads)
        FFS = 5 + 2 * (len(whole) + 1)

        PARTS = ((1, 0), (0, 1), (0, 0))

        def run(eng, body):
            body(1, 0, None, None, None)
            body(2, 1, 0, None, None)
            body(3, 2, 1, 0, None)
            with eng.Fori(2, IMGS - 2) as i:
                body(i + 2, i + 1, i, i - 1, i - 2)
            last = IMGS - 1
            body(None, last, last - 1, last - 2, last - 3)
            body(None, None, last, last - 1, last - 2)
            body(None, None, None, last, last - 1)
            body(None, None, None, None, last)

        @block.sync
        def _(sp):
            for dst, src in loads:
                sp.dma_start(dst, src).then_inc(weights, 16)

            def load(n):
                before(sp, "xn_ready", n)
                sp.dma_start(ht[:], h2[n].rearrange("(j p) d -> p j d", p=TC)).then_inc(S["ht_in"].sem, 16)

            def shift(n):
                was_read(sp, prep, n, "x2")
                before(sp, "xb_ready", n)
                sp.dma_start(xs[1:TC], x[0:TC - 1]).then_inc(S["shifted"].sem, 16)
                sp.dma_start(xs[0:1, 1:3, :], x[TC - 1:TC, 0:2, :]).then_inc(S["shifted"].sem, 16)

            def spread(n):
                now(sp, "scanned", n)
                before(sp, "lb_in", n)
                sp.dma_start(lam_d[n], cs16[8:16, :]).then_inc(S["lam_out"].sem, 16)
                now(sp, "lam_out", n)
                before(sp, "e_done", n)
                sp.dma_start(lb[:], lam_d[n].rearrange("(a h) t -> a h t", a=1).broadcast_to([TC, HEADS, TOKS])
                             ).then_inc(S["lb_in"].sem, 16)

            def load_res(t):
                before(sp, "h3_ready", t)
                sp.dma_start(res[:], h2[t].rearrange("(j p) d -> p j d", p=TC)).then_inc(S["res_in"].sem, 16)

            def store(t):
                now(sp, "h4_ready", t)
                sp.dma_start(out[t].rearrange("(j p) d -> p j d", p=TC), ob[:]).then_inc(S["stored"].sem, 16)

            def body(p, n, i, t, f):
                if t is not None:
                    load_res(t)
                if p is not None:
                    load(p)
                if f is not None:
                    store(f)
                if n is not None:
                    shift(n)
                    spread(n)

            sp.wait_ge(init, INIT)
            load(0)
            run(sp, body)
            sp.wait_ge(S["stored"].sem, S["stored"].before(IMGS))

        @block.tensor
        def _(pe):
            pe.wait_ge(weights, LOADED)
            pe.wait_ge(init, INIT)
            pe.wait_ge(ffs, FFS)

            def fill(ring, n, name, matmuls, after=()):
                bank, full, read, k = ring.at(name)
                latest = {read: k - 1}
                for piece in after:
                    _, _, other, m = ring.at(piece)
                    latest[other] = max(latest.get(other, 0), m)
                for signal, m in latest.items():
                    pe.wait_ge(signal.sem, signal.now(n, m))
                matmuls(bank).then_inc(full.sem, 1)

            def product(out, left, right):
                for c in range(DC):
                    for a, b in PARTS:
                        mm = pe.matmul(out, left(a, c), right(b, c), start=(a, c) == (1, 0),
                                       stop=(a, b, c) == (0, 0, DC - 1))
                return mm

            def turn_x(n, c):
                now(pe, "xn_ready", n)

                def mms(bank):
                    for j in range(3):
                        mm = pe.transpose(bank[:, j * TC:(j + 1) * TC], xn[:, j, c * P:(c + 1) * P], ident[0:TC, 0:TC])
                    return mm
                fill(prep, n, f"tA{c}", mms)

            def rows_of(n, name, w, width):
                def mms(bank):
                    for j in range(3):
                        mm = product(bank[0:TC, width * j:width * (j + 1)],
                                     lambda a, c: xnt[:, a, c, j * TC:(j + 1) * TC], lambda a, c: w[:, a, c, :])
                    return mm
                fill(prep, n, name, mms, after=("tA0", "tA1"))

            def tile_of(n, name, w, j):
                def mms(bank):
                    return product(bank[0:TC, :], lambda a, c: xnt[:, a, c, j * TC:(j + 1) * TC],
                                   lambda a, c: w[:, a, c, :])
                fill(prep, n, name, mms)

            def chans_of(n, name, w, m):
                def mms(bank):
                    return product(bank[0:m, 0:TOKS], lambda a, c: w[:, a, c, :], lambda a, c: xnt[:, a, c, :])
                fill(prep, n, name, mms)

            def turn_dd(n):
                now(pe, "g_step", n, NG - 4)

                def mms(bank):
                    for j in range(3):
                        mm = pe.transpose(bank[0:16, j * TC:(j + 1) * TC], dd[:, j, :], ident[0:TC, 0:TC])
                    return mm
                fill(prep, n, "dd", mms)

            def spread_dt(n, q):
                fill(prep, n, f"d{q}", lambda bank: pe.matmul(bank[:, 0:TOKS], sel[:, q, :], ddt[:],
                                                              start=True, stop=True), after=("dd",))

            def turn_lam(n):
                now(pe, "scanned", n)

                def mms(bank):
                    for j in range(3):
                        mm = pe.matmul(bank[0:TC, 16 * j:16 * (j + 1)], cs16[:, j * TC:(j + 1) * TC], ident[0:16, 0:16],
                                       start=True, stop=True)
                    return mm
                fill(prep, n, "lt", mms)

            def shared(n, name, tiles):
                def mms(bank):
                    for j in tiles:
                        o = OFFS[j] - OFFS[tiles[0]]
                        mm = pe.matmul(bank[0:TC, o:o + WIDTHS[j]], bsh[:, j * TC:(j + 1) * TC], csh[:, j * TC:],
                                       start=True, stop=True)
                    return mm
                fill(prep, n, name, mms, after=("Csh", "Bsh"))

            def scores(i, h):
                if h == 0:
                    was_read(pe, prep, i, "C")
                    was_read(pe, prep, i, "B")
                wait(pe, "a_done", 8 * i + 8 + h)
                r = slice(64 * (h % 2), 64 * (h % 2) + 64)
                for j in range(3):
                    o = 0 if j < 2 else WIDTHS[1]
                    mm = pe.matmul(rot[0:TC, min(j, 1), o:o + WIDTHS[j]], kr[r, h // 2, j * TC:(j + 1) * TC],
                                   qr[r, h // 2, j * TC:], start=True, stop=True)
                mm.then_inc(S["rot_done"].sem, 1)

            def apply(i, h):
                now(pe, "m_ready", i, h + 1)
                if h == 0:
                    now(pe, "u_ready", i)
                    before(pe, "y_read", i)
                for jt in range(3):
                    for js in range(jt + 1):
                        o = OFFS[js] + (jt - js) * TC
                        mm = pe.matmul(y[jt][0:TC, h * HD:(h + 1) * HD], mm_[:, h % 2, o:o + TC],
                                       u[:, js, h * HD:(h + 1) * HD], start=js == 0, stop=js == jt)
                mm.then_inc(S["y_done"].sem, 1)

            def turn_og(t, f):
                now(pe, "og_ready", t)

                def mms(bank):
                    for j in range(3):
                        mm = pe.transpose(bank[:, j * TC:(j + 1) * TC], og[:, j, f * P:(f + 1) * P], ident[0:TC, 0:TC])
                    return mm
                fill(tail, t, f"og{f}", mms)

            def project(t, j):
                def mms(bank):
                    for f in range(4):
                        mm = pe.matmul(bank[0:TC, 0:D], ogt[:, f, j * TC:(j + 1) * TC], wo[:, f, :],
                                       start=f == 0, stop=f == 3)
                    return mm
                fill(tail, t, f"wo{j}", mms, after=("og3",))

            def turn_xe(t, c):
                now(pe, "xe_ready", t)

                def mms(bank):
                    for j in range(3):
                        mm = pe.transpose(bank[:, j * TC:(j + 1) * TC], xe[:, j, c * P:(c + 1) * P], ident[0:TC, 0:TC])
                    return mm
                fill(tail, t, f"xe{c}", mms)

            def real_imag(t, j):
                def mms(bank):
                    return product(bank[0:TC, :], lambda a, c: xet[:, a, c, j * TC:(j + 1) * TC],
                                   lambda a, c: ffr[:, a, c, :])
                fill(tail, t, f"re{j}", mms, after=("xe1",))

            def body(p, n, i, t, f):
                for slot in range(9):
                    if n is not None and slot == 5:
                        turn_dd(n)
                    if i is not None and slot < 8:
                        scores(i, slot)
                    if i is not None and slot > 0:
                        apply(i, slot - 1)
                    if i is not None and slot == 0:
                        tile_of(i, "z1", wz, 1)
                    if t is not None and slot in (0, 1):
                        turn_og(t, 2 * slot)
                    if i is not None and slot == 0:
                        tile_of(i, "z2", wz, 2)
                    if n is not None:
                        if slot == 1:
                            turn_x(n, 0)
                            turn_x(n, 1)
                        if slot == 2:
                            rows_of(n, "gates", wg, 24)
                            chans_of(n, "ang", wrep[:, :, :, 0:P], P)
                        if slot == 3:
                            tile_of(n, "x0", wx, 0)
                            tile_of(n, "x1", wx, 1)
                        if slot == 4:
                            tile_of(n, "x2", wx, 2)
                    if t is not None:
                        if slot in (0, 1):
                            turn_og(t, 2 * slot + 1)
                        if slot in (2, 3, 4):
                            project(t, slot - 2)
                    if n is not None:
                        if slot == 5:
                            chans_of(n, "Csh", wsh[:, :, :, 0:NSH], NSH)
                            chans_of(n, "Bsh", wsh[:, :, :, NSH:], NSH)
                            spread_dt(n, 0)
                            spread_dt(n, 1)
                        if slot == 6:
                            spread_dt(n, 2)
                            spread_dt(n, 3)
                    if t is not None and slot in (6, 7):
                        turn_xe(t, slot - 6)
                    if n is not None and slot == 7:
                        turn_lam(n)
                        shared(n, "Ga", (0,))
                    if t is not None and slot == 7:
                        real_imag(t, 0)
                    if n is not None and slot == 7:
                        shared(n, "Gb", (1, 2))
                        chans_of(n, "C", wrep[:, :, :, P:2 * P], P)
                    if t is not None and slot == 7:
                        real_imag(t, 1)
                    if n is not None and slot == 8:
                        chans_of(n, "B", wrep[:, :, :, 2 * P:], P)
                    if t is not None and slot == 8:
                        real_imag(t, 2)
                    if n is not None and slot == 8:
                        tile_of(n, "z0", wz, 0)

            run(pe, body)

        @block.scalar
        def _(act):
            act.wait_ge(ffs, 4)
            act.activation(ff[:, 0], ff[:, 1], ACT.Sin, scale=TURN).then_inc(ffs, 1)
            act.wait_ge(init, INIT)

            def copy_turned(n, c):
                bank, _ = filled(act, prep, n, f"tA{c}")
                act.activation(xnt[:, 0, c, :], bank[:, 0:TOKS], ACT.Copy).then_inc(S["xn_high"].sem, 1)

            def tanh_gate(n):
                now(act, "g_step", n, 1)
                before(act, "g_step", n)
                act.activation(trt[:], gl[:, :, 16:24], ACT.Tanh, scale=0.5).then_inc(S["gate_tanh"].sem, 1)

            def exp_abs(n):
                now(act, "g_step", n, 3)
                act.activation(gx[:, 2], gx[:, 1], ACT.Exp).then_inc(S["u_exp"].sem, 1)

            def exp_da(n):
                now(act, "g_step", n, NG - 4)
                before(act, "g_step", n)
                act.activation(al[:], dd[:, :, 8:16], ACT.Exp).then_inc(S["al_exp"].sem, 1)

            def tanh_angle(n):
                before(act, "d_step", n)
                bank, read = filled(act, prep, n, "ang")
                act.activation(ta[:], bank[:, 0:TOKS], ACT.Tanh).then_inc(read, 1)

            def copy_x(n, j):
                if j == 0:
                    before(act, "ug_ready", n)
                    before(act, "xd_ready", n)
                    before(act, "shifted", n)
                bank, read = filled(act, prep, n, f"x{j}")
                act.activation(x[:, j, :], bank[0:TC, :], ACT.Copy).then_inc(read, 1)

            def copy_shared(n, name, dst):
                bank, read = filled(act, prep, n, name)
                act.activation(dst[:], bank[0:NSH, 0:TOKS], ACT.Copy).then_inc(read, 1)

            def copy_g(n, name, o, w):
                bank, read = filled(act, prep, n, name)
                before(act, "a_done", n)
                act.activation(gsh[:, o:o + w], bank[0:TC, 0:w], ACT.Copy).then_inc(read, 1)

            def sines(n):
                now(act, "angles", n)
                before(act, "sin_done", n)
                read_before(act, prep, n, "C")
                read_before(act, prep, n, "B")
                act.activation(cs[:], th[:, 1], ACT.Sin, scale=TURN).then_inc(S["sin_done"].sem, 1)

            def silu_z(n, j):
                before(act, "og_ready", n, j + 1)
                bank, read = filled(act, prep, n, f"z{j}")
                act.activation(zs[:, j, :], bank[0:TC, :], ACT.Silu).then_inc(read, 1)

            def decays(i, h):
                now(act, "ld_ready", i, 3 * h + 3)
                reused(act, "m_ready", i, h, 1)
                for j in range(3):
                    act.activation(ee[:, h % RING, OFFS[j]:OFFS[j] + TC], ld[:, h % RING, j, :], ACT.Exp,
                                   bias=nlam[:, j, h:h + 1]).then_inc(S["e_done"].sem, 1)
                    if j < 2:
                        act.activation(ee[:, h % RING, OFFS[j] + TC:OFFS[j] + WIDTHS[j]], lb[:, h, (j + 1) * TC:], ACT.Exp,
                                       bias=nlam[:, j, h:h + 1]).then_inc(S["e_done"].sem, 1)

            def copy_tail(t, name, dst):
                bank, read = filled(act, tail, t, name)
                act.activation(dst, bank[:, 0:TOKS], ACT.Copy).then_inc(read, 1)

            def copy_xe(t, c):
                bank, _ = filled(act, tail, t, f"xe{c}")
                act.activation(xet[:, 0, c, :], bank[:, 0:TOKS], ACT.Copy).then_inc(S["xe_high"].sem, 1)

            def squares(t, j):
                if j == 0:
                    before(act, "ss_ready", t)
                bank, read = filled(act, tail, t, f"re{j}")
                act.activation(sq[:, j, :], bank[0:TC, :], ACT.Square).then_inc(read, 1)

            def roots(t):
                now(act, "ss_ready", t)
                act.activation(ss[:], ss[:], ACT.Sqrt).then_inc(S["root"].sem, 1)

            def body(p, n, i, t, f):
                for slot in range(9):
                    if i is not None and slot == 0:
                        silu_z(i, 1)
                    if t is not None and slot in (0, 1):
                        copy_tail(t, f"og{2 * slot}", ogt[:, 2 * slot, :])
                    if i is not None and slot == 0:
                        silu_z(i, 2)
                    if n is not None:
                        if slot == 1:
                            copy_turned(n, 0)
                            copy_turned(n, 1)
                        if slot == 2:
                            tanh_gate(n)
                            tanh_angle(n)
                            exp_abs(n)
                        if slot == 3:
                            copy_x(n, 0)
                            copy_x(n, 1)
                            exp_da(n)
                        if slot == 4:
                            copy_x(n, 2)
                        if slot == 5:
                            copy_shared(n, "Csh", csh)
                            copy_shared(n, "Bsh", bsh)
                    if t is not None:
                        if slot in (0, 1):
                            copy_tail(t, f"og{2 * slot + 1}", ogt[:, 2 * slot + 1, :])
                        if slot in (6, 7):
                            copy_xe(t, slot - 6)
                    if n is not None and slot == 7:
                        sines(n)
                    if i is not None:
                        for h in AHEAD[slot]:
                            decays(i, h)
                    if n is not None and slot == 7:
                        copy_g(n, "Ga", 0, WIDTHS[0])
                    if t is not None and slot == 7:
                        squares(t, 0)
                    if n is not None and slot == 7:
                        copy_g(n, "Gb", WIDTHS[0], SPAN - WIDTHS[0])
                        decays(n, 0)
                    if t is not None and slot == 7:
                        squares(t, 1)
                    if n is not None and slot == 8:
                        decays(n, 1)
                    if t is not None and slot == 8:
                        squares(t, 2)
                        roots(t)
                    if n is not None and slot == 8:
                        silu_z(n, 0)

            run(act, body)

        @block.gpsimd
        def _(pool):
            for sig in Signal.every:
                pool.sem_inc(sig.sem, sig.per)
            pool.memset(neg[:], -0.5).then_inc(init, 1)
            pool.memset(eps[:], EPS).then_inc(init, 1)
            pool.memset(ones[:], 1.0).then_inc(init, 1)
            pool.memset(xs[:], 0.0).then_inc(init, 1)
            pool.sem_inc(init, 1)
            pool.wait_ge(init, INIT)

            def rsqrt(n, aggr, used, mv_, ln_, step, rstd):
                now(pool, aggr, n)
                before(pool, used, n)
                pool.tensor_tensor(ln_[:, 0, :], mv_[:, :, 1], eps[0:TC], ALU.add).then_inc(S[step].sem, 1)
                now(pool, step, n)
                pool.tensor_tensor(ln_[:, 1, :], ln_[:, 0, :], neg[0:TC], ALU.pow).then_inc(S[rstd].sem, 1)

            def beta_x(n):
                now(pool, "shifted", n)
                now(pool, "g_step", n)
                before(pool, "u_ready", n)
                pool.tensor_tensor(xb[:].rearrange("p j (h d) -> p (j h) d", d=HD),
                                   xs[:].rearrange("p j (h d) -> p (j h) d", d=HD),
                                   gb[:, 3].rearrange("p j h -> p (j h)").unsqueeze(2).broadcast_to([TC, 24, HD]),
                                   ALU.mult).then_inc(S["xb_ready"].sem, 1)

            def gamma_x(n):
                was_read(pool, prep, n, "x1")
                was_read(pool, prep, n, "x2")
                pool.tensor_tensor(xg[:].rearrange("p j (h d) -> p (j h) d", d=HD),
                                   x[:].rearrange("p j (h d) -> p (j h) d", d=HD),
                                   gb[:, 1].rearrange("p j h -> p (j h)").unsqueeze(2).broadcast_to([TC, 24, HD]),
                                   ALU.mult).then_inc(S["ug_ready"].sem, 1)

            def d_x(n):
                before(pool, "y_read", n)
                was_read(pool, prep, n, "x1")
                was_read(pool, prep, n, "x2")
                pool.tensor_tensor(xd[:], x[:], drep[0:TC].broadcast_to([TC, 3, INNER]), ALU.mult
                                   ).then_inc(S["xd_ready"].sem, 1)

            def body(p, n, i, t, f):
                if t is not None:
                    rsqrt(t, "aggr2", "xe_ready", mv2, ln2, "rs_step2", "rstd2")
                if n is not None:
                    beta_x(n)
                    gamma_x(n)
                if p is not None:
                    rsqrt(p, "aggr", "xn_ready", mv, ln, "rs_step", "rstd")
                if n is not None:
                    d_x(n)

            rsqrt(0, "aggr", "xn_ready", mv, ln, "rs_step", "rstd")
            run(pool, body)

        @block.vector
        def _(dve):
            dve.wait_ge(weights, LOADED)
            one = Chain(dve, ffs, 0)
            one(dve.tensor_tensor(ff[:, 0], ff[:, 0], ff[:, 1], ALU.add))
            dve.tensor_scalar(ff[:, 0, :, 0:D], ff[:, 0, :, 0:D], 1.0 / (2.0 * np.pi), 0.25, ALU.mult, ALU.add)
            one(dve.tensor_scalar(ff[:, 0, :, D:], ff[:, 0, :, D:], 1.0 / (2.0 * np.pi), None, ALU.mult))
            one(dve.tensor_scalar(ff[:, 1], ff[:, 0], ROUND, ROUND, ALU.add, ALU.subtract))
            one(dve.tensor_tensor(ff[:, 1], ff[:, 0], ff[:, 1], ALU.subtract))
            dve.wait_ge(ffs, 5)
            one.at = 5
            for parts, buf in (*whole.values(), (ffr, ff[:, 0])):
                one(dve.tensor_copy(parts[:, 0], buf))
                one(dve.tensor_tensor(parts[:, 1], buf, parts[:, 0], ALU.subtract))
            dve.sem_inc(init, 2)
            dve.wait_ge(init, INIT)

            def stats_of(n, src, st_, mv_, stats, aggr, rstd):
                before(dve, rstd, n)
                for j in range(3):
                    dve.bn_stats(st_[:, j, :], src[:, j, :]).then_inc(S[stats].sem, 1)
                now(dve, stats, n)
                dve.memset(hold[:], 0.0)
                for j in range(3):
                    dve.bn_aggr(mv_[:, j, :], st_[:, j, :]).then_inc(S[aggr].sem, 1)

            def norm(n, src, dst, mv_, ln_, rstd, ready):
                now(dve, rstd, n)
                for j in range(3):
                    dve.tensor_scalar(dst[:, j, :], src[:, j, :], mv_[:, j, 0:1], ln_[:, 1, j:j + 1],
                                      ALU.subtract, ALU.mult).then_inc(S[ready].sem, 1)

            def low_x(n, c):
                now(dve, "xn_high", n, c + 1)
                bank, read = filled(dve, prep, n, f"tA{c}")
                dve.tensor_tensor(xnt[:, 1, c, :], bank[:, 0:TOKS], xnt[:, 0, c, :], ALU.subtract).then_inc(read, 1)

            def low_xe(t, c):
                now(dve, "xe_high", t, c + 1)
                bank, read = filled(dve, tail, t, f"xe{c}")
                dve.tensor_tensor(xet[:, 1, c, :], bank[:, 0:TOKS], xet[:, 0, c, :], ALU.subtract).then_inc(read, 1)

            def gates(n):
                before(dve, "al_exp", n)
                before(dve, "gate_tanh", n)
                bank, _ = filled(dve, prep, n, "gates")
                step = Chain(dve, S["g_step"].sem, NG * n + NG)
                gv = bank[0:TC, 0:72].rearrange("p (j g) -> p j g", g=24)
                _, _, read, _ = prep.at("gates")
                step(dve.tensor_copy(gl[:], gv))
                dve.sem_inc(read.sem, 1)
                a, na, w, b, r, s_, s2, p = (gx[:, k] for k in range(8))
                step(dve.tensor_tensor(a, gl[:, :, 0:16], gbias[0:TC].broadcast_to([TC, 3, 16]), ALU.add))
                step(dve.scalar_tensor_tensor(na, a, -1.0, a, ALU.mult, ALU.min))

            def softplus(n):
                a, _, w, b, r, s_, s2, p = (gx[:, k] for k in range(8))
                step = Chain(dve, S["g_step"].sem, NG * n + NG + 3)
                now(dve, "u_exp", n)
                step(dve.tensor_scalar(b, w, 2.0, None, ALU.add))
                step(dve.reciprocal(r, b))
                step(dve.tensor_tensor(s_, w, r, ALU.mult))
                step(dve.tensor_tensor(s2, s_, s_, ALU.mult))
                step(dve.tensor_scalar(p, s2, 1.0 / (2 * KL + 1), None, ALU.mult))
                for k in range(KL - 1, 0, -1):
                    step(dve.scalar_tensor_tensor(p, p, 1.0 / (2 * k + 1), s2, ALU.add, ALU.mult))
                step(dve.scalar_tensor_tensor(p, p, 1.0, s_, ALU.add, ALU.mult))
                step(dve.tensor_scalar(b, a, 0.0, None, ALU.max))
                step(dve.scalar_tensor_tensor(p, p, 2.0, b, ALU.mult, ALU.add))
                dve.tensor_copy(dd[:, :, 0:8], p[:, :, 0:8])
                step(dve.tensor_scalar(r[:, :, 0:8], p[:, :, 8:16], -1.0, -1e-4, ALU.mult, ALU.min))
                step(dve.tensor_tensor(dd[:, :, 8:16], r[:, :, 0:8], p[:, :, 0:8], ALU.mult))

            def mixes(n):
                tr, ga, be, bb = (gb[:, k] for k in range(4))
                step = Chain(dve, S["g_step"].sem, NG * n + NG + NG - 4)
                before(dve, "ug_ready", n)
                now(dve, "gate_tanh", n)
                step(dve.tensor_scalar(tr, trt[:], 0.5, 0.5, ALU.mult, ALU.add))
                step(dve.tensor_tensor(ga, tr, dd[:, :, 0:8], ALU.mult))
                step(dve.tensor_tensor(be, dd[:, :, 0:8], ga, ALU.subtract))
                now(dve, "al_exp", n)
                step(dve.tensor_tensor(bb, be, al[:], ALU.mult))

            def cumulate(n):
                bank, read = filled(dve, prep, n, "dd")
                dve.tensor_copy(ddt[:], bank[0:16, 0:TOKS]).then_inc(read, 1)
                was_read(dve, prep, n, "dd")
                before(dve, "lam_out", n)
                dve.tensor_tensor_scan(cs16[:], ones[0:16, :], ddt[:], 0.0, ALU.mult, ALU.add
                                       ).then_inc(S["scanned"].sem, 1)

            def angle(n, q):
                if q == 0:
                    before(dve, "angles", n)
                    before(dve, "sin_done", n)
                    was_read(dve, prep, n, "ang")
                wait(dve, "turns", 4 * n + 4 + q)
                bank, _ = filled(dve, prep, n, f"d{q}")
                dve.tensor_tensor(thi[:], ta[:], bank[:, 0:TOKS], ALU.mult).then_inc(S["d_step"].sem, 1)
                now(dve, "d_step", n, q + 1)
                dve.sem_inc(prep.at(f"d{q}")[2].sem, 1)
                dve.tensor_tensor_scan(th[:, 0, q, :], ones[:], thi[:], phase[:, 0:1], ALU.mult, ALU.add
                                       ).then_inc(S["turns"].sem, 1)

            def reduce_angles(n):
                now(dve, "turns", n)
                dve.tensor_scalar(th[:, 1], th[:, 0], ROUND, ROUND, ALU.add, ALU.subtract).then_inc(S["r_step"].sem, 1)
                now(dve, "r_step", n)
                dve.tensor_tensor(th[:, 1], th[:, 0], th[:, 1], ALU.subtract).then_inc(S["angles"].sem, 1)

            def copy_lam(n):
                bank, _ = filled(dve, prep, n, "lt")
                before(dve, "e_done", n)
                lv = bank[0:TC, 0:48].rearrange("p (j g) -> p j g", g=16)[:, :, 8:16]
                dve.tensor_copy(lam[:], lv).then_inc(S["lam_step"].sem, 1)
                now(dve, "lam_step", n)
                dve.sem_inc(prep.at("lt")[2].sem, 1)
                dve.tensor_scalar(nlam[:], lam[:], -1.0, None, ALU.mult).then_inc(S["lam_ready"].sem, 1)

            def turn_qk(n, name, dst):
                now(dve, "sin_done", n)
                bank, read = filled(dve, prep, n, name)
                before(dve, "rot_done", n)
                dve.tensor_tensor(dst[:], cs[:], bank[:, 0:TOKS].unsqueeze(1).broadcast_to([P, 4, TOKS]),
                                  ALU.mult).then_inc(read, 1)

            def make_u(n):
                before(dve, "y_done", n)
                now(dve, "ug_ready", n)
                dve.tensor_tensor(u[:], xg[:], xb[:], ALU.add).then_inc(S["u_ready"].sem, 1)

            def diagonal(i, h):
                if h == 0:
                    now(dve, "lb_in", i)
                    now(dve, "lam_ready", i)
                reused(dve, "e_done", i, h, 5)
                for j in range(3):
                    dve.scalar_tensor_tensor(ld[:, h % RING, j, :], lb[:, h, j * TC:(j + 1) * TC], lam[:, j, h:h + 1],
                                             negmask[:], ALU.min, ALU.add).then_inc(S["ld_ready"].sem, 1)

            def decay(i, h):
                now(dve, "rot_done", i, h + 1)
                wait(dve, "y_done", 8 * i + h + 7)
                if h == 0:
                    was_read(dve, prep, i, "Ga")
                    was_read(dve, prep, i, "Gb")
                m = mm_[:, h % 2, :]
                dve.tensor_tensor(m.rearrange("p (a b) -> p a b", a=2), rot[0:TC, :, 0:WIDTHS[0]],
                                  gsh[:].rearrange("p (a b) -> p a b", a=2), ALU.add).then_inc(S["a_done"].sem, 1)
                now(dve, "a_done", i, h + 1)
                now(dve, "e_done", i, 5 * h + 5)
                dve.tensor_tensor(m, m, ee[:, h % RING, :], ALU.mult).then_inc(S["m_ready"].sem, 1)

            def add_dx(i):
                now(dve, "y_done", i)
                now(dve, "xd_ready", i)
                used_before(dve, tail, i, "og3")
                for j in range(3):
                    dve.tensor_tensor(og[:, j, :], y[j][0:TC, :], xd[:, j, :], ALU.add).then_inc(S["y_read"].sem, 1)

            def gate_y(i):
                was_read(dve, prep, i, "z1")
                was_read(dve, prep, i, "z2")
                for j in range(3):
                    now(dve, "y_read", i, j + 1)
                    dve.tensor_tensor(og[:, j, :], og[:, j, :], zs[:, j, :], ALU.mult).then_inc(S["og_ready"].sem, 1)

            def residual(t, j):
                if j == 0:
                    now(dve, "res_in", t)
                    before(dve, "h4_ready", t)
                bank, _ = filled(dve, tail, t, f"wo{j}")
                dve.tensor_tensor(h3[:, j, :], bank[0:TC, 0:D], res[:, j, :], ALU.add).then_inc(S["h3_ready"].sem, 1)
                now(dve, "h3_ready", t, j + 1)
                dve.sem_inc(tail.read[0].sem, 1)

            def sum_squares(t):
                was_read(dve, tail, t, "re2")
                before(dve, "h4_ready", t)
                dve.tensor_tensor(ss[:], sq[:, :, 0:D], sq[:, :, D:], ALU.add).then_inc(S["ss_ready"].sem, 1)

            def finish(t):
                now(dve, "root", t)
                before(dve, "stored", t)
                dve.tensor_tensor(ob[:], h3[:], ss[:], ALU.add).then_inc(S["h4_ready"].sem, 1)

            def norm_rows(p):
                now(dve, "ht_in", p)
                stats_of(p, ht, st, mv, "stats", "aggr", "rstd")
                used_before(dve, prep, p, "tA1")
                norm(p, ht, xn, mv, ln, "rstd", "xn_ready")

            def body(p, n, i, t, f):
                for slot in range(9):
                    if n is not None:
                        if slot == 5:
                            cumulate(n)
                        if slot == 6:
                            angle(n, 0)
                            angle(n, 1)
                    if i is not None and slot < 8:
                        decay(i, slot)
                    if n is not None and slot == 1:
                        low_x(n, 0)
                        low_x(n, 1)
                    if t is not None and slot == 7:
                        low_xe(t, 1)
                    if i is not None:
                        for h in AHEAD[slot]:
                            diagonal(i, h)
                    if f is not None and slot == 1:
                        finish(f)
                    if n is not None:
                        if slot == 2:
                            gates(n)
                        if slot == 3:
                            softplus(n)
                        if slot == 4:
                            mixes(n)
                        if slot == 6:
                            angle(n, 2)
                            angle(n, 3)
                    if t is not None and slot == 6:
                        low_xe(t, 0)
                    if n is not None:
                        if slot == 6:
                            reduce_angles(n)
                        if slot == 7:
                            copy_lam(n)
                            diagonal(n, 0)
                            diagonal(n, 1)
                    if p is not None and slot == 7:
                        norm_rows(p)
                    if t is not None:
                        if slot in (2, 3, 4):
                            residual(t, slot - 2)
                        if slot == 4:
                            stats_of(t, h3, st2, mv2, "stats2", "aggr2", "rstd2")
                        if slot == 5:
                            used_before(dve, tail, t, "xe1")
                            norm(t, h3, xe, mv2, ln2, "rstd2", "xe_ready")
                    if n is not None and slot == 8:
                        turn_qk(n, "C", qr)
                    if i is not None and slot == 8:
                        add_dx(i)
                    if n is not None and slot == 8:
                        turn_qk(n, "B", kr)
                    if t is not None and slot == 8:
                        sum_squares(t)
                    if i is not None and slot == 8:
                        gate_y(i)
                    if n is not None and slot == 8:
                        make_u(n)

            norm_rows(0)
            run(dve, body)


def program(nc, T, out):
    h0 = nc.dram_tensor("h0", [IMGS, TOKS, D], F32).ap()
    kpad = nc.dram_tensor("kpad", [D, IMGS * 2 * IMGS], F32).ap()
    xn_t = nc.dram_tensor("xn_t", [D, IMGS, TOKS], F32).ap()
    mx = nc.dram_tensor("mx", [TOKS, IMGS, D], F32).ap()
    taps_stage(nc, T, kpad)
    embed_stage(nc, T, h0, xn_t)
    ema_stage(nc, T, kpad, xn_t, mx)
    h2 = nc.dram_tensor("h2", [IMGS, TOKS, D], F32).ap()
    mix_stage(nc, T, h0, mx, h2)
    lam_d = nc.dram_tensor("lam_d", [IMGS, HEADS, TOKS], F32).ap()
    scan_stage(nc, T, h2, lam_d, out)


def laid_out(inputs):
    a = {k: np.asarray(v) for k, v in inputs.items()}
    x = a["x"].reshape(IMGS, 3, 14, 16, 14, 16).transpose(0, 1, 3, 5, 2, 4).reshape(IMGS, KC, P, PATCHES)
    def cols(v):
        return v.reshape(-1, P).T

    T = {"patches": x.transpose(0, 2, 1, 3).reshape(IMGS, P, KC * PATCHES), "txt": a["txt"],
         "tok_W1": a["L0_tok_W1"], "tok_b1": cols(a["L0_tok_b1"]), "tok_W2": a["L0_tok_W2"], "tok_b2": a["L0_tok_b2"],
         "delta": a["L0_attn_ema_delta"][:, :, 0], "alpha": a["L0_attn_ema_alpha"][:, :, 0],
         "beta": a["L0_attn_ema_beta"][:, :, 0], "gamma": a["L0_attn_ema_gamma"], "omega": cols(a["L0_attn_ema_omega"]),
         "ln_w": cols(a["L0_attn_ln_w"]), "ln_b": cols(a["L0_attn_ln_b"]), "ident": np.eye(P, dtype=np.float32)}
    wmx, bmx = a["L0_attn_Wmx"].T, a["L0_attn_bmx"]
    half = np.arange(P // 2, dtype=np.float32)
    ang = np.arange(IMGS, dtype=np.float32)[None, :] * np.exp(half * np.float32(-np.log(10000.0) / (P // 2)))[:, None]
    cos, sin = np.cos(ang), np.sin(ang)
    ra, rb = a["L0_attn_rot_alpha"][0], a["L0_attn_rot_beta"][0]
    e = np.arange(EXPERTS)
    T.update({
        "wv": a["L0_attn_Wv"].T, "wzr": wmx[:, D:D + 640], "wuh": np.concatenate([wmx[:, :D], wmx[:, D + 640:]], 1),
        "wh": a["L0_attn_Wh"].T, "bv": a["L0_attn_bv"][None], "bh": a["L0_attn_bh"][None],
        "buh": np.concatenate([bmx[:D], bmx[D + 640:]])[None], "bzr": cols(bmx[D:D + 640]),
        "qk": np.concatenate([a["L0_attn_qk_gamma"], a["L0_attn_qk_beta"]]).T,
        "rot": np.stack([ra, np.roll(ra, 64), rb, np.roll(rb, 64)], 1),
        "trig": np.stack([np.concatenate([cos, cos]), np.concatenate([-sin, sin])], 1).astype(np.float32),
        "w1": a["L0_ffn_w1"], "w2": a["L0_ffn_w2"], "wgu": a["L0_ffn_shared_gate_up"], "wsd": a["L0_ffn_shared_down"],
        "wr": np.concatenate([a["L0_ffn_router_w"], a["L0_ffn_shared_gate_w"]], 1),
        "lower": (e[None, :] < e[:, None]).astype(np.float32).reshape(1, -1)})
    win = a["L1_attn_w_in"].T
    z0, x0, b0, c0, g0, a0 = 0, INNER, 2 * INNER, 2 * INNER + P, 2 * INNER + 2 * P, 2 * INNER + 2 * P + 24
    head = np.arange(P) // 64
    sel = np.zeros((16, 4, P), np.float32)
    for q in range(4):
        sel[2 * q + head, q, np.arange(P)] = 0.5
    cosine = (np.arange(P) // R) % 2 == 0
    pos = np.arange(TC)
    T.update({
        "wg": win[:, g0:a0], "wx": win[:, x0:b0], "wz": win[:, z0:x0],
        "wrep": np.concatenate([np.tile(win[:, o:o + R], 4) for o in (a0, c0, b0)], 1),
        "wsh": np.concatenate([win[:, c0 + R:g0], win[:, b0 + R:c0]], 1),
        "wo": a["L1_attn_w_out"].T, "ff": np.concatenate([a["L1_ffn_theta"], a["L1_ffn_phi"]], 1),
        "ffn": np.concatenate([a["L1_ffn_theta_noise"], a["L1_ffn_phi_noise"]], 1),
        "gbias": np.concatenate([a["L1_attn_dt_bias"], np.zeros(8, np.float32)])[None],
        "drep": np.repeat(a["L1_attn_D"], HD)[None], "sel": sel,
        "phase": np.stack([np.where(cosine, 0.25, 0.0), np.zeros(P)], 1).astype(np.float32),
        "negmask": np.where(pos[None, :] < pos[:, None], -1e30, 0.0).astype(np.float32)})
    return {k: np.ascontiguousarray(v) for k, v in T.items()}


def kernel(**inputs):
    import concourse.bacc as _bacc
    from concourse.bass_utils import run_bass_kernel_spmd as _run

    nc = _bacc.Bacc("TRN2", target_bir_lowering=False, num_devices=1)
    arrays = laid_out(inputs)
    T = {k: nc.dram_tensor(f"in_{k}", v.shape, mybir.dt.from_np(v.dtype), kind="ExternalInput").ap()
         for k, v in arrays.items()}
    out = nc.dram_tensor("out_0", (IMGS, TOKS, D), F32, kind="ExternalOutput").ap()
    program(nc, T, out)
    r = _run(nc, [{f"in_{k}": v for k, v in arrays.items()}], core_ids=[0])
    return r.results[0]["out_0"]
```
